# Optimizing a Trainium2 kernel written in Bass

```python
import numpy as np
import jax
import jax.numpy as jnp

def _softmax(x, axis=-1):
    return jax.nn.softmax(x, axis=axis)

def _gelu(x):
    return jax.nn.gelu(x, approximate=True)

def _silu(x):
    return jax.nn.silu(x)

def _sigmoid(x):
    return jax.nn.sigmoid(x)

def _layernorm(x, axis=-1, eps=1e-05):
    m = jnp.mean(x, axis=axis, keepdims=True)
    v = jnp.var(x, axis=axis, keepdims=True)
    return (x - m) / jnp.sqrt(v + eps)

def _scatter_add(tgt, idx, src, axis=0):
    return tgt.at[idx].add(src)

def _segment_sum(src, seg, n):
    return jax.ops.segment_sum(src, seg, n)
kernel_name = 'mk_gnn_resnorm_d4_gnn_r8_b63580'

def setup_inputs(seed: int=0):
    np.random.seed(seed)
    _w = jnp.asarray

    def _rec_inputs():
        import jax
        import jax.numpy as jnp
        _gk = jax.random.key(seed)
        x = -8.776e-05 + 1 * jax.random.normal(jax.random.fold_in(_gk, 1), (1250, 512), jnp.float32)
        src = jax.random.randint(jax.random.fold_in(_gk, 2), (20000,), 0, 1250, jnp.int32)
        dst = jnp.minimum((1250 * jax.random.uniform(jax.random.fold_in(_gk, 3), (20000,)) ** 2.0).astype(jnp.int32), 9999)
        _o = jnp.argsort(dst, stable=True)
        src = src[_o]
        dst = dst[_o]
        edge_weight = jax.random.uniform(jax.random.fold_in(_gk, 13), (20000,), jnp.float32, 0.0, 0.999998)
        return (x, src, dst, edge_weight)
    x, src, dst, edge_weight = _rec_inputs()

    def _L0_gnn_setup():
        import jax, jax.numpy as jnp
        import numpy as np
        N, E = (1250, 80000)
        IN, HID, OUT = (512, 512, 512)

        def gcn_conv(x, edge_index, W, b, num_nodes):
            src, dst = (edge_index[0], edge_index[1])
            ones = jnp.ones((src.shape[0],), x.dtype)
            deg = jax.ops.segment_sum(ones, dst, num_segments=num_nodes) + 1.0
            inv = jax.lax.rsqrt(deg)
            h = x @ W
            norm = inv[src] * inv[dst]
            agg = jax.ops.segment_sum(h[src] * norm[:, None], dst, num_segments=num_nodes)
            agg = agg + h * (inv * inv)[:, None]
            return agg + b

        def gru(x_seq, W_ih, W_hh, b_ih, b_hh):
            H = W_hh.shape[1]
            pre_i = x_seq @ W_ih.T + b_ih

            def step(h, pi):
                ph = h @ W_hh.T + b_hh
                r = jax.nn.sigmoid(pi[:H] + ph[:H])
                z = jax.nn.sigmoid(pi[H:2 * H] + ph[H:2 * H])
                n = jnp.tanh(pi[2 * H:] + r * ph[2 * H:])
                h_new = (1.0 - z) * n + z * h
                return (h_new, h_new)
            h0 = jnp.zeros((H,), x_seq.dtype)
            _, ys = jax.lax.scan(step, h0, pre_i)
            return ys
        key = jax.random.key(seed)
        ks = jax.random.split(key, 8)
        x = jax.random.normal(ks[0], (N, IN), dtype=jnp.float32)
        edge_index = jax.random.randint(ks[1], (2, E), 0, N, dtype=jnp.int64)
        s = lambda fan: 1.0 / np.sqrt(fan)
        W1 = jax.random.normal(ks[2], (IN, HID), jnp.float32) * s(IN)
        b1 = jnp.zeros((HID,), jnp.float32)
        W2 = jax.random.normal(ks[3], (HID, OUT), jnp.float32) * s(HID)
        b2 = jnp.zeros((OUT,), jnp.float32)
        W_ih = jax.random.normal(ks[4], (3 * HID, OUT), jnp.float32) * s(HID)
        W_hh = jax.random.normal(ks[5], (3 * HID, HID), jnp.float32) * s(HID)
        b_ih = jnp.zeros((3 * HID,), jnp.float32)
        b_hh = jnp.zeros((3 * HID,), jnp.float32)
        W_fc = jax.random.normal(ks[6], (HID, OUT), jnp.float32) * s(HID)
        b_fc = jnp.zeros((OUT,), jnp.float32)
        return {'x': x, 'edge_index': edge_index, 'W1': W1, 'b1': b1, 'W2': W2, 'b2': b2, 'W_ih': W_ih, 'W_hh': W_hh, 'b_ih': b_ih, 'b_hh': b_hh, 'W_fc': W_fc, 'b_fc': b_fc}
    _L0_gnn_all = _L0_gnn_setup()
    _L0_gnn_in = {k: v for k, v in _L0_gnn_all.items() if k in ('W1', 'b1', 'W2', 'b2', 'W_ih', 'W_hh', 'b_ih', 'b_hh', 'W_fc', 'b_fc')}
    del _L0_gnn_all

    def _L1_gnn_setup():
        import jax, jax.numpy as jnp
        import numpy as np
        N = 1250
        E = 20000
        IN_C = 512
        HID = 512
        OUT_C = 512
        BN_EPS = 1e-05
        key = jax.random.key(seed)
        ks = jax.random.split(key, 8)
        x = jax.random.normal(ks[0], (N, IN_C), dtype=jnp.float32)
        src = jax.random.randint(ks[1], (E,), 0, N)
        off = jax.random.randint(ks[2], (E,), 1, N)
        dst = (src + off) % N
        edge_index = jnp.stack([src, dst]).astype(jnp.int64)
        W1 = jax.random.normal(ks[3], (IN_C, HID), dtype=jnp.float32) * (1.0 / np.sqrt(IN_C))
        b1 = jnp.zeros((HID,), dtype=jnp.float32)
        gamma = jnp.ones((HID,), dtype=jnp.float32)
        beta = jnp.zeros((HID,), dtype=jnp.float32)
        W2 = jax.random.normal(ks[4], (HID, OUT_C), dtype=jnp.float32) * (1.0 / np.sqrt(HID))
        b2 = jnp.zeros((OUT_C,), dtype=jnp.float32)
        return {'x': x, 'W1': W1, 'b1': b1, 'gamma': gamma, 'beta': beta, 'W2': W2, 'b2': b2, 'edge_index': edge_index}
    _L1_gnn_all = _L1_gnn_setup()
    _L1_gnn_in = {k: v for k, v in _L1_gnn_all.items() if k in ('W1', 'b1', 'gamma', 'beta', 'W2', 'b2')}
    del _L1_gnn_all

    def _L2_gnn_setup():
        import jax, jax.numpy as jnp
        import numpy as np
        N_NODES = 4096
        N_EDGES = 32768
        D = 512
        NUM_EXPERTS = 4
        TOP_K = 2
        LAYERS = 2
        key = jax.random.key(seed)
        ks = jax.random.split(key, 8)
        x = jax.random.normal(ks[0], (N_NODES, D), dtype=jnp.float32)
        edge_index = jax.random.randint(ks[1], (2, N_EDGES), 0, N_NODES, dtype=jnp.int64)
        s = 1.0 / np.sqrt(D)
        gate_W = jax.random.uniform(ks[2], (D, NUM_EXPERTS), jnp.float32, -s, s)
        gate_b = jax.random.uniform(ks[3], (NUM_EXPERTS,), jnp.float32, -s, s)
        Wl = jax.random.uniform(ks[4], (NUM_EXPERTS, LAYERS, D, D), jnp.float32, -s, s)
        bl = jax.random.uniform(ks[5], (NUM_EXPERTS, LAYERS, D), jnp.float32, -s, s)
        Wr = jax.random.uniform(ks[6], (NUM_EXPERTS, LAYERS, D, D), jnp.float32, -s, s)
        return {'x': x, 'gate_W': gate_W, 'gate_b': gate_b, 'Wl': Wl, 'bl': bl, 'Wr': Wr, 'edge_index': edge_index}
    _L2_gnn_all = _L2_gnn_setup()
    _L2_gnn_in = {k: v for k, v in _L2_gnn_all.items() if k in ('gate_W', 'gate_b', 'Wl', 'bl', 'Wr')}
    del _L2_gnn_all

    def _L3_gnn_setup():
        import jax, jax.numpy as jnp
        import numpy as np
        N_NODES = 6250
        N_EDGES = 100000
        M_IN = 512
        H_OUT = 512
        key = jax.random.key(seed)
        k1, k2, k3, k4, k5 = jax.random.split(key, 5)
        X = jax.random.normal(k1, (N_NODES, M_IN), dtype=jnp.float32)
        limit = float(np.sqrt(6.0 / (M_IN + H_OUT)))
        W = jax.random.uniform(k2, (M_IN, H_OUT), dtype=jnp.float32, minval=-limit, maxval=limit)
        edge_src = jax.random.randint(k3, (N_EDGES,), 0, N_NODES, dtype=jnp.int64 if jax.config.jax_enable_x64 else jnp.int32)
        edge_dst = jax.random.randint(k4, (N_EDGES,), 0, N_NODES, dtype=jnp.int64 if jax.config.jax_enable_x64 else jnp.int32)
        edge_vals = jax.random.uniform(k5, (N_EDGES,), dtype=jnp.float32, minval=0.0, maxval=1.0)
        return {'X': X, 'W': W, 'edge_src': edge_src, 'edge_dst': edge_dst, 'edge_vals': edge_vals}
    _L3_gnn_all = _L3_gnn_setup()
    _L3_gnn_in = {k: v for k, v in _L3_gnn_all.items() if k in ('W',)}
    del _L3_gnn_all
    return {'x': x, 'src': src, 'dst': dst, 'edge_weight': edge_weight, 'L0_gnn_W1': _L0_gnn_in['W1'], 'L0_gnn_b1': _L0_gnn_in['b1'], 'L0_gnn_W2': _L0_gnn_in['W2'], 'L0_gnn_b2': _L0_gnn_in['b2'], 'L0_gnn_W_ih': _L0_gnn_in['W_ih'], 'L0_gnn_W_hh': _L0_gnn_in['W_hh'], 'L0_gnn_b_ih': _L0_gnn_in['b_ih'], 'L0_gnn_b_hh': _L0_gnn_in['b_hh'], 'L0_gnn_W_fc': _L0_gnn_in['W_fc'], 'L0_gnn_b_fc': _L0_gnn_in['b_fc'], 'L1_gnn_W1': _L1_gnn_in['W1'], 'L1_gnn_b1': _L1_gnn_in['b1'], 'L1_gnn_gamma': _L1_gnn_in['gamma'], 'L1_gnn_beta': _L1_gnn_in['beta'], 'L1_gnn_W2': _L1_gnn_in['W2'], 'L1_gnn_b2': _L1_gnn_in['b2'], 'L2_gnn_gate_W': _L2_gnn_in['gate_W'], 'L2_gnn_gate_b': _L2_gnn_in['gate_b'], 'L2_gnn_Wl': _L2_gnn_in['Wl'], 'L2_gnn_bl': _L2_gnn_in['bl'], 'L2_gnn_Wr': _L2_gnn_in['Wr'], 'L3_gnn_W': _L3_gnn_in['W']}

def reference(x, src, dst, edge_weight, L0_gnn_W1, L0_gnn_b1, L0_gnn_W2, L0_gnn_b2, L0_gnn_W_ih, L0_gnn_W_hh, L0_gnn_b_ih, L0_gnn_b_hh, L0_gnn_W_fc, L0_gnn_b_fc, L1_gnn_W1, L1_gnn_b1, L1_gnn_gamma, L1_gnn_beta, L1_gnn_W2, L1_gnn_b2, L2_gnn_gate_W, L2_gnn_gate_b, L2_gnn_Wl, L2_gnn_bl, L2_gnn_Wr, L3_gnn_W):
    import jax
    import jax.numpy as jnp

    def _L0_gnn_ref(x, edge_index, W1, b1, W2, b2, W_ih, W_hh, b_ih, b_hh, W_fc, b_fc):
        import jax, jax.numpy as jnp
        import numpy as np
        N, E = (1250, 80000)
        IN, HID, OUT = (512, 512, 512)

        def gcn_conv(x, edge_index, W, b, num_nodes):
            src, dst = (edge_index[0], edge_index[1])
            ones = jnp.ones((src.shape[0],), x.dtype)
            deg = jax.ops.segment_sum(ones, dst, num_segments=num_nodes) + 1.0
            inv = jax.lax.rsqrt(deg)
            h = x @ W
            norm = inv[src] * inv[dst]
            agg = jax.ops.segment_sum(h[src] * norm[:, None], dst, num_segments=num_nodes)
            agg = agg + h * (inv * inv)[:, None]
            return agg + b

        def gru(x_seq, W_ih, W_hh, b_ih, b_hh):
            H = W_hh.shape[1]
            pre_i = x_seq @ W_ih.T + b_ih

            def step(h, pi):
                ph = h @ W_hh.T + b_hh
                r = jax.nn.sigmoid(pi[:H] + ph[:H])
                z = jax.nn.sigmoid(pi[H:2 * H] + ph[H:2 * H])
                n = jnp.tanh(pi[2 * H:] + r * ph[2 * H:])
                h_new = (1.0 - z) * n + z * h
                return (h_new, h_new)
            h0 = jnp.zeros((H,), x_seq.dtype)
            _, ys = jax.lax.scan(step, h0, pre_i)
            return ys
        h = jax.nn.relu(gcn_conv(x, edge_index, W1, b1, N))
        h = jax.nn.relu(gcn_conv(h, edge_index, W2, b2, N))
        h = gru(h, W_ih, W_hh, b_ih, b_hh)
        return h @ W_fc + b_fc

    def _L1_gnn_ref(x, W1, b1, gamma, beta, W2, b2, edge_index):
        import jax, jax.numpy as jnp
        import numpy as np
        N = 1250
        E = 20000
        IN_C = 512
        HID = 512
        OUT_C = 512
        BN_EPS = 1e-05
        n = x.shape[0]
        loops = jnp.arange(n, dtype=edge_index.dtype)
        src = jnp.concatenate([edge_index[0], loops])
        dst = jnp.concatenate([edge_index[1], loops])
        deg = jax.ops.segment_sum(jnp.ones_like(dst, dtype=x.dtype), dst, num_segments=n)
        dinv = jnp.where(deg > 0, deg ** (-0.5), 0.0)
        w = dinv[src] * dinv[dst]

        def agg(h):
            return jax.ops.segment_sum(w[:, None] * h[dst], src, num_segments=n)
        h = x @ W1 + b1
        h = agg(h)
        mu = jnp.mean(h, axis=0)
        var = jnp.var(h, axis=0)
        h = gamma * (h - mu) * jax.lax.rsqrt(var + BN_EPS) + beta
        h = jax.nn.relu(h)
        h = h @ W2 + b2
        h = agg(h)
        return h

    def _L2_gnn_ref(x, gate_W, gate_b, Wl, bl, Wr, edge_index):
        import jax, jax.numpy as jnp
        import numpy as np
        N_NODES = 4096
        N_EDGES = 32768
        D = 512
        NUM_EXPERTS = 4
        TOP_K = 2
        LAYERS = 2
        n = x.shape[0]
        src, dst = (edge_index[0], edge_index[1])
        gates = jax.nn.softmax(x @ gate_W + gate_b, axis=-1)
        top_v, top_i = jax.lax.top_k(gates, TOP_K)
        deg = jax.ops.segment_sum(jnp.ones((src.shape[0],), x.dtype), dst, num_segments=n)
        inv_deg = jnp.where(deg > 0, 1.0 / jnp.maximum(deg, 1.0), 0.0)[:, None]

        def sage_conv(h, W_l, b_l, W_r):
            aggr = jax.ops.segment_sum(h[src], dst, num_segments=n) * inv_deg
            return aggr @ W_l + b_l + h @ W_r
        expert_outs = []
        for e in range(NUM_EXPERTS):
            h = x
            for l in range(LAYERS):
                h = sage_conv(h, Wl[e, l], bl[e, l], Wr[e, l])
                h = jax.nn.relu(h)
            expert_outs.append(h)
        expert_outputs = jnp.stack(expert_outs, axis=1)
        sel = jnp.take_along_axis(expert_outputs, top_i[:, :, None], axis=1)
        out = jnp.sum(sel * top_v[:, :, None], axis=1)
        return out

    def _L3_gnn_ref(X, W, edge_src, edge_dst, edge_vals):
        import jax, jax.numpy as jnp
        import numpy as np
        N_NODES = 6250
        N_EDGES = 100000
        M_IN = 512
        H_OUT = 512
        Z = jnp.matmul(X, W)
        msg = Z[edge_src] * edge_vals[:, None]
        agg = jax.ops.segment_sum(msg, edge_dst, num_segments=X.shape[0])
        return jax.nn.relu(agg)
    edge_index = jnp.stack([src, dst])
    x = _layernorm(x + _L0_gnn_ref(x, edge_index, L0_gnn_W1, L0_gnn_b1, L0_gnn_W2, L0_gnn_b2, L0_gnn_W_ih, L0_gnn_W_hh, L0_gnn_b_ih, L0_gnn_b_hh, L0_gnn_W_fc, L0_gnn_b_fc), axis=-1)
    x = _layernorm(x + _L1_gnn_ref(x, L1_gnn_W1, L1_gnn_b1, L1_gnn_gamma, L1_gnn_beta, L1_gnn_W2, L1_gnn_b2, edge_index), axis=-1)
    x = _layernorm(x + _L2_gnn_ref(x, L2_gnn_gate_W, L2_gnn_gate_b, L2_gnn_Wl, L2_gnn_bl, L2_gnn_Wr, edge_index), axis=-1)
    x = _layernorm(x + _L3_gnn_ref(x, L3_gnn_W, src, dst, edge_weight), axis=-1)
    return x

_drawn_inputs = setup_inputs


def setup_inputs(seed=0):
    import zlib

    import numpy as np

    out = dict(_drawn_inputs(seed))
    spreads = {'L0_gnn_b1': (0.0, 0.1),
     'L0_gnn_b2': (0.0, 0.1),
     'L0_gnn_b_ih': (0.0, 0.1),
     'L0_gnn_b_hh': (0.0, 0.1),
     'L0_gnn_b_fc': (0.0, 0.1),
     'L1_gnn_b1': (0.0, 0.1),
     'L1_gnn_gamma': (1.0, 0.2),
     'L1_gnn_beta': (0.0, 0.1),
     'L1_gnn_b2': (0.0, 0.1)}
    factors = {'L2_gnn_gate_b': 4.168, 'L2_gnn_bl': 3.708}
    for name, (base, spread) in spreads.items():
        noise = np.random.default_rng([zlib.crc32(name.encode()), seed]).standard_normal(out[name].shape)
        drawn = base * np.exp(spread * noise) if base else spread * noise
        out[name] = jnp.asarray(drawn.astype(out[name].dtype))
    for name, factor in factors.items():
        out[name] = (out[name] * factor).astype(out[name].dtype)
    return out
```

```python
from contextlib import ExitStack

import concourse.bass as bass
from concourse import mybir

ACT = mybir.ActivationFunctionType
ALU = mybir.AluOpType
AX = mybir.AxisListType
F32 = mybir.dt.float32
F16 = mybir.dt.float16
BF16 = mybir.dt.bfloat16
I32 = mybir.dt.int32

N, D, E = 1250, 512, 20000
P = 128
NP, NT = 125, 10
KT = D // P
EP, ET = 125, 160
EH = ET // 2
WD = 25
NW = N // WD
RING = 4
NCH = [(0, 417), (417, 834), (834, 1250)]
NE = 4
LN_EPS = 1e-5
HS = 4096.0
GMAX = ET * (NW + 1)
WSLOT = KT * D


def layout(nc, io):
    ctx = ExitStack()
    with ctx:
        def sb(name, shape, dt=F32):
            return ctx.enter_context(nc.sbuf_tensor(name, shape, dt))

        def sem(name):
            return ctx.enter_context(nc.semaphore(name))


        adj = sb("adj", [P, NT * N])
        big = sb("big", [P, (N + 2) * 12])
        xr = sb("xr", [P, NT, D])
        r1 = sb("r1", [P, KT, N])
        r2 = sb("r2", [P, KT, N])
        hn = sb("hn", [P, NT, D])
        ws = sb("ws", [P, 2 * WSLOT])
        psum = ctx.enter_context(nc.psum_tensor("psum", [P, 8, 512], F32))

        adj_v = adj[:].rearrange("p (t n) -> p t n", n=N)
        wt_v = big[:, 0:NT * N].rearrange("p (t n) -> p t n", n=N)
        pi_v = big[:].rearrange("p (t q) -> p t q", q=12)
        tail = NT * N
        inv_row = big[:, tail:tail + N]
        invdeg_row = big[:, tail + N:tail + 2 * N]
        l1_bias = big[:, tail:tail + D]
        hn_f = hn[:].rearrange("p t d -> p (t d)")
        r2_f = r2[:].rearrange("p k n -> p (k n)")
        fc_bias = r2_f[:, 4400:4400 + D]

        def weight(ap):
            return ap.rearrange("p (k n) -> p k n", k=KT)

        def wslot(i):
            return weight(ws[:, i * WSLOT:(i + 1) * WSLOT])

        w_fc = weight(hn_f[:, 0:WSLOT])
        whh = [r2_f[:, 0:WSLOT], r2_f[:, WSLOT:2 * WSLOT], hn_f[:, WSLOT:2 * WSLOT]]
        whh16 = [a.bitcast(F16).rearrange("p (a k n) -> p a k n", a=2, k=KT) for a in whh]
        l2w = [weight(adj[:, i * WSLOT:(i + 1) * WSLOT]) for i in range(4)]
        at = 4 * WSLOT
        agg_x = [big[:, tail:tail + N], big[:, tail + N:tail + 2 * N], adj[:, at:at + N], adj[:, at + N:at + 2 * N]]
        l2_bias = adj[:, at + 2 * N:at + 2 * N + D]
        at += 2 * N + D
        l2_tmp = [adj[0:NP, at + i * D:at + (i + 1) * D] for i in range(2)]

        iota16 = r2_f[:, 0:625].bitcast(F16)
        src_hot = r2_f[:, 625:625 * (1 + RING)].bitcast(BF16)
        dst_hot = r2_f[:, 3125:3125 + RING * 50].bitcast(BF16)
        zero_b = r2_f[:, 3400:3400 + 250].bitcast(BF16)
        e_stage = hn_f[:, 0:750].rearrange("p (a h e) -> p a h e", a=3, h=2)
        e_int = hn_f[:, 750:1250].bitcast(I32).rearrange("p (a h e) -> p a h e", a=2, h=2)
        e_col = hn_f[:, 1250:1250 + 3 * ET].rearrange("p (a t) -> p a t", a=3)
        e_src, e_dst, e_w = e_col[:, 0], e_col[:, 1], e_col[:, 2]
        w_part = hn_f[:, 1730:2370].rearrange("p (t a) -> p t a", a=4)
        w_bf = hn_f[:, 2370:2450].bitcast(BF16)
        w_res = hn_f[:, 2610:2610 + 2 * ET].rearrange("p (a t) -> p a t", a=2)
        t_lim = hn_f[0:EH, 2930:2934].rearrange("p (a h) -> p a h", a=2)
        w_lim = hn_f[:, 2934:2936]
        tile_no = hn_f[:, 2936:2936 + 2 * ET].rearrange("p (a t) -> p a t", a=2)
        hit = hn_f[:, 3256:3416]
        hit_b = hn_f[:, 3416:3416 + ET]
        span = hn_f[:, 3576:3578]
        row = hn_f[0:1, 3578:3578 + 6 * NW].rearrange("p (a w) -> p a w", a=6)
        cparts = [a.rearrange("p (t c) -> p t c", t=NT) for a in (hn_f[:, 3880:4630], r2_f[:, 3650:4400])]

        ident = sb("ident", [P, P])
        ones = sb("ones", [P, P])
        bounds = sb("bounds", [1, 5, NW], I32)
        inv_col = sb("inv_col", [P, NT])
        bcol = sb("bcol_sb", [P, 56])
        b1c, b2c, bihc, bhhc = bcol[:, 0:4], bcol[:, 4:8], bcol[:, 8:20], bcol[:, 20:32]
        gamc, betc, blc = bcol[:, 32:36], bcol[:, 36:40], bcol[:, 40:56]
        gate_w = sb("gate_w", [P, KT, NE])
        gate_b = sb("gate_b_sb", [P, NE])
        gates = sb("gates", [P, NT, NE])
        gsel = sb("gsel", [P, NE, NT])
        gtmp = sb("gtmp", [P, 3, NT])
        stat = sb("stat", [P, 3, 6])
        mv = sb("mv", [P, 4])
        bnc = sb("bnc", [P, 2, KT])
        wmax = sb("wmax", [P, 12])
        scl = sb("scl", [P, 4])
        scw = sb("scw", [P, 2])
        pbias = sb("pbias", [P, 12])
        bhn = sb("bhn", [P, 4])
        h16 = sb("h16", [P, 2, 2, 2, 4], F16)
        hf = sb("hf", [P, 2, 2, 4])
        chain = sb("chain", [P, 24])
        sums = sb("sums", [P, 2, 24])
        rz = sb("rz", [P, 2, 16])
        vn = sb("vn", [P, 2, 8])
        zmul = sb("zmul", [P, 2, 4])
        zadd = sb("zadd", [P, 2, 4])
        minus_half = sb("minus_half", [P, 1])
        ebias = sb("ebias", [P, KT])
        warm = sb("warm", [P, 1])

        d_cnt = nc.dram_tensor("edge_counts", [NT, NP, N], F32, kind="Internal").ap()
        d_wt = nc.dram_tensor("edge_weights", [NT, NP, N], F32, kind="Internal").ap()
        d_adj = nc.dram_tensor("adj_rows", [NT, NP, N], F32, kind="Internal").ap()
        d_invdeg = nc.dram_tensor("invdeg", [NP, N], F32, kind="Internal").ap()

        sems = {}

        def s(name):
            if name not in sems:
                sems[name] = sem(name)
            return sems[name]

        block = ctx.enter_context(nc.Block())

        def w_rows(dst_ap, src):
            return dst_ap, src.rearrange("(k p) n -> p k n", p=P)

        def tiles(ap):
            return ap.rearrange("t p n -> p t n")

        @block.sync
        def _(sp):
            for a, name in enumerate(("src", "dst")):
                sp.dma_start(e_int[0:EH, a], io[name].rearrange("(h q e) -> q h e", h=2, e=EP)).then_inc(s("edges_in"), 16)
            sp.dma_start(e_stage[0:EH, 2], io["edge_weight"].rearrange("(h q e) -> q h e", h=2, e=EP)).then_inc(s("edges_in"), 16)
            sp.dma_start(r1[:], io["xT"].rearrange("(k p) n -> p k n", p=P)).then_inc(s("xcols_in"), 16)
            sp.dma_start(*w_rows(wslot(0), io["W1"])).then_inc(s("w1_in"), 16)
            sp.dma_start(*w_rows(wslot(1), io["W2"])).then_inc(s("w2_in"), 16)
            sp.dma_start(bcol[:], io["bcol"]).then_inc(s("small_in"), 16)
            sp.dma_start(gate_w[:], io["gate_W"].rearrange("(k p) e -> p k e", p=P)).then_inc(s("small_in"), 16)
            sp.dma_start(gate_b[:], io["gate_b"].partition_broadcast(P)).then_inc(s("small_in"), 16)
            sp.dma_start(xr[0:NP], io["x"].rearrange("(t p) d -> p t d", p=NP)).then_inc(s("x_in"), 16)
            sp.dma_start(fc_bias, io["b_fc"].partition_broadcast(P)).then_inc(s("bfc_in"), 16)
            sp.wait_ge(s("win_counts"), NW)
            for h in range(2):
                half = slice(5 * h, 5 * h + 5)
                sp.dma_start(tiles(d_cnt[half]), adj_v[0:NP, half]).then_inc(s(f"cnt_out{h}"), 16)
            sp.wait_ge(s("win_weights"), NW + 2)
            sp.dma_start(tiles(d_wt), wt_v[0:NP]).then_inc(s("wt_out"), 16)
            sp.wait_ge(s("invdeg_ready"), 1)
            sp.dma_start(d_invdeg, invdeg_row[0:NP]).then_inc(s("invdeg_out"), 16)
            sp.wait_ge(s("tr_stored"), 3 * NT)
            sp.dma_start(tiles(d_adj), wt_v[0:NP]).then_inc(s("adj_out"), 16)
            sp.wait_ge(s("h2_done"), NT)
            for g, place in enumerate((weight(whh[0]), weight(whh[1]), wslot(1))):
                sp.dma_start(*w_rows(place, io["W_hhT"][:, g * D:(g + 1) * D])).then_inc(s("whh_in"), 16)
            sp.wait_ge(s("whh_split"), 2)
            sp.dma_start(*w_rows(wslot(0), io["W_ihT"][:, 0:D])).then_inc(s("wih_in0"), 16)
            sp.wait_ge(s("whh_split"), 3)
            sp.dma_start(*w_rows(wslot(1), io["W_ihT"][:, D:2 * D])).then_inc(s("wih_in1"), 16)
            sp.wait_ge(s("conv2_done"), 12)
            sp.dma_start(*w_rows(w_fc, io["W_fc"])).then_inc(s("wfc_in"), 16)
            sp.wait_ge(s("adj_out"), 16)
            sp.dma_start(adj_v[0:NP], tiles(d_adj)).then_inc(s("adj_in"), 16)
            sp.wait_ge(s("pre_done"), 12)
            sp.dma_start(*w_rows(wslot(0), io["W_ihT"][:, 2 * D:3 * D])).then_inc(s("wih_in2"), 16)
            sp.wait_ge(s("pre_done"), 36)
            sp.dma_start(*w_rows(wslot(0), io["l1_W1"])).then_inc(s("l1w1_in"), 16)
            sp.dma_start(*w_rows(wslot(1), io["l1_W2"])).then_inc(s("l1w2_in"), 16)
            for c in range(2):
                sp.wait_ge(s(f"gru_put{c}"), N + 2)
            sp.dma_start(l1_bias, io["l1_b1"].partition_broadcast(P)).then_inc(s("l1b1_in"), 16)
            sp.dma_start(invdeg_row[0:NP], d_invdeg).then_inc(s("invdeg_in"), 16)
            sp.wait_ge(s("cnt_out0"), 16)
            sp.wait_ge(s("cnt_out1"), 16)
            sp.dma_start(wt_v[0:NP], tiles(d_cnt)).then_inc(s("cnt_in"), 16)
            sp.wait_ge(s("l1h1_stored"), NT)
            sp.dma_start(l1_bias, io["l1_b2"].partition_broadcast(P)).then_inc(s("l1b2_in"), 16)
            sp.wait_ge(s("l1out_done"), NT)
            with sp.Fori(0, NE) as e:
                sp.wait_ge(s("layer1_done"), e * 12)
                for m, name in enumerate(("Wl0", "Wr0")):
                    sp.dma_start(l2w[m], io[name][bass.ds(e, 1)].rearrange("e (k p) n -> p (e k) n", p=P)).then_inc(s("ew0_in"), 16)
                sp.wait_ge(s("eout_stored"), e * NT)
                sp.dma_start(l2_bias, io["bl1"][bass.ds(e, 1)].rearrange("e d -> (e d)").partition_broadcast(P)).then_inc(s("eb_in"), 16)
                for m, name in enumerate(("Wl1", "Wr1")):
                    sp.dma_start(l2w[2 + m], io[name][bass.ds(e, 1)].rearrange("e (k p) n -> p (e k) n", p=P)).then_inc(s("ew1_in"), 16)
            sp.dma_start(*w_rows(wslot(0), io["l3_W"])).then_inc(s("l3w_in"), 16)
            sp.wait_ge(s("eadd"), NE * NT)
            sp.wait_ge(s("wt_out"), 16)
            sp.dma_start(adj_v[0:NP], tiles(d_wt)).then_inc(s("wt_in"), 16)
            for t in range(NT):
                sp.wait_ge(s("final_ln"), t + 1)
                sp.dma_start(io["out"][t * NP:(t + 1) * NP], xr[0:NP, t]).then_inc(s("out_stored"), 16)
            sp.wait_ge(s("out_stored"), 16 * NT)

        @block.gpsimd
        def _(pool):
            pool.memset(ident[:], 0.0).then_inc(s("ident0"), 1)
            pool.memset(ones[:], 1.0).then_inc(s("const"), 1)
            pool.memset(zero_b, 0.0).then_inc(s("const"), 1)
            pool.memset(minus_half[:], -0.5).then_inc(s("const"), 1)
            pool.memset(big[:, N * 12:], 0.0).then_inc(s("const"), 1)
            pool.wait_ge(s("ident0"), 1)
            pool.affine_select(out=ident[:], in_=ident[:], compare_op=ALU.not_equal, fill=1.0, base=0,
                               pattern=[[-1, P]], channel_multiplier=1).then_inc(s("const"), 1)
            small = dict(allow_small_or_imprecise_dtypes=True)
            pool.iota(iota16, [[1, N]], base=0, channel_multiplier=0, **small).then_inc(s("const"), 1)
            pool.iota(tile_no[:, 0], [[1, ET]], base=1, channel_multiplier=0, **small).then_inc(s("const"), 1)
            pool.iota(tile_no[:, 1], [[-1, ET]], base=ET, channel_multiplier=0, **small).then_inc(s("const"), 1)
            pool.iota(w_lim, [[WD, 2]], base=0, channel_multiplier=WD, **small).then_inc(s("const"), 1)
            pool.sem_inc(s("win_weights"), 2)
            with pool.Fori(0, NW // 2) as i:
                for u in range(2):
                    w = 2 * i + u
                    c = cparts[u][0:NP]
                    pool.wait_ge(s("parts_ready"), w + 1)
                    pool.tensor_tensor(c[:, :, 0:WD], c[:, :, 0:WD], c[:, :, WD:2 * WD], ALU.add).then_inc(s("parts_half"), 1)
                    pool.wait_ge(s("parts_half"), w + 1)
                    pool.tensor_tensor(c[:, :, 0:WD], c[:, :, 0:WD], c[:, :, 2 * WD:3 * WD], ALU.add).then_inc(s("parts_sum"), 1)
                    pool.wait_ge(s("parts_sum"), w + 1)
                    pool.tensor_copy(wt_v[0:NP, :, bass.ds(w * WD, WD)], c[:, :, 0:WD]).then_inc(s("win_weights"), 1)
            for c, (n0, n1) in enumerate(NCH):
                pool.wait_ge(s("deg1"), c + 1)
                pool.tensor_tensor(inv_row[:, n0:n1], inv_row[:, n0:n1], minus_half[:, 0:1].to_broadcast([P, n1 - n0]), ALU.pow).then_inc(s("inv_ready"), 1)
            pool.wait_ge(s("wmax_part"), 1)
            pool.partition_all_reduce(wmax[:, 7:8], wmax[:, 6:7], P, bass.bass_isa.ReduceOp.max).then_inc(s("wmax_all"), 1)
            for c in range(2):
                pool.sem_inc(s(f"gru_kept{c}"), 2)
            with pool.Fori(0, N // 2) as i:
                for u in range(2):
                    t = 2 * i + u
                    for c in range(2):
                        pool.wait_ge(s(f"gru_h{c}"), 2 * t + 2)
                        pool.tensor_copy(r1[:, 2 * c:2 * c + 2, bass.ds(t, 1)], hf[:, 1 - u, c, 1:4:2]).then_inc(s(f"gru_kept{c}"), 1)
            for n in range(4 * NT + KT):
                p = slice(0, P) if NT <= n < NT + KT else slice(0, NP)
                pool.wait_ge(s("var"), n + 1)
                pool.tensor_tensor(mv[p, 2:3], mv[p, 2:3], minus_half[p, 0:1], ALU.pow).then_inc(s("root"), 1)

        @block.tensor
        def _(pe):
            mm = nc.tensor.matmul

            def out_rows(i, bank0, done, stored, base=0):
                if i >= 4:
                    pe.wait_ge(s(stored), base + i - 3)
                return psum[:, bank0 + i % 4]

            def rows_product(name, bank0, cols, w, base=0, before=None):
                for t in range(NT):
                    if before:
                        before(t)
                    o = out_rows(t, bank0, None, f"{name}_stored", base)
                    for k in range(KT):
                        m = mm(o[0:NP], cols[:, k, t * NP:(t + 1) * NP], w[:, k], start=(k == 0), stop=(k == KT - 1))
                    m.then_inc(s(f"{name}_done"), 1)

            def agg_cols(name, bank0, rows, mat):
                i = 0
                for f in range(KT):
                    for n0, n1 in NCH:
                        o = out_rows(i, bank0, None, f"{name}_stored")
                        for t in range(NT):
                            m = mm(o[:, 0:n1 - n0], rows[0:NP, t, f * P:(f + 1) * P], mat[0:NP, t, n0:n1],
                                   start=(t == 0), stop=(t == NT - 1))
                        m.then_inc(s(f"{name}_done"), 1)
                        i += 1

            def turn(name, t, bank0):
                pe.wait_ge(s(f"{name}_ln"), t + 1)
                if t >= 4:
                    pe.wait_ge(s(f"{name}_turned"), t - 3)
                for k in range(KT):
                    m = nc.tensor.transpose(psum[:, bank0 + t % 4, k * NP:(k + 1) * NP], xr[0:NP, t, k * P:(k + 1) * P], ident[0:NP, 0:NP])
                m.then_inc(s(f"{name}_turn"), 1)

            pe.wait_ge(s("const"), 9)
            pe.wait_ge(s("edges_f"), 1)
            for a in range(3):
                for h in range(2):
                    m = nc.tensor.transpose(psum[0:EP, a, h * EH:(h + 1) * EH], e_stage[0:EH, a, h], ident[0:EH, 0:EH])
            m.then_inc(s("edges_turn"), 1)
            pe.wait_ge(s("limits"), 1)
            for a in range(2):
                for h in range(2):
                    m = mm(psum[0:NW, 3, a * ET + h * EH:a * ET + (h + 1) * EH], t_lim[:, a, h:h + 1].to_broadcast([EH, NW]), ident[0:EH, 0:EH],
                           start=True, stop=True, skip_group_check=True)
            m.then_inc(s("limits_all"), 1)
            pe.wait_ge(s("span"), 1)
            for a in range(2):
                m = mm(psum[0:1, 4, a * NW:(a + 1) * NW], span[0:NW, a:a + 1], ident[0:NW, 0:NW], start=True, stop=True, skip_group_check=True)
            m.then_inc(s("span_row"), 1)
            pe.wait_ge(s("bounds"), 1)
            with pe.Fori(0, NW // 2) as i:
                for u in range(2):
                    w = 2 * i + u
                    blocks = pe.value_load(bounds[0:1, 2, bass.ds(w, 1)], min_val=1, max_val=ET)
                    before = pe.value_load(bounds[0:1, 4, bass.ds(w, 1)], min_val=0, max_val=GMAX)
                    pe.wait_ge(s("win_read"), w + 1)
                    for b in range(2):
                        mm(psum[0:NP, 2 * u + b, 0:500], zero_b[0:NP, 0:NP], zero_b[0:NP], start=True, stop=False, skip_group_check=True)
                    with pe.Fori(0, blocks) as j:
                        g = before + j
                        slot = pe.snap(g % RING)
                        pe.wait_ge(s("hot_ready"), g + 1)
                        for t in range(NT):
                            m = mm(psum[0:NP, 2 * u + t // 5, (t % 5) * 100:(t % 5) * 100 + 100],
                                   src_hot[0:EP, bass.ds(slot * N + t * NP, NP)], dst_hot[0:EP, bass.ds(slot * 100, 100)],
                                   start=False, stop=False, skip_group_check=True)
                        m.then_inc(s("hot_used"), 1)
                    for b in range(2):
                        m = mm(psum[0:NP, 2 * u + b, 0:1], zero_b[0:NP, 0:NP], zero_b[0:NP, 0:1], start=False, stop=True, skip_group_check=True)
                    m.then_inc(s("win_done"), 1)
            pe.wait_ge(s("win_counts"), NW)
            for c, (n0, n1) in enumerate(NCH):
                for t in range(NT):
                    m = mm(psum[:, 4 + c, 0:n1 - n0], ones[0:NP], adj_v[0:NP, t, n0:n1], start=(t == 0), stop=(t == NT - 1))
                m.then_inc(s("deg"), 1)
            pe.wait_ge(s("xcols_in"), 16)
            pe.wait_ge(s("w1_in"), 16)
            pe.wait_ge(s("win_read"), NW + 2)
            rows_product("h1", 0, r1, wslot(0))
            pe.wait_ge(s("inv_ready"), 3)
            for t in range(NT):
                m = mm(psum[0:NP, 7, t:t + 1], inv_row[0:1, t * NP:(t + 1) * NP], ones[0:1, 0:1], start=True, stop=True, skip_group_check=True)
            m.then_inc(s("inv_col_done"), 1)
            pe.wait_ge(s("h1_stored"), NT)
            pe.wait_ge(s("norm"), NT)
            agg_cols("conv1", 4, hn, adj_v)
            for d in range(NT):
                for q in range(3):
                    n = 3 * d + q
                    if n >= 4:
                        pe.wait_ge(s("tr_stored"), n - 3)
                    for t in range(4 * q, min(4 * q + 4, NT)):
                        m = nc.tensor.transpose(psum[0:NP, n % 4, (t - 4 * q) * NP:(t - 4 * q + 1) * NP], adj_v[0:NP, t, d * NP:(d + 1) * NP], ident[0:NP, 0:NP])
                    m.then_inc(s("tr_done"), 1)
            pe.wait_ge(s("conv1_stored"), 12)
            pe.wait_ge(s("w2_in"), 16)
            rows_product("h2", 4, r2, wslot(1))
            pe.wait_ge(s("h2_stored"), NT)
            pe.wait_ge(s("tr_stored"), 3 * NT)
            agg_cols("conv2", 0, hn, adj_v)
            pe.wait_ge(s("conv2_stored"), 12)
            i = 0
            for g in range(3):
                pe.wait_ge(s(f"wih_in{g}"), 16)
                for j in range(KT):
                    for n0, n1 in NCH:
                        o = out_rows(i, 4, None, "pre_stored")
                        for k in range(KT):
                            m = mm(o[:, 0:n1 - n0], wslot(g % 2)[:, k, j * P:(j + 1) * P], r1[:, k, n0:n1], start=(k == 0), stop=(k == KT - 1))
                        m.then_inc(s("pre_done"), 1)
                        i += 1
            pe.wait_ge(s("gru_init"), 1)
            pe.wait_ge(s("whh_split"), 3)

            def gru_half(u, c, kc):
                for k in (2 * kc, 2 * kc + 1):
                    for part in range(2):
                        for q in range(6):
                            g, j = q // 2, 2 * c + q % 2
                            m = mm(psum[:, 2 * u + c, 4 * q:4 * q + 2], whh16[g][:, part, k, j * P:(j + 1) * P], h16[:, u, kc, :, 2 * (k % 2) + 1],
                                   start=(k == 0 and part == 0 and q == 0), stop=(k == KT - 1 and part == 1), skip_group_check=True)
                return m

            with pe.Fori(0, N // 2) as i:
                for u in range(2):
                    t = 2 * i + u
                    pe.wait_ge(s("gru_state0"), t + 1)
                    for c in range(2):
                        pe.wait_ge(s(f"gru_put{c}"), t + 1)
                        gru_half(u, c, 0)
                    pe.wait_ge(s("gru_state1"), t + 1)
                    for c in range(2):
                        gru_half(u, c, 1).then_inc(s(f"gru_mm{c}"), 1)
            for c in range(2):
                pe.wait_ge(s(f"gru_kept{c}"), N + 2)
                pe.wait_ge(s(f"gru_put{c}"), N + 2)
            pe.wait_ge(s("wfc_in"), 16)
            rows_product("fc", 4, r1, w_fc, before=lambda t: turn("fc", t - 3, 0) if t >= 3 else None)
            for t in range(NT - 3, NT):
                turn("fc", t, 0)
            pe.wait_ge(s("fc_turned"), NT)
            pe.wait_ge(s("l1w1_in"), 16)
            rows_product("l1h1", 4, r2, wslot(0))
            pe.wait_ge(s("l1h1_stored"), NT)
            pe.wait_ge(s("adj_in"), 16)
            agg_cols("l1agg", 0, hn, adj_v)
            pe.wait_ge(s("l1norm"), KT)
            pe.wait_ge(s("l1w2_in"), 16)
            rows_product("l1h2", 4, r1, wslot(1))
            pe.wait_ge(s("l1h2_stored"), NT)
            for d in range(NT):
                if d >= 3:
                    turn("l1out", d - 3, 4)
                o = out_rows(d, 0, None, "l1out_stored")
                for t in range(NT):
                    m = mm(o[0:NP], adj_v[0:NP, t, d * NP:(d + 1) * NP], hn[0:NP, t], start=(t == 0), stop=(t == NT - 1))
                m.then_inc(s("l1out_done"), 1)
            for t in range(NT - 3, NT):
                turn("l1out", t, 4)
            pe.wait_ge(s("l1out_turned"), NT)
            for t in range(NT):
                for k in range(KT):
                    m = mm(psum[0:NP, 0, t * NE:(t + 1) * NE], r2[:, k, t * NP:(t + 1) * NP], gate_w[:, k], start=(k == 0), stop=(k == KT - 1), skip_group_check=True)
            m.then_inc(s("logits"), 1)
            pe.wait_ge(s("mean_ready"), NT)
            agg_cols("aggx", 4, xr, wt_v)
            pe.wait_ge(s("aggx_stored"), 12)
            pe.wait_ge(s("gates_read"), 1)
            with pe.Fori(0, NE // 2) as ei:
                for u in range(2):
                    e = 2 * ei + u
                    b0, b1 = (0, 4) if u == 0 else (4, 0)
                    pe.wait_ge(s("ew0_in"), e * 32 + 32)
                    i = 0
                    for f in range(KT):
                        for n0, n1 in NCH:
                            o = out_rows(i, b0, None, "layer1_stored", e * 12)
                            for k in range(KT):
                                mm(o[:, 0:n1 - n0], l2w[0][:, k, f * P:(f + 1) * P], agg_x[k][:, n0:n1], start=(k == 0), stop=False)
                                m = mm(o[:, 0:n1 - n0], l2w[1][:, k, f * P:(f + 1) * P], r2[:, k, n0:n1], start=False, stop=(k == KT - 1))
                            m.then_inc(s("layer1_done"), 1)
                            i += 1
                    pe.wait_ge(s("layer1_stored"), e * 12 + 12)
                    pe.wait_ge(s("ew1_in"), e * 32 + 32)
                    pe.wait_ge(s("eout_stored"), e * NT)
                    rows_product("u", b1, r1, l2w[2], base=e * NT)
                    pe.wait_ge(s("u_stored"), e * NT + NT)
                    for d in range(NT):
                        o = out_rows(d, b0, None, "eout_stored", e * NT)
                        for k in range(KT):
                            mm(o[0:NP], r1[:, k, d * NP:(d + 1) * NP], l2w[3][:, k], start=(k == 0), stop=False)
                        for t in range(NT):
                            m = mm(o[0:NP], wt_v[0:NP, t, d * NP:(d + 1) * NP], hn[0:NP, t], start=False, stop=(t == NT - 1))
                        m.then_inc(s("eout_done"), 1)
            for t in range(NT):
                turn("l2", t, 0)
            pe.wait_ge(s("l2_turned"), NT)
            pe.wait_ge(s("l3w_in"), 16)
            rows_product("z", 4, r2, wslot(0))
            pe.wait_ge(s("z_stored"), NT)
            pe.wait_ge(s("wt_in"), 16)
            for d in range(NT):
                o = out_rows(d, 0, None, "l3_stored")
                for t in range(NT):
                    m = mm(o[0:NP], adj_v[0:NP, t, d * NP:(d + 1) * NP], hn[0:NP, t], start=(t == 0), stop=(t == NT - 1))
                m.then_inc(s("l3_done"), 1)

        @block.scalar
        def _(act):
            def take_cols(name, bank0, dst, func, bias=None, base=0, bias_at=None):
                i = 0
                for f in range(KT):
                    for n0, n1 in NCH:
                        act.wait_ge(s(f"{name}_done"), base + i + 1)
                        o = psum[:, bank0 + i % 4, 0:n1 - n0]
                        to = dst[f][:, n0:n1] if isinstance(dst, list) else dst[:, f, n0:n1]
                        if func is None:
                            m = nc.scalar.copy(to, o)
                        else:
                            m = nc.scalar.activation(to, o, func, bias=bias[:, f:f + 1])
                        m.then_inc(s(f"{name}_stored"), 1)
                        i += 1

            def take_rows(name, bank0, base=0):
                for t in range(NT):
                    act.wait_ge(s(f"{name}_done"), base + t + 1)
                    nc.scalar.copy(hn[0:NP, t], psum[0:NP, bank0 + t % 4]).then_inc(s(f"{name}_stored"), 1)

            def take_turned(name, bank0):
                for t in range(NT):
                    act.wait_ge(s(f"{name}_turn"), t + 1)
                    nc.scalar.copy(r2[:, :, t * NP:(t + 1) * NP], psum[:, bank0 + t % 4, 0:4 * NP].rearrange("p (k n) -> p k n", k=KT)).then_inc(s(f"{name}_turned"), 1)

            act.sem_inc(s("win_read"), 2)
            with act.Fori(0, NW // 2) as i:
                for u in range(2):
                    w = 2 * i + u
                    acc = psum[0:NP, 2 * u:2 * u + 2, 0:500].rearrange("p b (t c) -> p b t c", c=100)
                    act.wait_ge(s("win_done"), w + 1)
                    nc.scalar.copy(adj_v[0:NP, :, bass.ds(w * WD, WD)].rearrange("p (b t) c -> p b t c", b=2), acc[:, :, :, 0:WD]).then_inc(s("win_counts"), 1)
                    act.wait_ge(s("win_weights"), w + 1)
                    nc.scalar.copy(cparts[u][0:NP].rearrange("p (b t) c -> p b t c", b=2), acc[:, :, :, WD:4 * WD]).then_inc(s("parts_ready"), 1)
                    act.wait_ge(s("parts_ready"), w + 1)
                    act.sem_inc(s("win_read"), 1)
            act.wait_ge(s("win_weights"), NW + 2)
            take_rows("h1", 0)
            act.wait_ge(s("small_in"), 48)
            act.wait_ge(s("fc_bias_used"), 1)
            take_cols("conv1", 4, r2, ACT.Relu, b1c)
            take_rows("h2", 4)
            take_cols("conv2", 0, r1, ACT.Relu, b2c)
            act.wait_ge(s("gru_init"), 1)
            nc.scalar.activation(warm[:], scl[:, 2:3], ACT.Sigmoid).then_inc(s("warm"), 1)

            def put(t, u, c):
                nc.scalar.copy(psum[:, 2 * u + c, 3:24:4], big[:, bass.ds(t * 12 + c * 6, 6)]).then_inc(s(f"gru_put{c}"), 1)

            for u in range(2):
                for c in range(2):
                    put(u, u, c)
            with act.Fori(0, N // 2) as i:
                for u in range(2):
                    t = 2 * i + u

                    def sigmoids(c):
                        act.wait_ge(s(f"gru_sums{c}"), t + 1)
                        nc.scalar.activation(rz[:, c, 3:16:4], sums[:, c, 3:16:4], ACT.Sigmoid, scale=scl[:, 2:3]).then_inc(s(f"gru_rz{c}"), 1)

                    def new(c):
                        act.wait_ge(s(f"gru_n_in{c}"), t + 1)
                        nc.scalar.activation(zadd[:, c, 0:4:2], vn[:, c, 3:8:4], ACT.Tanh, scale=scl[:, 3:4]).then_inc(s(f"gru_n{c}"), 1)

                    sigmoids(0)
                    new(0)
                    sigmoids(1)
                    put(t + 2, u, 0)
                    new(1)
                    put(t + 2, u, 1)
            take_turned("fc", 0)
            take_cols("l1agg", 0, r1, None)
            for f in range(KT):
                act.wait_ge(s("bn_ready"), f + 1)
                nc.scalar.activation(r1[:, f], r1[:, f], ACT.Relu, scale=bnc[:, 0, f:f + 1], bias=bnc[:, 1, f:f + 1]).then_inc(s("l1norm"), 1)
            take_turned("l1out", 4)
            act.wait_ge(s("gate_in"), 1)
            nc.scalar.activation(gates[0:NP], gates[0:NP], ACT.Exp).then_inc(s("gate_exp"), 1)
            act.wait_ge(s("mean_ready"), NT)
            take_cols("aggx", 4, agg_x, None)
            with act.Fori(0, NE // 2) as ei:
                for u in range(2):
                    e = 2 * ei + u
                    b0, b1 = (0, 4) if u == 0 else (4, 0)
                    nc.scalar.copy(ebias[:], blc[:, bass.ds(e * KT, KT)]).then_inc(s("ebias"), 1)
                    act.wait_ge(s("ebias"), e + 1)
                    i = 0
                    for f in range(KT):
                        for n0, n1 in NCH:
                            act.wait_ge(s("layer1_done"), e * 12 + i + 1)
                            nc.scalar.activation(r1[:, f, n0:n1], psum[:, b0 + i % 4, 0:n1 - n0], ACT.Relu,
                                                 bias=ebias[:, f:f + 1]).then_inc(s("layer1_stored"), 1)
                            i += 1
                    take_rows("u", b1, base=e * NT)
            take_turned("l2", 0)
            take_rows("z", 4)

        @block.vector
        def _(dve):
            v = nc.vector
            linked, roots = [0], [0]

            def link(ins):
                linked[0] += 1
                ins.then_inc(s("dve_link"), 1)
                dve.wait_ge(s("dve_link"), linked[0])

            def ln_rows(t, name):
                x = xr[0:NP, t]
                link(v.bn_stats(stat[0:NP, 0], x))
                link(v.bn_aggr(mv[0:NP, 0:2], stat[0:NP, 0]))
                roots[0] += 1
                v.tensor_scalar(mv[0:NP, 2:3], mv[0:NP, 1:2], LN_EPS, None, ALU.add).then_inc(s("var"), 1)
                dve.wait_ge(s("root"), roots[0])
                v.tensor_scalar(x, x, mv[0:NP, 0:1], mv[0:NP, 2:3], ALU.subtract, ALU.mult).then_inc(s(name), 1)

            dve.wait_ge(s("edges_in"), 48)
            link(v.tensor_copy(e_stage[0:EH, 0:2], e_int[0:EH]))
            dve.sem_inc(s("edges_f"), 1)
            link(v.tensor_reduce(t_lim[:, 0], e_stage[0:EH, 1], AX.X, ALU.min))
            link(v.tensor_reduce(t_lim[:, 1], e_stage[0:EH, 1], AX.X, ALU.max))
            dve.sem_inc(s("limits"), 1)
            dve.wait_ge(s("edges_turn"), 1)
            link(v.tensor_copy(e_col[0:EP], psum[0:EP, 0:3, 0:ET]))
            link(v.memset(w_part[0:EP, :, 0], 1.0))
            rest = e_w
            for a in range(3):
                link(v.tensor_copy(w_bf[0:EP], rest[0:EP]))
                link(v.tensor_copy(w_part[0:EP, :, a + 1], w_bf[0:EP]))
                if a < 2:
                    link(v.tensor_tensor(w_res[0:EP, a], rest[0:EP], w_bf[0:EP], ALU.subtract))
                    rest = w_res[:, a]
            dve.wait_ge(s("const"), 9)
            dve.wait_ge(s("limits_all"), 1)
            link(v.tensor_scalar(hit[0:NW], psum[0:NW, 3, 0:ET], w_lim[0:NW, 1:2], None, ALU.is_lt))
            link(v.scalar_tensor_tensor(out=hit_b[0:NW], in0=psum[0:NW, 3, ET:2 * ET], scalar=w_lim[0:NW, 0:1], in1=hit[0:NW], op0=ALU.is_ge, op1=ALU.mult))
            for a in range(2):
                link(v.tensor_tensor(hit[0:NW], hit_b[0:NW], tile_no[0:NW, a], ALU.mult))
                link(v.tensor_reduce(span[0:NW, a:a + 1], hit[0:NW], AX.X, ALU.max))
            dve.sem_inc(s("span"), 1)
            dve.wait_ge(s("span_row"), 1)
            last, first, count, total, before = (row[:, a] for a in range(5))
            link(v.tensor_scalar(first, psum[0:1, 4, NW:2 * NW], -1.0, float(ET), ALU.mult, ALU.add))
            link(v.tensor_scalar(first, first, float(ET - 1), None, ALU.min))
            link(v.tensor_copy(last, psum[0:1, 4, 0:NW]))
            link(v.scalar_tensor_tensor(out=last, in0=first, scalar=1.0, in1=last, op0=ALU.add, op1=ALU.max))
            link(v.tensor_tensor(count, last, first, ALU.subtract))
            link(v.tensor_tensor_scan(total, ones[0:1, 0:NW], count, 0.0, ALU.mult, ALU.add))
            link(v.tensor_tensor(before, total, count, ALU.subtract))
            offset = row[:, 5]
            link(v.tensor_scalar(before, before, float(ET), None, ALU.add))
            link(v.tensor_tensor(offset, before, first, ALU.subtract))
            for a, val in enumerate((first, last, count, offset, before)):
                link(v.tensor_copy(bounds[:, a], val))
            dve.sem_inc(s("bounds"), 1)
            dve.sem_inc(s("hot_used"), RING + ET)
            dve.sem_inc(s("hot_ready"), ET)
            with dve.Fori(0, NW) as w:
                tile0 = dve.value_load(bounds[0:1, 0, bass.ds(w, 1)], min_val=0, max_val=ET - 1)
                end = dve.value_load(bounds[0:1, 1, bass.ds(w, 1)], min_val=1, max_val=ET)
                offset = dve.value_load(bounds[0:1, 3, bass.ds(w, 1)], min_val=0, max_val=GMAX)
                with dve.Fori(tile0, end) as tile:
                    g = offset + tile
                    slot = dve.snap(g % RING)
                    dve.wait_ge(s("hot_used"), g + 1)
                    v.tensor_scalar(src_hot[0:EP, bass.ds(slot * N, N)], iota16[0:EP], e_src[0:EP, bass.ds(tile, 1)], None, ALU.is_equal)
                    v.scalar_tensor_tensor(
                        out=dst_hot[0:EP, bass.ds(slot * 100, 100)].rearrange("p (a c) -> p a c", a=4),
                        in0=iota16[0:EP, bass.ds(w * WD, WD)].unsqueeze(1).broadcast_to([EP, 4, WD]), scalar=e_dst[0:EP, bass.ds(tile, 1)],
                        in1=w_part[0:EP, bass.ds(tile, 1), :].rearrange("p t a -> p (t a)").unsqueeze(2).broadcast_to([EP, 4, WD]),
                        op0=ALU.is_equal, op1=ALU.mult).then_inc(s("hot_ready"), 1)
            dve.wait_ge(s("x_in"), 16)
            dve.wait_ge(s("bfc_in"), 16)
            link(v.tensor_tensor(xr[0:NP], xr[0:NP], fc_bias[0:NP].unsqueeze(1).broadcast_to([NP, NT, D]), ALU.add))
            dve.sem_inc(s("fc_bias_used"), 1)
            for c, (n0, n1) in enumerate(NCH):
                dve.wait_ge(s("deg"), c + 1)
                v.tensor_scalar(inv_row[:, n0:n1], psum[:, 4 + c, 0:n1 - n0], 1.0, None, ALU.add).then_inc(s("deg1"), 1)
                link(v.tensor_scalar(invdeg_row[:, n0:n1], psum[:, 4 + c, 0:n1 - n0], 1.0, None, ALU.max))
            link(v.reciprocal(invdeg_row, invdeg_row))
            dve.sem_inc(s("invdeg_ready"), 1)
            dve.wait_ge(s("inv_col_done"), 1)
            link(v.tensor_copy(inv_col[0:NP], psum[0:NP, 7, 0:NT]))
            for t in range(NT):
                dve.wait_ge(s(f"cnt_out{t // 5}"), 16)
                diag = adj_v[0:NP, t, t * NP:(t + 1) * NP]
                link(v.tensor_tensor(diag, diag, ident[0:NP, 0:NP], ALU.add))
                v.scalar_tensor_tensor(out=adj_v[0:NP, t], in0=adj_v[0:NP, t], scalar=inv_col[0:NP, t:t + 1], in1=inv_row[0:NP],
                                       op0=ALU.mult, op1=ALU.mult).then_inc(s("norm"), 1)
            dve.wait_ge(s("wt_out"), 16)
            for d in range(NT):
                for q in range(3):
                    n = 3 * d + q
                    dve.wait_ge(s("tr_done"), n + 1)
                    width = min(4, NT - 4 * q) * NP
                    v.tensor_copy(wt_v[0:NP, d, 4 * q * NP:4 * q * NP + width], psum[0:NP, n % 4, 0:width]).then_inc(s("tr_stored"), 1)
            dve.wait_ge(s("whh_in"), 48)
            for g, place in enumerate((whh[0], whh[1], ws[:, WSLOT:2 * WSLOT])):
                link(v.tensor_reduce(wmax[:, 2 * g:2 * g + 1], place, AX.X, ALU.max))
                link(v.tensor_reduce(wmax[:, 2 * g + 1:2 * g + 2], place, AX.X, ALU.min))
            link(v.tensor_scalar(wmax[:, 8:11], wmax[:, 1:6:2], -1.0, None, ALU.mult))
            link(v.tensor_tensor(wmax[:, 8:11], wmax[:, 8:11], wmax[:, 0:6:2], ALU.max))
            link(v.tensor_reduce(wmax[:, 6:7], wmax[:, 8:11], AX.X, ALU.max))
            dve.sem_inc(s("wmax_part"), 1)
            dve.wait_ge(s("wmax_all"), 1)
            link(v.tensor_scalar(wmax[:, 7:8], wmax[:, 7:8], 2.0 ** -60, None, ALU.max))
            bits = wmax[:, 7:8].bitcast(I32)
            link(v.tensor_scalar(bits, bits, 0x7F800000, None, ALU.bitwise_and))
            one = float(1 << 23)
            scl_i, scw_i = scl[:].bitcast(I32), scw[:].bitcast(I32)
            link(v.tensor_scalar(scw_i[:, 0:1], bits, -1.0, (13 + 2 * 127) * one, ALU.mult, ALU.add))
            link(v.tensor_scalar(scl_i[:, 0:1], scw_i[:, 0:1], 12 * one, None, ALU.add))
            link(v.tensor_scalar(scl_i[:, 2:3], scl_i[:, 0:1], -1.0, 2 * 127 * one, ALU.mult, ALU.add))
            link(v.tensor_scalar(scw[:, 1:2], scw[:, 0:1], -1.0, None, ALU.mult))
            link(v.tensor_scalar(scl[:, 1:2], scl[:, 0:1], -1.0, None, ALU.mult))
            link(v.tensor_scalar(scl[:, 3:4], scl[:, 2:3], -1.0, None, ALU.mult))

            def split(g, source):
                flat = whh[g].bitcast(F16)
                hi, lo = flat[:, 0:WSLOT], flat[:, WSLOT:2 * WSLOT]
                sc = scw[:, 1:2] if g == 1 else scw[:, 0:1]
                link(v.tensor_scalar(hi, source, sc, None, ALU.mult))
                link(v.scalar_tensor_tensor(out=lo, in0=source, scalar=sc, in1=hi, op0=ALU.mult, op1=ALU.subtract))
                dve.sem_inc(s("whh_split"), 1)

            dve.wait_ge(s("h1_done"), NT)
            for g in range(2):
                link(v.tensor_copy(ws[:, 0:WSLOT], whh[g]))
                split(g, ws[:, 0:WSLOT])
            dve.wait_ge(s("conv2_done"), 12)
            split(2, ws[:, WSLOT:2 * WSLOT])
            link(v.tensor_tensor(pbias[:, 0:8], bihc[:, 0:8], bhhc[:, 0:8], ALU.add))
            link(v.tensor_copy(pbias[:, 8:12], bihc[:, 8:12]))
            for g in range(3):
                sc = scl[:, 1:2] if g == 1 else scl[:, 0:1]
                link(v.tensor_scalar(pbias[:, 4 * g:4 * g + 4], pbias[:, 4 * g:4 * g + 4], sc, None, ALU.mult))
            link(v.tensor_scalar(bhn[:], bhhc[:, 8:12], scl[:, 0:1], None, ALU.mult))
            dve.wait_ge(s("adj_out"), 16)
            dve.wait_ge(s("invdeg_out"), 16)
            i = 0
            for g in range(3):
                sc = scl[:, 1:2] if g == 1 else scl[:, 0:1]
                for j in range(KT):
                    for n0, n1 in NCH:
                        dve.wait_ge(s("pre_done"), i + 1)
                        q = (j // 2) * 6 + g * 2 + j % 2
                        to = pi_v[:, n0:n1, q]
                        link(v.tensor_scalar(to, psum[:, 4 + i % 4, 0:n1 - n0], sc, pbias[:, 4 * g + j:4 * g + j + 1], ALU.mult, ALU.add))
                        v.tensor_scalar(to, to, 2.0 ** 110, -2.0 ** 110, ALU.min, ALU.max).then_inc(s("pre_stored"), 1)
                        i += 1
            dve.wait_ge(s("pre_stored"), 36)
            link(v.memset(h16[:], 0.0))
            link(v.memset(hf[:], 0.0))
            link(v.memset(chain[:], 1.0))
            link(v.memset(rz[:], 0.0))
            link(v.memset(zmul[:], 0.0))
            ch = chain[:].rearrange("p (q c) -> p q c", c=4)
            link(v.memset(ch[:, :, 0], 0.0))
            link(v.memset(ch[:, 4:6, 3], 0.0))
            link(v.memset(psum[:, 0:4, 0:24], 0.0))
            for u in range(2):
                for c in range(2):
                    link(v.tensor_copy(psum[:, 2 * u + c, 18:24:4], bhn[:, 2 * c:2 * c + 2]))
            dve.sem_inc(s("gru_init"), 1)
            for c in range(2):
                dve.sem_inc(s(f"gru_state{c}"), 1)

            def gru_sums(t, u, c):
                dve.wait_ge(s(f"gru_mm{c}"), t + 1)
                v.tensor_tensor_scan(sums[:, c], chain[:], psum[:, 2 * u + c, 0:24], 0.0, ALU.mult, ALU.add).then_inc(s(f"gru_sums{c}"), 1)

            def gru_gates(t, u, c):
                dve.wait_ge(s(f"gru_rz{c}"), t + 1)
                v.tensor_tensor_scan(vn[:, c], rz[:, c, 0:8], sums[:, c, 16:24], 0.0, ALU.mult, ALU.add).then_inc(s(f"gru_n_in{c}"), 1)
                zc = rz[:, c, 11:16:4]
                v.tensor_scalar(zmul[:, c, 1:4:2], zc, HS, None, ALU.mult).then_inc(s(f"gru_z{c}"), 1)
                v.scalar_tensor_tensor(out=zadd[:, c, 1:4:2], in0=zc, scalar=-1.0, in1=hf[:, u, c, 1:4:2], op0=ALU.add, op1=ALU.mult).then_inc(s(f"gru_z{c}"), 1)

            def gru_update(t, u, c):
                dve.wait_ge(s(f"gru_z{c}"), 2 * t + 2)
                dve.wait_ge(s(f"gru_kept{c}"), t + 1)
                dve.wait_ge(s(f"gru_n{c}"), t + 1)
                v.tensor_tensor_scan(h16[:, 1 - u, c, 0], zmul[:, c], zadd[:, c], 0.0, ALU.mult, ALU.subtract).then_inc(s(f"gru_h{c}"), 1)
                v.tensor_tensor_scan(hf[:, 1 - u, c], zmul[:, c], zadd[:, c], 0.0, ALU.mult, ALU.subtract).then_inc(s(f"gru_h{c}"), 1)
                dve.wait_ge(s(f"gru_h{c}"), 2 * t + 2)
                v.tensor_tensor(h16[:, 1 - u, c, 1, 1:4:2], hf[:, 1 - u, c, 1:4:2], h16[:, 1 - u, c, 0, 1:4:2], ALU.subtract).then_inc(s(f"gru_state{c}"), 1)

            with dve.Fori(0, N // 2) as i:
                for u in range(2):
                    t = 2 * i + u
                    gru_sums(t, u, 0)
                    gru_gates(t, u, 0)
                    gru_sums(t, u, 1)
                    gru_update(t, u, 0)
                    gru_gates(t, u, 1)
                    gru_update(t, u, 1)
            for t in range(NT):
                dve.wait_ge(s("fc_done"), t + 1)
                v.scalar_tensor_tensor(out=xr[0:NP, t], in0=psum[0:NP, 4 + t % 4], scalar=1.0 / HS, in1=xr[0:NP, t], op0=ALU.mult, op1=ALU.add).then_inc(s("fc_stored"), 1)
                dve.wait_ge(s("fc_stored"), t + 1)
                ln_rows(t, "fc_ln")
            dve.wait_ge(s("l1b1_in"), 16)
            for t in range(NT):
                dve.wait_ge(s("l1h1_done"), t + 1)
                v.tensor_tensor(hn[0:NP, t], psum[0:NP, 4 + t % 4], l1_bias[0:NP], ALU.add).then_inc(s("l1h1_stored"), 1)
            dve.wait_ge(s("cnt_in"), 16)
            dve.wait_ge(s("invdeg_in"), 16)
            for t in range(NT):
                v.tensor_tensor(wt_v[0:NP, t], wt_v[0:NP, t], invdeg_row[0:NP], ALU.mult).then_inc(s("mean_ready"), 1)
            for f in range(KT):
                for c, (n0, n1) in enumerate(NCH):
                    dve.wait_ge(s("l1agg_stored"), 3 * f + c + 1)
                    link(v.bn_stats(stat[:, c], r1[:, f, n0:n1]))
                link(v.bn_aggr(mv[:, 0:2], stat[:].rearrange("p a b -> p (a b)")))
                roots[0] += 1
                v.tensor_scalar(mv[:, 2:3], mv[:, 1:2], 1e-5, None, ALU.add).then_inc(s("var"), 1)
                dve.wait_ge(s("root"), roots[0])
                link(v.tensor_tensor(bnc[:, 0, f:f + 1], mv[:, 2:3], gamc[:, f:f + 1], ALU.mult))
                link(v.tensor_tensor(mv[:, 3:4], mv[:, 0:1], bnc[:, 0, f:f + 1], ALU.mult))
                link(v.tensor_tensor(bnc[:, 1, f:f + 1], betc[:, f:f + 1], mv[:, 3:4], ALU.subtract))
                dve.sem_inc(s("bn_ready"), 1)
            dve.wait_ge(s("l1b2_in"), 16)
            for t in range(NT):
                dve.wait_ge(s("l1h2_done"), t + 1)
                v.tensor_tensor(hn[0:NP, t], psum[0:NP, 4 + t % 4], l1_bias[0:NP], ALU.add).then_inc(s("l1h2_stored"), 1)
            for t in range(NT):
                dve.wait_ge(s("l1out_done"), t + 1)
                v.tensor_tensor(xr[0:NP, t], psum[0:NP, t % 4], xr[0:NP, t], ALU.add).then_inc(s("l1out_stored"), 1)
                dve.wait_ge(s("l1out_stored"), t + 1)
                ln_rows(t, "l1out_ln")
            dve.wait_ge(s("logits"), 1)
            link(v.tensor_tensor(gates[0:NP], psum[0:NP, 0, 0:NT * NE].rearrange("p (t e) -> p t e", e=NE), gate_b[0:NP].unsqueeze(1).broadcast_to([NP, NT, NE]), ALU.add))
            dve.sem_inc(s("gates_read"), 1)
            link(v.tensor_reduce(gtmp[0:NP, 0], gates[0:NP], AX.X, ALU.max))
            link(v.tensor_tensor(gates[0:NP], gates[0:NP], gtmp[0:NP, 0].unsqueeze(2).broadcast_to([NP, NT, NE]), ALU.subtract))
            dve.sem_inc(s("gate_in"), 1)
            dve.wait_ge(s("gate_exp"), 1)
            link(v.tensor_reduce(gtmp[0:NP, 0], gates[0:NP], AX.X, ALU.add))
            link(v.reciprocal(gtmp[0:NP, 0], gtmp[0:NP, 0]))
            link(v.tensor_tensor(gates[0:NP], gates[0:NP], gtmp[0:NP, 0].unsqueeze(2).broadcast_to([NP, NT, NE]), ALU.mult))
            for a in range(NE):
                n_beat = gtmp[0:NP, 1]
                link(v.memset(n_beat, 0.0))
                for b in range(NE):
                    if b != a:
                        link(v.tensor_tensor(gtmp[0:NP, 2], gates[0:NP, :, b], gates[0:NP, :, a], ALU.is_ge if b < a else ALU.is_gt))
                        link(v.tensor_tensor(n_beat, n_beat, gtmp[0:NP, 2], ALU.add))
                link(v.scalar_tensor_tensor(out=gsel[0:NP, a], in0=n_beat, scalar=2.0, in1=gates[0:NP, :, a], op0=ALU.is_lt, op1=ALU.mult))
            dve.wait_ge(s("aggx_done"), 12)
            with dve.Fori(0, NE // 2) as ei:
                for u in range(2):
                    e = 2 * ei + u
                    b0 = 0 if u == 0 else 4
                    dve.wait_ge(s("eb_in"), e * 16 + 16)
                    for t in range(NT):
                        tmp = l2_tmp[t % 2]
                        dve.wait_ge(s("eout_done"), e * NT + t + 1)
                        v.tensor_tensor(tmp, psum[0:NP, b0 + t % 4], l2_bias[0:NP], ALU.add).then_inc(s("eout_stored"), 1)
                        dve.wait_ge(s("eout_stored"), e * NT + t + 1)
                        v.tensor_scalar(tmp, tmp, 0.0, gsel[0:NP, bass.ds(e, 1), t:t + 1].rearrange("p a t -> p (a t)"), ALU.max, ALU.mult).then_inc(s("eweighted"), 1)
                        dve.wait_ge(s("eweighted"), e * NT + t + 1)
                        v.tensor_tensor(xr[0:NP, t], xr[0:NP, t], tmp, ALU.add).then_inc(s("eadd"), 1)
            dve.wait_ge(s("eadd"), NE * NT)
            for t in range(NT):
                ln_rows(t, "l2_ln")
            dve.wait_ge(s("l2_ln"), NT)
            for t in range(NT):
                dve.wait_ge(s("l3_done"), t + 1)
                v.scalar_tensor_tensor(out=xr[0:NP, t], in0=psum[0:NP, t % 4], scalar=0.0, in1=xr[0:NP, t], op0=ALU.max, op1=ALU.add).then_inc(s("l3_stored"), 1)
                dve.wait_ge(s("l3_stored"), t + 1)
                ln_rows(t, "final_ln")


def kernel(**inputs):
    import numpy as np
    import concourse.bacc as bacc
    from concourse.bass_utils import run_bass_kernel_spmd

    a = {k: np.asarray(x) for k, x in inputs.items()}

    def cols(x):
        return x.reshape(-1, P).T

    arrays = {
        "x": a["x"], "xT": a["x"].T, "src": a["src"], "dst": a["dst"], "edge_weight": a["edge_weight"],
        "W1": a["L0_gnn_W1"], "W2": a["L0_gnn_W2"], "W_ihT": a["L0_gnn_W_ih"].T, "W_hhT": a["L0_gnn_W_hh"].T,
        "W_fc": a["L0_gnn_W_fc"], "b_fc": a["L0_gnn_b_fc"],
        "l1_W1": a["L1_gnn_W1"], "l1_b1": a["L1_gnn_b1"], "l1_W2": a["L1_gnn_W2"], "l1_b2": a["L1_gnn_b2"],
        "gate_W": a["L2_gnn_gate_W"], "gate_b": a["L2_gnn_gate_b"],
        "Wl0": a["L2_gnn_Wl"][:, 0], "Wl1": a["L2_gnn_Wl"][:, 1], "Wr0": a["L2_gnn_Wr"][:, 0], "Wr1": a["L2_gnn_Wr"][:, 1],
        "bl1": a["L2_gnn_bl"][:, 1], "l3_W": a["L3_gnn_W"],
        "bcol": np.concatenate([cols(a[n]) for n in ("L0_gnn_b1", "L0_gnn_b2", "L0_gnn_b_ih", "L0_gnn_b_hh", "L1_gnn_gamma", "L1_gnn_beta")]
                               + [cols(a["L2_gnn_bl"][:, 0])], axis=1),
    }
    arrays = {f"in_{k}": np.ascontiguousarray(x) for k, x in arrays.items()}
    nc = bacc.Bacc("TRN2", target_bir_lowering=False, num_devices=1)
    io = {k[3:]: nc.dram_tensor(k, x.shape, mybir.dt.from_np(x.dtype), kind="ExternalInput").ap() for k, x in arrays.items()}
    io["out"] = nc.dram_tensor("out", (N, D), F32, kind="ExternalOutput").ap()
    layout(nc, io)
    r = run_bass_kernel_spmd(nc, [arrays], core_ids=[0])
    return r.results[0]["out"]
```

```python
from contextlib import ExitStack

import concourse.bass as bass
from concourse import mybir

ACT = mybir.ActivationFunctionType
ALU = mybir.AluOpType
AX = mybir.AxisListType
F32 = mybir.dt.float32
F16 = mybir.dt.float16
BF16 = mybir.dt.bfloat16
I32 = mybir.dt.int32

N, D, E = 1250, 512, 20000
P = 128
NP, NT = 125, 10
KT = D // P
EP, ET = 125, 160
EH = ET // 2
WD = 25
NW = N // WD
NCH = [(0, 417), (417, 834), (834, 1250)]
NE = 4
LN_EPS = 1e-5
HS = 4096.0
ROUND = 1.5 * 2.0 ** 24
WSLOT = KT * D


def layout(nc, io):
    ctx = ExitStack()
    with ctx:
        def sb(name, shape, dt=F32):
            return ctx.enter_context(nc.sbuf_tensor(name, shape, dt))

        def sem(name):
            return ctx.enter_context(nc.semaphore(name))


        adj = sb("adj", [P, NT * N])
        big = sb("big", [P, (N + 1) * 12])
        xr = sb("xr", [P, NT, D])
        r1 = sb("r1", [P, KT, N])
        r2 = sb("r2", [P, KT, N])
        hn = sb("hn", [P, NT, D])
        ws = sb("ws", [P, 2 * WSLOT])
        psum = ctx.enter_context(nc.psum_tensor("psum", [P, 8, 512], F32))

        adj_v = adj[:].rearrange("p (t n) -> p t n", n=N)
        wt_v = big[:, 0:NT * N].rearrange("p (t n) -> p t n", n=N)
        pi_v = big[:].rearrange("p (t q) -> p t q", q=12)
        tail = NT * N
        inv_row = big[:, tail:tail + N]
        invdeg_row = big[:, tail + N:tail + 2 * N]
        l1_bias = big[:, tail:tail + D]
        hn_f = hn[:].rearrange("p t d -> p (t d)")
        r2_f = r2[:].rearrange("p k n -> p (k n)")
        fc_bias = r2_f[:, 4400:4400 + D]

        def weight(ap):
            return ap.rearrange("p (k n) -> p k n", k=KT)

        def wslot(i):
            return weight(ws[:, i * WSLOT:(i + 1) * WSLOT])

        w_fc = weight(hn_f[:, 0:WSLOT])
        whh = [r2_f[:, 0:WSLOT], r2_f[:, WSLOT:2 * WSLOT], hn_f[:, WSLOT:2 * WSLOT]]
        whh16 = [a.bitcast(F16).rearrange("p (a k n) -> p a k n", a=2, k=KT) for a in whh]
        l2w = [weight(adj[:, i * WSLOT:(i + 1) * WSLOT]) for i in range(4)]
        at = 4 * WSLOT
        agg_x = [big[:, tail:tail + N], big[:, tail + N:tail + 2 * N], adj[:, at:at + N], adj[:, at + N:at + 2 * N]]
        l2_bias = adj[:, at + 2 * N:at + 2 * N + D]
        at += 2 * N + D
        l2_tmp = [adj[0:NP, at + i * D:at + (i + 1) * D] for i in range(2)]

        iota16 = r2_f[:, 0:625].bitcast(F16)
        src_hot = r2_f[:, 625:625 * 3].bitcast(BF16).rearrange("p (h n) -> p h n", h=2)
        dst_hot = r2_f[:, 3125:3225].bitcast(BF16).rearrange("p (h n) -> p h n", h=2)
        zero_b = r2_f[:, 3400:3400 + 250].bitcast(BF16)
        e_stage = hn_f[:, 0:750].rearrange("p (a h e) -> p a h e", a=3, h=2)
        e_int = hn_f[:, 750:1250].bitcast(I32).rearrange("p (a h e) -> p a h e", a=2, h=2)
        e_col = hn_f[:, 1250:1250 + 3 * ET].rearrange("p (a t) -> p a t", a=3)
        e_src, e_dst, e_w = e_col[:, 0], e_col[:, 1], e_col[:, 2]
        w_part = hn_f[:, 1730:2370].rearrange("p (t a) -> p t a", a=4)
        w_bf = hn_f[:, 2370:2450].bitcast(BF16)
        w_res = hn_f[:, 2610:2610 + 2 * ET].rearrange("p (a t) -> p a t", a=2)
        p_lim = hn_f[0:EH, 2930:2932]
        w_lim = hn_f[:, 2934:2936]
        pair_no = hn_f[:, 2936:2936 + 2 * EH].rearrange("p (a t) -> p a t", a=2)
        hit = hn_f[:, 3256:3256 + EH]
        hit_b = hn_f[:, 3416:3416 + EH]
        span = hn_f[:, 3576:3578]
        row = hn_f[0:1, 3578:3578 + 6 * NW].rearrange("p (a w) -> p a w", a=6)
        cparts = [a.rearrange("p (t c) -> p t c", t=NT) for a in (hn_f[:, 3880:4630], r2_f[:, 3650:4400])]

        ident = sb("ident", [P, P])
        ones = sb("ones", [P, P])
        bounds = sb("bounds", [1, 4, NW], I32)
        inv_col = sb("inv_col", [P, NT])
        bcol = sb("bcol_sb", [P, 56])
        b1c, b2c, bihc, bhhc = bcol[:, 0:4], bcol[:, 4:8], bcol[:, 8:20], bcol[:, 20:32]
        gamc, betc, blc = bcol[:, 32:36], bcol[:, 36:40], bcol[:, 40:56]
        gate_w = sb("gate_w", [P, KT, NE])
        gate_b = sb("gate_b_sb", [P, NE])
        gates = sb("gates", [P, NT, NE])
        gsel = sb("gsel", [P, NE, NT])
        gtmp = sb("gtmp", [P, 3, NT])
        stat = sb("stat", [P, 3, 6])
        mv = sb("mv", [P, 4])
        bnc = sb("bnc", [P, 2, KT])
        wmax = sb("wmax", [P, 12])
        scl = sb("scl", [P, 2])
        scw = sb("scw", [P, 2])
        pbias = sb("pbias", [P, 12])
        h16 = sb("h16", [P, 2, 2, 2, 2], F16)
        mul_rz = sb("mul_rz", [P, 6])
        mul_n = sb("mul_n", [P, 2, 8])
        sum_rz = sb("sum_rz", [P, 2, 2, 6])
        sum_n = sb("sum_n", [P, 2, 8])
        upd_mul = sb("upd_mul", [P, 2, 14])
        upd_add = sb("upd_add", [P, 2, 14])
        upd = sb("upd", [P, 2, 2, 14])
        signs = sb("signs", [P, 4])
        minus_half = sb("minus_half", [P, 1])
        ebias = sb("ebias", [P, KT])
        warm = sb("warm", [P, 1])

        d_cnt = nc.dram_tensor("edge_counts", [NT, NP, N], F32, kind="Internal").ap()
        d_wt = nc.dram_tensor("edge_weights", [NT, NP, N], F32, kind="Internal").ap()
        d_adj = nc.dram_tensor("adj_rows", [NT, NP, N], F32, kind="Internal").ap()
        d_invdeg = nc.dram_tensor("invdeg", [NP, N], F32, kind="Internal").ap()

        sems = {}

        def s(name):
            if name not in sems:
                sems[name] = sem(name)
            return sems[name]

        block = ctx.enter_context(nc.Block())

        def w_rows(dst_ap, src):
            return dst_ap, src.rearrange("(k p) n -> p k n", p=P)

        def tiles(ap):
            return ap.rearrange("t p n -> p t n")

        @block.sync
        def _(sp):
            for a, name in enumerate(("src", "dst")):
                sp.dma_start(e_int[0:EH, a], io[name].rearrange("(q h e) -> q h e", h=2, e=EP)).then_inc(s("edges_in"), 16)
            sp.dma_start(e_stage[0:EH, 2], io["edge_weight"].rearrange("(q h e) -> q h e", h=2, e=EP)).then_inc(s("edges_in"), 16)
            sp.dma_start(r1[:], io["xT"].rearrange("(k p) n -> p k n", p=P)).then_inc(s("xcols_in"), 16)
            sp.dma_start(*w_rows(wslot(0), io["W1"])).then_inc(s("w1_in"), 16)
            sp.dma_start(*w_rows(wslot(1), io["W2"])).then_inc(s("w2_in"), 16)
            sp.dma_start(bcol[:], io["bcol"]).then_inc(s("small_in"), 16)
            sp.dma_start(gate_w[:], io["gate_W"].rearrange("(k p) e -> p k e", p=P)).then_inc(s("small_in"), 16)
            sp.dma_start(gate_b[:], io["gate_b"].partition_broadcast(P)).then_inc(s("small_in"), 16)
            sp.dma_start(xr[0:NP], io["x"].rearrange("(t p) d -> p t d", p=NP)).then_inc(s("x_in"), 16)
            sp.dma_start(fc_bias, io["b_fc"].partition_broadcast(P)).then_inc(s("bfc_in"), 16)
            sp.wait_ge(s("win_counts"), NW)
            for h in range(2):
                half = slice(5 * h, 5 * h + 5)
                sp.dma_start(tiles(d_cnt[half]), adj_v[0:NP, half]).then_inc(s(f"cnt_out{h}"), 16)
            sp.wait_ge(s("win_weights"), NW + 2)
            sp.dma_start(tiles(d_wt), wt_v[0:NP]).then_inc(s("wt_out"), 16)
            sp.wait_ge(s("invdeg_ready"), 1)
            sp.dma_start(d_invdeg, invdeg_row[0:NP]).then_inc(s("invdeg_out"), 16)
            sp.wait_ge(s("tr_stored"), 3 * NT)
            sp.dma_start(tiles(d_adj), wt_v[0:NP]).then_inc(s("adj_out"), 16)
            sp.wait_ge(s("h2_done"), NT)
            for g, place in enumerate((weight(whh[0]), weight(whh[1]), wslot(1))):
                sp.dma_start(*w_rows(place, io["W_hhT"][:, g * D:(g + 1) * D])).then_inc(s("whh_in"), 16)
            sp.wait_ge(s("whh_split"), 2)
            sp.dma_start(*w_rows(wslot(0), io["W_ihT"][:, 0:D])).then_inc(s("wih_in0"), 16)
            sp.wait_ge(s("whh_split"), 3)
            sp.dma_start(*w_rows(wslot(1), io["W_ihT"][:, D:2 * D])).then_inc(s("wih_in1"), 16)
            sp.wait_ge(s("conv2_done"), 12)
            sp.dma_start(*w_rows(w_fc, io["W_fc"])).then_inc(s("wfc_in"), 16)
            sp.wait_ge(s("adj_out"), 16)
            sp.dma_start(adj_v[0:NP], tiles(d_adj)).then_inc(s("adj_in"), 16)
            sp.wait_ge(s("pre_done"), 12)
            sp.dma_start(*w_rows(wslot(0), io["W_ihT"][:, 2 * D:3 * D])).then_inc(s("wih_in2"), 16)
            sp.wait_ge(s("pre_done"), 36)
            sp.dma_start(*w_rows(wslot(0), io["l1_W1"])).then_inc(s("l1w1_in"), 16)
            sp.dma_start(*w_rows(wslot(1), io["l1_W2"])).then_inc(s("l1w2_in"), 16)
            for c in range(2):
                sp.wait_ge(s(f"gru_put{c}"), N + 1)
            sp.dma_start(l1_bias, io["l1_b1"].partition_broadcast(P)).then_inc(s("l1b1_in"), 16)
            sp.dma_start(invdeg_row[0:NP], d_invdeg).then_inc(s("invdeg_in"), 16)
            sp.wait_ge(s("cnt_out0"), 16)
            sp.wait_ge(s("cnt_out1"), 16)
            sp.dma_start(wt_v[0:NP], tiles(d_cnt)).then_inc(s("cnt_in"), 16)
            sp.wait_ge(s("l1h1_stored"), NT)
            sp.dma_start(l1_bias, io["l1_b2"].partition_broadcast(P)).then_inc(s("l1b2_in"), 16)
            sp.wait_ge(s("l1out_done"), NT)
            with sp.Fori(0, NE) as e:
                sp.wait_ge(s("layer1_done"), e * 12)
                for m, name in enumerate(("Wl0", "Wr0")):
                    sp.dma_start(l2w[m], io[name][bass.ds(e, 1)].rearrange("e (k p) n -> p (e k) n", p=P)).then_inc(s("ew0_in"), 16)
                sp.wait_ge(s("eout_stored"), e * NT)
                sp.dma_start(l2_bias, io["bl1"][bass.ds(e, 1)].rearrange("e d -> (e d)").partition_broadcast(P)).then_inc(s("eb_in"), 16)
                for m, name in enumerate(("Wl1", "Wr1")):
                    sp.dma_start(l2w[2 + m], io[name][bass.ds(e, 1)].rearrange("e (k p) n -> p (e k) n", p=P)).then_inc(s("ew1_in"), 16)
            sp.dma_start(*w_rows(wslot(0), io["l3_W"])).then_inc(s("l3w_in"), 16)
            sp.wait_ge(s("eadd"), NE * NT)
            sp.wait_ge(s("wt_out"), 16)
            sp.dma_start(adj_v[0:NP], tiles(d_wt)).then_inc(s("wt_in"), 16)
            for t in range(NT):
                sp.wait_ge(s("final_ln"), t + 1)
                sp.dma_start(io["out"][t * NP:(t + 1) * NP], xr[0:NP, t]).then_inc(s("out_stored"), 16)
            sp.wait_ge(s("out_stored"), 16 * NT)

        @block.gpsimd
        def _(pool):
            pool.memset(ident[:], 0.0).then_inc(s("ident0"), 1)
            pool.memset(ones[:], 1.0).then_inc(s("const"), 1)
            pool.memset(zero_b, 0.0).then_inc(s("const"), 1)
            pool.memset(minus_half[:], -0.5).then_inc(s("const"), 1)
            pool.memset(big[:, N * 12:], 0.0).then_inc(s("const"), 1)
            pool.wait_ge(s("ident0"), 1)
            pool.affine_select(out=ident[:], in_=ident[:], compare_op=ALU.not_equal, fill=1.0, base=0,
                               pattern=[[-1, P]], channel_multiplier=1).then_inc(s("const"), 1)
            small = dict(allow_small_or_imprecise_dtypes=True)
            pool.iota(iota16, [[1, N]], base=0, channel_multiplier=0, **small).then_inc(s("const"), 1)
            pool.iota(pair_no[:, 0], [[1, EH]], base=1, channel_multiplier=0, **small).then_inc(s("const"), 1)
            pool.iota(pair_no[:, 1], [[-1, EH]], base=EH, channel_multiplier=0, **small).then_inc(s("const"), 1)
            pool.iota(w_lim, [[WD, 2]], base=0, channel_multiplier=WD, **small).then_inc(s("const"), 1)
            pool.sem_inc(s("win_weights"), 2)
            with pool.Fori(0, NW // 2) as i:
                for u in range(2):
                    w = 2 * i + u
                    c = cparts[u][0:NP]
                    pool.wait_ge(s("parts_ready"), w + 1)
                    pool.tensor_tensor(c[:, :, 0:WD], c[:, :, 0:WD], c[:, :, WD:2 * WD], ALU.add).then_inc(s("parts_half"), 1)
                    pool.wait_ge(s("parts_half"), w + 1)
                    pool.tensor_tensor(c[:, :, 0:WD], c[:, :, 0:WD], c[:, :, 2 * WD:3 * WD], ALU.add).then_inc(s("parts_sum"), 1)
                    pool.wait_ge(s("parts_sum"), w + 1)
                    pool.tensor_copy(wt_v[0:NP, :, bass.ds(w * WD, WD)], c[:, :, 0:WD]).then_inc(s("win_weights"), 1)
            pool.wait_ge(s("deg1_col"), 1)
            pool.tensor_tensor(inv_col[0:NP], inv_col[0:NP], minus_half[0:NP, 0:1].to_broadcast([NP, NT]), ALU.pow).then_inc(s("inv_col_ready"), 1)
            pool.wait_ge(s("wmax_part"), 1)
            pool.partition_all_reduce(wmax[:, 7:8], wmax[:, 6:7], P, bass.bass_isa.ReduceOp.max).then_inc(s("wmax_all"), 1)
            for c in range(2):
                pool.sem_inc(s(f"gru_kept{c}"), 2)
            with pool.Fori(0, N // 2) as i:
                for u in range(2):
                    t = 2 * i + u
                    for c in range(2):
                        pool.wait_ge(s(f"gru_upd{c}"), t + 1)
                        pool.tensor_copy(r1[:, 2 * c:2 * c + 2, bass.ds(t, 1)], upd[:, 1 - u, c, 2:14:7]).then_inc(s(f"gru_kept{c}"), 1)
            for n in range(4 * NT + KT):
                p = slice(0, P) if NT <= n < NT + KT else slice(0, NP)
                pool.wait_ge(s("var"), n + 1)
                pool.tensor_tensor(mv[p, 2:3], mv[p, 2:3], minus_half[p, 0:1], ALU.pow).then_inc(s("root"), 1)

        @block.tensor
        def _(pe):
            mm = nc.tensor.matmul

            def out_rows(i, bank0, done, stored, base=0):
                if i >= 4:
                    pe.wait_ge(s(stored), base + i - 3)
                return psum[:, bank0 + i % 4]

            def rows_product(name, bank0, cols, w, base=0, before=None):
                for t in range(NT):
                    if before:
                        before(t)
                    o = out_rows(t, bank0, None, f"{name}_stored", base)
                    for k in range(KT):
                        m = mm(o[0:NP], cols[:, k, t * NP:(t + 1) * NP], w[:, k], start=(k == 0), stop=(k == KT - 1))
                    m.then_inc(s(f"{name}_done"), 1)

            def agg_cols(name, bank0, rows, mat):
                i = 0
                for f in range(KT):
                    for n0, n1 in NCH:
                        o = out_rows(i, bank0, None, f"{name}_stored")
                        for t in range(NT):
                            m = mm(o[:, 0:n1 - n0], rows[0:NP, t, f * P:(f + 1) * P], mat[0:NP, t, n0:n1],
                                   start=(t == 0), stop=(t == NT - 1))
                        m.then_inc(s(f"{name}_done"), 1)
                        i += 1

            def turn(name, t, bank0):
                pe.wait_ge(s(f"{name}_ln"), t + 1)
                if t >= 4:
                    pe.wait_ge(s(f"{name}_turned"), t - 3)
                for k in range(KT):
                    m = nc.tensor.transpose(psum[:, bank0 + t % 4, k * NP:(k + 1) * NP], xr[0:NP, t, k * P:(k + 1) * P], ident[0:NP, 0:NP])
                m.then_inc(s(f"{name}_turn"), 1)

            pe.wait_ge(s("const"), 9)
            pe.wait_ge(s("edges_f"), 1)
            for a in range(3):
                for h in range(2):
                    m = nc.tensor.transpose(psum[0:EP, a, h * EH:(h + 1) * EH], e_stage[0:EH, a, h], ident[0:EH, 0:EH])
            m.then_inc(s("edges_turn"), 1)
            pe.wait_ge(s("limits"), 1)
            for a in range(2):
                m = mm(psum[0:NW, 3, a * EH:(a + 1) * EH], p_lim[:, a:a + 1].to_broadcast([EH, NW]), ident[0:EH, 0:EH],
                       start=True, stop=True, skip_group_check=True)
            m.then_inc(s("limits_all"), 1)
            pe.wait_ge(s("span"), 1)
            for a in range(2):
                m = mm(psum[0:1, 4, a * NW:(a + 1) * NW], span[0:NW, a:a + 1], ident[0:NW, 0:NW], start=True, stop=True, skip_group_check=True)
            m.then_inc(s("span_row"), 1)
            pe.wait_ge(s("bounds"), 1)
            with pe.Fori(0, NW // 2) as i:
                for u in range(2):
                    w = 2 * i + u
                    blocks = pe.value_load(bounds[0:1, 1, bass.ds(w, 1)], min_val=1, max_val=EH)
                    before = pe.value_load(bounds[0:1, 2, bass.ds(w, 1)], min_val=0, max_val=EH * (NW + 1))
                    pe.wait_ge(s("win_read"), w + 1)
                    for b in range(2):
                        mm(psum[0:NP, 2 * u + b, 0:1], zero_b[0:NP, 0:NP], zero_b[0:NP, 0:1], start=True, stop=False, skip_group_check=True)
                    with pe.Fori(0, blocks) as j:
                        g = before + j
                        for h in range(2):
                            pe.wait_ge(s(f"hot_ready{h}"), g + 1)
                            for t in range(NT):
                                m = mm(psum[0:NP, 2 * u + t // 5, (t % 5) * 100:(t % 5) * 100 + 100],
                                       src_hot[0:EP, h, t * NP:(t + 1) * NP], dst_hot[0:EP, h], start=False, stop=False, skip_group_check=True)
                            m.then_inc(s(f"hot_used{h}"), 1)
                    for b in range(2):
                        m = mm(psum[0:NP, 2 * u + b, 0:1], zero_b[0:NP, 0:NP], zero_b[0:NP, 0:1], start=False, stop=True, skip_group_check=True)
                    m.then_inc(s("win_done"), 1)
            pe.wait_ge(s("win_counts"), NW)
            for c, (n0, n1) in enumerate(NCH):
                for t in range(NT):
                    m = mm(psum[:, 4 + c, 0:n1 - n0], ones[0:NP], adj_v[0:NP, t, n0:n1], start=(t == 0), stop=(t == NT - 1))
                m.then_inc(s("deg"), 1)
            pe.wait_ge(s("xcols_in"), 16)
            pe.wait_ge(s("w1_in"), 16)
            pe.wait_ge(s("win_read"), NW + 2)
            pe.wait_ge(s("deg1"), 3)
            for t in range(NT):
                m = mm(psum[0:NP, 7, t:t + 1], inv_row[0:1, t * NP:(t + 1) * NP], ones[0:1, 0:1], start=True, stop=True, skip_group_check=True)
            m.then_inc(s("deg1_turn"), 1)

            def inv_everywhere(h1_tile):
                if h1_tile == 2:
                    pe.wait_ge(s("inv_col_ready"), 1)
                    for t in range(NT):
                        m = mm(psum[:, 4 + t // 4, (t % 4) * NP:(t % 4 + 1) * NP], inv_col[0:NP, t:t + 1].to_broadcast([NP, P]), ident[0:NP, 0:NP],
                               start=True, stop=True, skip_group_check=True)
                    m.then_inc(s("inv_rows"), 1)

            rows_product("h1", 0, r1, wslot(0), before=inv_everywhere)
            pe.wait_ge(s("h1_stored"), NT)
            pe.wait_ge(s("norm"), NT)
            agg_cols("conv1", 4, hn, adj_v)
            for d in range(NT):
                for q in range(3):
                    n = 3 * d + q
                    if n >= 4:
                        pe.wait_ge(s("tr_stored"), n - 3)
                    for t in range(4 * q, min(4 * q + 4, NT)):
                        m = nc.tensor.transpose(psum[0:NP, n % 4, (t - 4 * q) * NP:(t - 4 * q + 1) * NP], adj_v[0:NP, t, d * NP:(d + 1) * NP], ident[0:NP, 0:NP])
                    m.then_inc(s("tr_done"), 1)
            pe.wait_ge(s("conv1_stored"), 12)
            pe.wait_ge(s("w2_in"), 16)
            rows_product("h2", 4, r2, wslot(1))
            pe.wait_ge(s("h2_stored"), NT)
            pe.wait_ge(s("tr_stored"), 3 * NT)
            agg_cols("conv2", 0, hn, adj_v)
            pe.wait_ge(s("conv2_stored"), 12)
            i = 0
            for g in range(3):
                pe.wait_ge(s(f"wih_in{g}"), 16)
                for j in range(KT):
                    for n0, n1 in NCH:
                        o = out_rows(i, 4, None, "pre_stored")
                        for k in range(KT):
                            m = mm(o[:, 0:n1 - n0], wslot(g % 2)[:, k, j * P:(j + 1) * P], r1[:, k, n0:n1], start=(k == 0), stop=(k == KT - 1))
                        m.then_inc(s("pre_done"), 1)
                        i += 1
            pe.wait_ge(s("gru_init"), 1)
            pe.wait_ge(s("whh_split"), 3)

            every = ((0, 0), (0, 1), (1, 0), (1, 1))

            def gru_gate(u, c, kc, g, pieces=every):
                for j, k in pieces:
                    at = (4 if g == 2 else 3) * j
                    for part in range(2):
                        m = mm(psum[:, 4 * c + g, at:at + 2], whh16[g][:, part, 2 * kc + k, (2 * c + j) * P:(2 * c + j + 1) * P],
                               h16[:, u, kc, k], start=(kc == 0 and j == 0 and k == 0 and part == 0),
                               stop=(kc == 1 and k == 1 and part == 1), skip_group_check=True)
                return m

            with pe.Fori(0, N // 2) as i:
                for u in range(2):
                    t = 2 * i + u
                    pe.wait_ge(s("gru_state0"), t + 1)
                    pe.wait_ge(s("gru_put0"), t + 1)
                    for g in (0, 2, 1):
                        gru_gate(u, 0, 0, g)
                    pe.wait_ge(s("gru_put1"), t + 1)
                    gru_gate(u, 1, 0, 0)
                    gru_gate(u, 1, 0, 2, every[:1])
                    pe.wait_ge(s("gru_state1"), t + 1)
                    gru_gate(u, 0, 1, 0).then_inc(s("gru_r_mm0"), 1)
                    gru_gate(u, 0, 1, 2).then_inc(s("gru_n_mm0"), 1)
                    gru_gate(u, 0, 1, 1).then_inc(s("gru_z_mm0"), 1)
                    gru_gate(u, 1, 1, 0).then_inc(s("gru_r_mm1"), 1)
                    gru_gate(u, 1, 0, 2, every[1:])
                    gru_gate(u, 1, 1, 2).then_inc(s("gru_n_mm1"), 1)
                    gru_gate(u, 1, 0, 1)
                    gru_gate(u, 1, 1, 1).then_inc(s("gru_z_mm1"), 1)
            for c in range(2):
                pe.wait_ge(s(f"gru_kept{c}"), N + 2)
                pe.wait_ge(s(f"gru_put{c}"), N + 1)
            pe.wait_ge(s("wfc_in"), 16)
            rows_product("fc", 4, r1, w_fc, before=lambda t: turn("fc", t - 3, 0) if t >= 3 else None)
            for t in range(NT - 3, NT):
                turn("fc", t, 0)
            pe.wait_ge(s("fc_turned"), NT)
            pe.wait_ge(s("l1w1_in"), 16)
            rows_product("l1h1", 4, r2, wslot(0))
            pe.wait_ge(s("l1h1_stored"), NT)
            pe.wait_ge(s("adj_in"), 16)
            agg_cols("l1agg", 0, hn, adj_v)
            pe.wait_ge(s("l1norm"), KT)
            pe.wait_ge(s("l1w2_in"), 16)
            rows_product("l1h2", 4, r1, wslot(1))
            pe.wait_ge(s("l1h2_stored"), NT)
            for d in range(NT):
                if d >= 3:
                    turn("l1out", d - 3, 4)
                o = out_rows(d, 0, None, "l1out_stored")
                for t in range(NT):
                    m = mm(o[0:NP], adj_v[0:NP, t, d * NP:(d + 1) * NP], hn[0:NP, t], start=(t == 0), stop=(t == NT - 1))
                m.then_inc(s("l1out_done"), 1)
            for t in range(NT - 3, NT):
                turn("l1out", t, 4)
            pe.wait_ge(s("l1out_turned"), NT)
            for t in range(NT):
                for k in range(KT):
                    m = mm(psum[0:NP, 0, t * NE:(t + 1) * NE], r2[:, k, t * NP:(t + 1) * NP], gate_w[:, k], start=(k == 0), stop=(k == KT - 1), skip_group_check=True)
            m.then_inc(s("logits"), 1)
            pe.wait_ge(s("mean_ready"), NT)
            agg_cols("aggx", 4, xr, wt_v)
            pe.wait_ge(s("aggx_stored"), 12)
            pe.wait_ge(s("gates_read"), 1)
            with pe.Fori(0, NE // 2) as ei:
                for u in range(2):
                    e = 2 * ei + u
                    b0, b1 = (0, 4) if u == 0 else (4, 0)
                    pe.wait_ge(s("ew0_in"), e * 32 + 32)
                    i = 0
                    for f in range(KT):
                        for n0, n1 in NCH:
                            o = out_rows(i, b0, None, "layer1_stored", e * 12)
                            for k in range(KT):
                                mm(o[:, 0:n1 - n0], l2w[0][:, k, f * P:(f + 1) * P], agg_x[k][:, n0:n1], start=(k == 0), stop=False)
                                m = mm(o[:, 0:n1 - n0], l2w[1][:, k, f * P:(f + 1) * P], r2[:, k, n0:n1], start=False, stop=(k == KT - 1))
                            m.then_inc(s("layer1_done"), 1)
                            i += 1
                    pe.wait_ge(s("layer1_stored"), e * 12 + 12)
                    pe.wait_ge(s("ew1_in"), e * 32 + 32)
                    pe.wait_ge(s("eout_stored"), e * NT)
                    rows_product("u", b1, r1, l2w[2], base=e * NT)
                    pe.wait_ge(s("u_stored"), e * NT + NT)
                    for d in range(NT):
                        o = out_rows(d, b0, None, "eout_stored", e * NT)
                        for k in range(KT):
                            mm(o[0:NP], r1[:, k, d * NP:(d + 1) * NP], l2w[3][:, k], start=(k == 0), stop=False)
                        for t in range(NT):
                            m = mm(o[0:NP], wt_v[0:NP, t, d * NP:(d + 1) * NP], hn[0:NP, t], start=False, stop=(t == NT - 1))
                        m.then_inc(s("eout_done"), 1)
            for t in range(NT):
                turn("l2", t, 0)
            pe.wait_ge(s("l2_turned"), NT)
            pe.wait_ge(s("l3w_in"), 16)
            rows_product("z", 4, r2, wslot(0))
            pe.wait_ge(s("z_stored"), NT)
            pe.wait_ge(s("wt_in"), 16)
            for d in range(NT):
                o = out_rows(d, 0, None, "l3_stored")
                for t in range(NT):
                    m = mm(o[0:NP], adj_v[0:NP, t, d * NP:(d + 1) * NP], hn[0:NP, t], start=(t == 0), stop=(t == NT - 1))
                m.then_inc(s("l3_done"), 1)

        @block.scalar
        def _(act):
            def take_cols(name, bank0, dst, func, bias=None, base=0, bias_at=None):
                i = 0
                for f in range(KT):
                    for n0, n1 in NCH:
                        act.wait_ge(s(f"{name}_done"), base + i + 1)
                        o = psum[:, bank0 + i % 4, 0:n1 - n0]
                        to = dst[f][:, n0:n1] if isinstance(dst, list) else dst[:, f, n0:n1]
                        if func is None:
                            m = nc.scalar.copy(to, o)
                        else:
                            m = nc.scalar.activation(to, o, func, bias=bias[:, f:f + 1])
                        m.then_inc(s(f"{name}_stored"), 1)
                        i += 1

            def take_rows(name, bank0, base=0):
                for t in range(NT):
                    act.wait_ge(s(f"{name}_done"), base + t + 1)
                    nc.scalar.copy(hn[0:NP, t], psum[0:NP, bank0 + t % 4]).then_inc(s(f"{name}_stored"), 1)

            def take_turned(name, bank0):
                for t in range(NT):
                    act.wait_ge(s(f"{name}_turn"), t + 1)
                    nc.scalar.copy(r2[:, :, t * NP:(t + 1) * NP], psum[:, bank0 + t % 4, 0:4 * NP].rearrange("p (k n) -> p k n", k=KT)).then_inc(s(f"{name}_turned"), 1)

            act.wait_ge(s("const"), 9)
            nc.scalar.copy(warm[:], ident[:, 0:1]).then_inc(s("warm"), 1)
            act.sem_inc(s("win_read"), 2)
            with act.Fori(0, NW // 2) as i:
                for u in range(2):
                    w = 2 * i + u
                    acc = psum[0:NP, 2 * u:2 * u + 2, 0:500].rearrange("p b (t c) -> p b t c", c=100)
                    act.wait_ge(s("win_done"), w + 1)
                    nc.scalar.copy(adj_v[0:NP, :, bass.ds(w * WD, WD)].rearrange("p (b t) c -> p b t c", b=2), acc[:, :, :, 0:WD]).then_inc(s("win_counts"), 1)
                    act.wait_ge(s("win_weights"), w + 1)
                    nc.scalar.copy(cparts[u][0:NP].rearrange("p (b t) c -> p b t c", b=2), acc[:, :, :, WD:4 * WD]).then_inc(s("parts_ready"), 1)
                    act.wait_ge(s("parts_ready"), w + 1)
                    act.sem_inc(s("win_read"), 1)
            act.wait_ge(s("win_weights"), NW + 2)
            take_rows("h1", 0)
            act.wait_ge(s("small_in"), 48)
            act.wait_ge(s("fc_bias_used"), 1)
            take_cols("conv1", 4, r2, ACT.Relu, b1c)
            take_rows("h2", 4)
            take_cols("conv2", 0, r1, ACT.Relu, b2c)
            act.wait_ge(s("gru_init"), 1)
            nc.scalar.activation(warm[:], scl[:, 1:2], ACT.Sigmoid).then_inc(s("warm"), 1)

            def put(t, c, g):
                columns = psum[:, 4 * c + 2, 3:8:4] if g == 2 else psum[:, 4 * c + g, 2:6:3]
                return nc.scalar.copy(columns, big[:, bass.ds(t * 12 + c * 6 + 2 * g, 2)])

            for c in range(2):
                for g in range(2):
                    put(0, c, g)
                put(0, c, 2).then_inc(s(f"gru_put{c}"), 1)
            with act.Fori(0, N // 2) as i:
                for u in range(2):
                    t = 2 * i + u

                    def gate_r(c):
                        act.wait_ge(s(f"gru_r_sum{c}"), t + 1)
                        nc.scalar.activation(mul_n[:, c, 3:8:4], sum_rz[:, c, 0, 2:6:3], ACT.Sigmoid).then_inc(s(f"gru_r{c}"), 1)

                    def gate_z(c):
                        act.wait_ge(s(f"gru_z_sum{c}"), t + 1)
                        nc.scalar.activation(upd_mul[:, c, 2:14:7], sum_rz[:, c, 1, 2:6:3], ACT.Sigmoid).then_inc(s(f"gru_z{c}"), 1)

                    def gate_n(c):
                        act.wait_ge(s(f"gru_n_sum{c}"), t + 1)
                        nc.scalar.activation(upd_add[:, c, 0:14:7], sum_n[:, c, 3:8:4], ACT.Tanh).then_inc(s(f"gru_n{c}"), 1)

                    gate_r(0)
                    put(t + 1, 0, 0)
                    gate_z(0)
                    gate_n(0)
                    gate_r(1)
                    put(t + 1, 0, 1)
                    put(t + 1, 0, 2).then_inc(s("gru_put0"), 1)
                    put(t + 1, 1, 0)
                    gate_n(1)
                    put(t + 1, 1, 2)
                    gate_z(1)
                    put(t + 1, 1, 1).then_inc(s("gru_put1"), 1)
            take_turned("fc", 0)
            take_cols("l1agg", 0, r1, None)
            for f in range(KT):
                act.wait_ge(s("bn_ready"), f + 1)
                nc.scalar.activation(r1[:, f], r1[:, f], ACT.Relu, scale=bnc[:, 0, f:f + 1], bias=bnc[:, 1, f:f + 1]).then_inc(s("l1norm"), 1)
            take_turned("l1out", 4)
            act.wait_ge(s("gate_in"), 1)
            nc.scalar.activation(gates[0:NP], gates[0:NP], ACT.Exp).then_inc(s("gate_exp"), 1)
            act.wait_ge(s("mean_ready"), NT)
            take_cols("aggx", 4, agg_x, None)
            with act.Fori(0, NE // 2) as ei:
                for u in range(2):
                    e = 2 * ei + u
                    b0, b1 = (0, 4) if u == 0 else (4, 0)
                    nc.scalar.copy(ebias[:], blc[:, bass.ds(e * KT, KT)]).then_inc(s("ebias"), 1)
                    act.wait_ge(s("ebias"), e + 1)
                    i = 0
                    for f in range(KT):
                        for n0, n1 in NCH:
                            act.wait_ge(s("layer1_done"), e * 12 + i + 1)
                            nc.scalar.activation(r1[:, f, n0:n1], psum[:, b0 + i % 4, 0:n1 - n0], ACT.Relu,
                                                 bias=ebias[:, f:f + 1]).then_inc(s("layer1_stored"), 1)
                            i += 1
                    take_rows("u", b1, base=e * NT)
            take_turned("l2", 0)
            take_rows("z", 4)

        @block.vector
        def _(dve):
            v = nc.vector
            linked, roots = [0], [0]

            def link(ins):
                linked[0] += 1
                ins.then_inc(s("dve_link"), 1)
                dve.wait_ge(s("dve_link"), linked[0])

            def ln_rows(t, name):
                x = xr[0:NP, t]
                link(v.bn_stats(stat[0:NP, 0], x))
                link(v.bn_aggr(mv[0:NP, 0:2], stat[0:NP, 0]))
                roots[0] += 1
                v.tensor_scalar(mv[0:NP, 2:3], mv[0:NP, 1:2], LN_EPS, None, ALU.add).then_inc(s("var"), 1)
                dve.wait_ge(s("root"), roots[0])
                v.tensor_scalar(x, x, mv[0:NP, 0:1], mv[0:NP, 2:3], ALU.subtract, ALU.mult).then_inc(s(name), 1)

            dve.wait_ge(s("edges_in"), 48)
            link(v.tensor_copy(e_stage[0:EH, 0:2], e_int[0:EH]))
            dve.sem_inc(s("edges_f"), 1)
            pair_dst = e_stage[0:EH, 1].rearrange("p h e -> p (h e)")
            link(v.tensor_reduce(p_lim[:, 0:1], pair_dst, AX.X, ALU.min))
            link(v.tensor_reduce(p_lim[:, 1:2], pair_dst, AX.X, ALU.max))
            dve.sem_inc(s("limits"), 1)
            dve.wait_ge(s("edges_turn"), 1)
            link(v.tensor_copy(e_col[0:EP], psum[0:EP, 0:3, 0:ET]))
            link(v.memset(w_part[0:EP, :, 0], 1.0))
            rest = e_w
            for a in range(3):
                link(v.tensor_copy(w_bf[0:EP], rest[0:EP]))
                link(v.tensor_copy(w_part[0:EP, :, a + 1], w_bf[0:EP]))
                if a < 2:
                    link(v.tensor_tensor(w_res[0:EP, a], rest[0:EP], w_bf[0:EP], ALU.subtract))
                    rest = w_res[:, a]
            dve.wait_ge(s("const"), 9)
            dve.wait_ge(s("limits_all"), 1)
            link(v.tensor_scalar(hit[0:NW], psum[0:NW, 3, 0:EH], w_lim[0:NW, 1:2], None, ALU.is_lt))
            link(v.scalar_tensor_tensor(out=hit_b[0:NW], in0=psum[0:NW, 3, EH:2 * EH], scalar=w_lim[0:NW, 0:1], in1=hit[0:NW], op0=ALU.is_ge, op1=ALU.mult))
            for a in range(2):
                link(v.tensor_tensor(hit[0:NW], hit_b[0:NW], pair_no[0:NW, a], ALU.mult))
                link(v.tensor_reduce(span[0:NW, a:a + 1], hit[0:NW], AX.X, ALU.max))
            dve.sem_inc(s("span"), 1)
            dve.wait_ge(s("span_row"), 1)
            last, first, count, total, before = (row[:, a] for a in range(5))
            link(v.tensor_scalar(first, psum[0:1, 4, NW:2 * NW], -1.0, float(EH), ALU.mult, ALU.add))
            link(v.tensor_scalar(first, first, float(EH - 1), None, ALU.min))
            link(v.tensor_copy(last, psum[0:1, 4, 0:NW]))
            link(v.scalar_tensor_tensor(out=last, in0=first, scalar=1.0, in1=last, op0=ALU.add, op1=ALU.max))
            link(v.tensor_tensor(count, last, first, ALU.subtract))
            link(v.tensor_tensor_scan(total, ones[0:1, 0:NW], count, 0.0, ALU.mult, ALU.add))
            link(v.tensor_tensor(before, total, count, ALU.subtract))
            offset = row[:, 5]
            link(v.tensor_scalar(before, before, float(EH), None, ALU.add))
            link(v.tensor_tensor(offset, before, first, ALU.subtract))
            link(v.scalar_tensor_tensor(out=offset, in0=offset, scalar=float(EH), in1=last, op0=ALU.mult, op1=ALU.add))
            link(v.tensor_scalar(offset, offset, -1.0, None, ALU.add))
            for a, val in enumerate((first, count, before, offset)):
                link(v.tensor_copy(bounds[:, a], val))
            dve.sem_inc(s("bounds"), 1)
            for h in range(2):
                dve.sem_inc(s(f"hot_used{h}"), EH + 1)
                dve.sem_inc(s(f"hot_ready{h}"), EH)
            with dve.Fori(0, NW) as w:
                first = dve.value_load(bounds[0:1, 0, bass.ds(w, 1)], min_val=0, max_val=EH - 1)
                packed = dve.value_load(bounds[0:1, 3, bass.ds(w, 1)], min_val=0, max_val=EH * EH * (NW + 2))
                end, offset = dve.snap(packed % EH + 1), dve.snap(packed // EH)
                with dve.Fori(first, end) as pair:
                    for h in range(2):
                        column = pair + h * EH
                        dve.wait_ge(s(f"hot_used{h}"), offset + pair + 1)
                        v.tensor_scalar(src_hot[0:EP, h], iota16[0:EP], e_src[0:EP, bass.ds(column, 1)], None, ALU.is_equal)
                        v.scalar_tensor_tensor(
                            out=dst_hot[0:EP, h].rearrange("p (a c) -> p a c", a=4),
                            in0=iota16[0:EP, bass.ds(w * WD, WD)].unsqueeze(1).broadcast_to([EP, 4, WD]), scalar=e_dst[0:EP, bass.ds(column, 1)],
                            in1=w_part[0:EP, bass.ds(column, 1), :].rearrange("p t a -> p (t a)").unsqueeze(2).broadcast_to([EP, 4, WD]),
                            op0=ALU.is_equal, op1=ALU.mult).then_inc(s(f"hot_ready{h}"), 1)
            dve.wait_ge(s("x_in"), 16)
            dve.wait_ge(s("bfc_in"), 16)
            link(v.tensor_tensor(xr[0:NP], xr[0:NP], fc_bias[0:NP].unsqueeze(1).broadcast_to([NP, NT, D]), ALU.add))
            dve.sem_inc(s("fc_bias_used"), 1)
            for c, (n0, n1) in enumerate(NCH):
                dve.wait_ge(s("deg"), c + 1)
                v.tensor_scalar(inv_row[:, n0:n1], psum[:, 4 + c, 0:n1 - n0], 1.0, None, ALU.add).then_inc(s("deg1"), 1)
                v.tensor_scalar(invdeg_row[:, n0:n1], psum[:, 4 + c, 0:n1 - n0], 1.0, None, ALU.max).then_inc(s("deg_max"), 1)
            dve.wait_ge(s("deg1_turn"), 1)
            v.tensor_copy(inv_col[0:NP], psum[0:NP, 7, 0:NT]).then_inc(s("deg1_col"), 1)
            dve.wait_ge(s("deg_max"), 3)
            link(v.reciprocal(invdeg_row, invdeg_row))
            dve.sem_inc(s("invdeg_ready"), 1)
            dve.wait_ge(s("inv_rows"), 1)
            for b in range(3):
                n0, n1 = 4 * NP * b, min(4 * NP * (b + 1), N)
                link(v.tensor_copy(inv_row[:, n0:n1], psum[:, 4 + b, 0:n1 - n0]))
            for t in range(NT):
                dve.wait_ge(s(f"cnt_out{t // 5}"), 16)
                diag = adj_v[0:NP, t, t * NP:(t + 1) * NP]
                link(v.tensor_tensor(diag, diag, ident[0:NP, 0:NP], ALU.add))
                v.scalar_tensor_tensor(out=adj_v[0:NP, t], in0=adj_v[0:NP, t], scalar=inv_col[0:NP, t:t + 1], in1=inv_row[0:NP],
                                       op0=ALU.mult, op1=ALU.mult).then_inc(s("norm"), 1)
            dve.wait_ge(s("wt_out"), 16)
            for d in range(NT):
                for q in range(3):
                    n = 3 * d + q
                    dve.wait_ge(s("tr_done"), n + 1)
                    width = min(4, NT - 4 * q) * NP
                    v.tensor_copy(wt_v[0:NP, d, 4 * q * NP:4 * q * NP + width], psum[0:NP, n % 4, 0:width]).then_inc(s("tr_stored"), 1)
            dve.wait_ge(s("whh_in"), 48)
            for g, place in enumerate((whh[0], whh[1], ws[:, WSLOT:2 * WSLOT])):
                link(v.tensor_reduce(wmax[:, 2 * g:2 * g + 1], place, AX.X, ALU.max))
                link(v.tensor_reduce(wmax[:, 2 * g + 1:2 * g + 2], place, AX.X, ALU.min))
            link(v.tensor_scalar(wmax[:, 8:11], wmax[:, 1:6:2], -1.0, None, ALU.mult))
            link(v.tensor_tensor(wmax[:, 8:11], wmax[:, 8:11], wmax[:, 0:6:2], ALU.max))
            link(v.tensor_reduce(wmax[:, 6:7], wmax[:, 8:11], AX.X, ALU.max))
            dve.sem_inc(s("wmax_part"), 1)
            dve.wait_ge(s("wmax_all"), 1)
            link(v.tensor_scalar(wmax[:, 7:8], wmax[:, 7:8], 2.0 ** -60, None, ALU.max))
            bits = wmax[:, 7:8].bitcast(I32)
            link(v.tensor_scalar(bits, bits, 0x7F800000, None, ALU.bitwise_and))
            one = float(1 << 23)
            scl_i, scw_i = scl[:].bitcast(I32), scw[:].bitcast(I32)
            link(v.tensor_scalar(scw_i[:, 0:1], bits, -1.0, (13 + 2 * 127) * one, ALU.mult, ALU.add))
            link(v.tensor_scalar(scl_i[:, 0:1], scw_i[:, 0:1], 12 * one, None, ALU.add))
            link(v.tensor_scalar(scl_i[:, 1:2], scl_i[:, 0:1], -1.0, 2 * 127 * one, ALU.mult, ALU.add))
            link(v.tensor_scalar(scw[:, 1:2], scw[:, 0:1], -1.0, None, ALU.mult))

            def split(g, source):
                flat = whh[g].bitcast(F16)
                hi, lo = flat[:, 0:WSLOT], flat[:, WSLOT:2 * WSLOT]
                sc = scw[:, 1:2] if g == 1 else scw[:, 0:1]
                link(v.tensor_scalar(hi, source, sc, None, ALU.mult))
                link(v.scalar_tensor_tensor(out=lo, in0=source, scalar=sc, in1=hi, op0=ALU.mult, op1=ALU.subtract))
                dve.sem_inc(s("whh_split"), 1)

            dve.wait_ge(s("h1_done"), NT)
            for g in range(2):
                link(v.tensor_copy(ws[:, 0:WSLOT], whh[g]))
                split(g, ws[:, 0:WSLOT])
            dve.wait_ge(s("conv2_done"), 12)
            split(2, ws[:, WSLOT:2 * WSLOT])
            link(v.tensor_tensor(pbias[:, 0:8], bihc[:, 0:8], bhhc[:, 0:8], ALU.add))
            link(v.tensor_copy(pbias[:, 8:12], bihc[:, 8:12]))
            link(v.tensor_scalar(pbias[:, 4:8], pbias[:, 4:8], -1.0, None, ALU.mult))
            dve.wait_ge(s("adj_out"), 16)
            dve.wait_ge(s("invdeg_out"), 16)
            i = 0
            for g in range(3):
                for j in range(KT):
                    for n0, n1 in NCH:
                        dve.wait_ge(s("pre_done"), i + 1)
                        q = (j // 2) * 6 + g * 2 + j % 2
                        v.tensor_scalar(pi_v[:, n0:n1, q], psum[:, 4 + i % 4, 0:n1 - n0], -1.0 if g == 1 else 1.0,
                                        pbias[:, 4 * g + j:4 * g + j + 1], ALU.mult, ALU.add).then_inc(s("pre_stored"), 1)
                        i += 1
            dve.wait_ge(s("pre_stored"), 36)
            link(v.memset(h16[:], 0.0))
            link(v.memset(mul_rz[:], 1.0))
            link(v.memset(mul_rz[:, 0:6:3], 0.0))
            link(v.tensor_copy(mul_rz[:, 2:6:3], scl[:, 1:2].to_broadcast([P, 2])))
            link(v.memset(mul_n[:], 1.0))
            link(v.memset(mul_n[:, :, 0:8:4], 0.0))
            for c in range(2):
                link(v.tensor_copy(mul_n[:, c, 2:8:4], scl[:, 1:2].to_broadcast([P, 2])))
            link(v.memset(upd_mul[:], 1.0))
            link(v.memset(upd_mul[:, :, 0:14:7], 0.0))
            link(v.memset(upd_mul[:, :, 3:14:7], HS))
            link(v.memset(upd_mul[:, :, 6:14:7], 0.0))
            link(v.memset(upd_add[:], 0.0))
            link(v.memset(upd_add[:, :, 4:14:7], ROUND))
            link(v.memset(upd_add[:, :, 5:14:7], -ROUND))
            link(v.memset(signs[:], 1.0))
            link(v.memset(signs[:, 0:4:2], -1.0))
            for c in range(2):
                link(v.memset(psum[:, 4 * c:4 * c + 3, 0:8], 0.0))
                link(v.tensor_copy(psum[:, 4 * c + 2, 2:8:4], bhhc[:, 8 + 2 * c:10 + 2 * c]))
            dve.sem_inc(s("gru_init"), 1)
            for c in range(2):
                dve.sem_inc(s(f"gru_state{c}"), 1)
                dve.sem_inc(s(f"gru_fresh{c}"), 1)
            signs_v = signs[:].rearrange("p (j a) -> p j a", a=2)

            def sevens(ap):
                return ap.rearrange("p (j a) -> p j a", a=7)

            def scan_rz(t, c, g):
                dve.wait_ge(s(f"gru_{'rz'[g]}_mm{c}"), t + 1)
                v.tensor_tensor_scan(sum_rz[:, c, g], mul_rz[:], psum[:, 4 * c + g, 0:6], 0.0, ALU.mult, ALU.add).then_inc(s(f"gru_{'rz'[g]}_sum{c}"), 1)

            def scan_n(t, c):
                dve.wait_ge(s(f"gru_n_mm{c}"), t + 1)
                dve.wait_ge(s(f"gru_r{c}"), t + 1)
                v.tensor_tensor_scan(sum_n[:, c], mul_n[:, c], psum[:, 4 * c + 2, 0:8], 0.0, ALU.mult, ALU.add).then_inc(s(f"gru_n_sum{c}"), 1)

            def update(t, u, c):
                dve.wait_ge(s(f"gru_kept{c}"), t + 1)
                dve.wait_ge(s(f"gru_fresh{c}"), t + 1)
                for gate in "zn" if c == 0 else "nz":
                    dve.wait_ge(s(f"gru_{gate}{c}"), t + 1)
                v.tensor_tensor_scan(upd[:, 1 - u, c], upd_mul[:, c], upd_add[:, c], 0.0, ALU.mult, ALU.add).then_inc(s(f"gru_upd{c}"), 1)

            def parts(t, u, c):
                dve.wait_ge(s(f"gru_upd{c}"), t + 1)
                new = sevens(upd[:, 1 - u, c])
                v.tensor_tensor(h16[:, 1 - u, c], new[:, :, 3:6:2], new[:, :, 5:7], ALU.subtract).then_inc(s(f"gru_state{c}"), 1)
                v.tensor_tensor(sevens(upd_add[:, c])[:, :, 1:3], new[:, :, 2:3].broadcast_to([P, 2, 2]), signs_v, ALU.mult).then_inc(s(f"gru_fresh{c}"), 1)

            with dve.Fori(0, N // 2) as i:
                for u in range(2):
                    t = 2 * i + u
                    scan_rz(t, 0, 0)
                    scan_rz(t, 0, 1)
                    scan_n(t, 0)
                    scan_rz(t, 1, 0)
                    update(t, u, 0)
                    scan_n(t, 1)
                    parts(t, u, 0)
                    scan_rz(t, 1, 1)
                    update(t, u, 1)
                    parts(t, u, 1)
            for t in range(NT):
                dve.wait_ge(s("fc_done"), t + 1)
                v.tensor_tensor(xr[0:NP, t], psum[0:NP, 4 + t % 4], xr[0:NP, t], ALU.add).then_inc(s("fc_stored"), 1)
                dve.wait_ge(s("fc_stored"), t + 1)
                ln_rows(t, "fc_ln")
            dve.wait_ge(s("l1b1_in"), 16)
            for t in range(NT):
                dve.wait_ge(s("l1h1_done"), t + 1)
                v.tensor_tensor(hn[0:NP, t], psum[0:NP, 4 + t % 4], l1_bias[0:NP], ALU.add).then_inc(s("l1h1_stored"), 1)
            dve.wait_ge(s("cnt_in"), 16)
            dve.wait_ge(s("invdeg_in"), 16)
            for t in range(NT):
                v.tensor_tensor(wt_v[0:NP, t], wt_v[0:NP, t], invdeg_row[0:NP], ALU.mult).then_inc(s("mean_ready"), 1)
            for f in range(KT):
                for c, (n0, n1) in enumerate(NCH):
                    dve.wait_ge(s("l1agg_stored"), 3 * f + c + 1)
                    link(v.bn_stats(stat[:, c], r1[:, f, n0:n1]))
                link(v.bn_aggr(mv[:, 0:2], stat[:].rearrange("p a b -> p (a b)")))
                roots[0] += 1
                v.tensor_scalar(mv[:, 2:3], mv[:, 1:2], 1e-5, None, ALU.add).then_inc(s("var"), 1)
                dve.wait_ge(s("root"), roots[0])
                link(v.tensor_tensor(bnc[:, 0, f:f + 1], mv[:, 2:3], gamc[:, f:f + 1], ALU.mult))
                link(v.tensor_tensor(mv[:, 3:4], mv[:, 0:1], bnc[:, 0, f:f + 1], ALU.mult))
                link(v.tensor_tensor(bnc[:, 1, f:f + 1], betc[:, f:f + 1], mv[:, 3:4], ALU.subtract))
                dve.sem_inc(s("bn_ready"), 1)
            dve.wait_ge(s("l1b2_in"), 16)
            for t in range(NT):
                dve.wait_ge(s("l1h2_done"), t + 1)
                v.tensor_tensor(hn[0:NP, t], psum[0:NP, 4 + t % 4], l1_bias[0:NP], ALU.add).then_inc(s("l1h2_stored"), 1)
            for t in range(NT):
                dve.wait_ge(s("l1out_done"), t + 1)
                v.tensor_tensor(xr[0:NP, t], psum[0:NP, t % 4], xr[0:NP, t], ALU.add).then_inc(s("l1out_stored"), 1)
                dve.wait_ge(s("l1out_stored"), t + 1)
                ln_rows(t, "l1out_ln")
            dve.wait_ge(s("logits"), 1)
            link(v.tensor_tensor(gates[0:NP], psum[0:NP, 0, 0:NT * NE].rearrange("p (t e) -> p t e", e=NE), gate_b[0:NP].unsqueeze(1).broadcast_to([NP, NT, NE]), ALU.add))
            dve.sem_inc(s("gates_read"), 1)
            link(v.tensor_reduce(gtmp[0:NP, 0], gates[0:NP], AX.X, ALU.max))
            link(v.tensor_tensor(gates[0:NP], gates[0:NP], gtmp[0:NP, 0].unsqueeze(2).broadcast_to([NP, NT, NE]), ALU.subtract))
            dve.sem_inc(s("gate_in"), 1)
            dve.wait_ge(s("gate_exp"), 1)
            link(v.tensor_reduce(gtmp[0:NP, 0], gates[0:NP], AX.X, ALU.add))
            link(v.reciprocal(gtmp[0:NP, 0], gtmp[0:NP, 0]))
            link(v.tensor_tensor(gates[0:NP], gates[0:NP], gtmp[0:NP, 0].unsqueeze(2).broadcast_to([NP, NT, NE]), ALU.mult))
            for a in range(NE):
                n_beat = gtmp[0:NP, 1]
                link(v.memset(n_beat, 0.0))
                for b in range(NE):
                    if b != a:
                        link(v.tensor_tensor(gtmp[0:NP, 2], gates[0:NP, :, b], gates[0:NP, :, a], ALU.is_ge if b < a else ALU.is_gt))
                        link(v.tensor_tensor(n_beat, n_beat, gtmp[0:NP, 2], ALU.add))
                link(v.scalar_tensor_tensor(out=gsel[0:NP, a], in0=n_beat, scalar=2.0, in1=gates[0:NP, :, a], op0=ALU.is_lt, op1=ALU.mult))
            dve.wait_ge(s("aggx_done"), 12)
            with dve.Fori(0, NE // 2) as ei:
                for u in range(2):
                    e = 2 * ei + u
                    b0 = 0 if u == 0 else 4
                    dve.wait_ge(s("eb_in"), e * 16 + 16)
                    for t in range(NT):
                        tmp = l2_tmp[t % 2]
                        dve.wait_ge(s("eout_done"), e * NT + t + 1)
                        v.tensor_tensor(tmp, psum[0:NP, b0 + t % 4], l2_bias[0:NP], ALU.add).then_inc(s("eout_stored"), 1)
                        dve.wait_ge(s("eout_stored"), e * NT + t + 1)
                        v.tensor_scalar(tmp, tmp, 0.0, gsel[0:NP, bass.ds(e, 1), t:t + 1].rearrange("p a t -> p (a t)"), ALU.max, ALU.mult).then_inc(s("eweighted"), 1)
                        dve.wait_ge(s("eweighted"), e * NT + t + 1)
                        v.tensor_tensor(xr[0:NP, t], xr[0:NP, t], tmp, ALU.add).then_inc(s("eadd"), 1)
            dve.wait_ge(s("eadd"), NE * NT)
            for t in range(NT):
                ln_rows(t, "l2_ln")
            dve.wait_ge(s("l2_ln"), NT)
            for t in range(NT):
                dve.wait_ge(s("l3_done"), t + 1)
                v.scalar_tensor_tensor(out=xr[0:NP, t], in0=psum[0:NP, t % 4], scalar=0.0, in1=xr[0:NP, t], op0=ALU.max, op1=ALU.add).then_inc(s("l3_stored"), 1)
                dve.wait_ge(s("l3_stored"), t + 1)
                ln_rows(t, "final_ln")


def kernel(**inputs):
    import numpy as np
    import concourse.bacc as bacc
    from concourse.bass_utils import run_bass_kernel_spmd

    a = {k: np.asarray(x) for k, x in inputs.items()}

    def cols(x):
        return x.reshape(-1, P).T

    arrays = {
        "x": a["x"], "xT": a["x"].T, "src": a["src"], "dst": a["dst"], "edge_weight": a["edge_weight"],
        "W1": a["L0_gnn_W1"], "W2": a["L0_gnn_W2"], "W_ihT": a["L0_gnn_W_ih"].T, "W_hhT": a["L0_gnn_W_hh"].T,
        "W_fc": a["L0_gnn_W_fc"], "b_fc": a["L0_gnn_b_fc"],
        "l1_W1": a["L1_gnn_W1"], "l1_b1": a["L1_gnn_b1"], "l1_W2": a["L1_gnn_W2"], "l1_b2": a["L1_gnn_b2"],
        "gate_W": a["L2_gnn_gate_W"], "gate_b": a["L2_gnn_gate_b"],
        "Wl0": a["L2_gnn_Wl"][:, 0], "Wl1": a["L2_gnn_Wl"][:, 1], "Wr0": a["L2_gnn_Wr"][:, 0], "Wr1": a["L2_gnn_Wr"][:, 1],
        "bl1": a["L2_gnn_bl"][:, 1], "l3_W": a["L3_gnn_W"],
        "bcol": np.concatenate([cols(a[n]) for n in ("L0_gnn_b1", "L0_gnn_b2", "L0_gnn_b_ih", "L0_gnn_b_hh", "L1_gnn_gamma", "L1_gnn_beta")]
                               + [cols(a["L2_gnn_bl"][:, 0])], axis=1),
    }
    arrays = {f"in_{k}": np.ascontiguousarray(x) for k, x in arrays.items()}
    nc = bacc.Bacc("TRN2", target_bir_lowering=False, num_devices=1)
    io = {k[3:]: nc.dram_tensor(k, x.shape, mybir.dt.from_np(x.dtype), kind="ExternalInput").ap() for k, x in arrays.items()}
    io["out"] = nc.dram_tensor("out", (N, D), F32, kind="ExternalOutput").ap()
    layout(nc, io)
    r = run_bass_kernel_spmd(nc, [arrays], core_ids=[0])
    return r.results[0]["out"]
```

```python
from contextlib import ExitStack

import concourse.bass as bass
from concourse import mybir

ACT = mybir.ActivationFunctionType
ALU = mybir.AluOpType
AX = mybir.AxisListType
F32 = mybir.dt.float32
F16 = mybir.dt.float16
BF16 = mybir.dt.bfloat16
I32 = mybir.dt.int32

N, D, E = 1250, 512, 20000
P = 128
NP, NT = 125, 10
KT = D // P
EP, ET = 125, 160
EH = ET // 2
WD = 25
NW = N // WD
NCH = [(0, 417), (417, 834), (834, 1250)]
NE = 4
LN_EPS = 1e-5
HS = 4096.0
ROUND = 1.5 * 2.0 ** 24
XS = 2.0 ** 10
US = 2.0 ** -15
EXACT = 2048.0
L2_STEPS = 35
WSLOT = KT * D


def layout(nc, io):
    ctx = ExitStack()
    with ctx:
        def sb(name, shape, dt=F32):
            return ctx.enter_context(nc.sbuf_tensor(name, shape, dt))

        def sem(name):
            return ctx.enter_context(nc.semaphore(name))


        adj = sb("adj", [P, NT * N])
        big = sb("big", [P, (N + 1) * 12])
        xr = sb("xr", [P, NT, D])
        r1 = sb("r1", [P, KT, N])
        r2 = sb("r2", [P, KT, N])
        hn = sb("hn", [P, NT, D])
        ws = sb("ws", [P, 2 * WSLOT])
        psum = ctx.enter_context(nc.psum_tensor("psum", [P, 8, 512], F32))

        adj_v = adj[:].rearrange("p (t n) -> p t n", n=N)
        wt_v = big[:, 0:NT * N].rearrange("p (t n) -> p t n", n=N)
        pi_v = big[:].rearrange("p (t q) -> p t q", q=12)
        tail = NT * N
        inv_row = big[:, tail:tail + N]
        invdeg_row = big[:, tail + N:tail + 2 * N]
        l1_bias = big[:, tail:tail + D]
        hn_f = hn[:].rearrange("p t d -> p (t d)")
        r2_f = r2[:].rearrange("p k n -> p (k n)")
        fc_bias = r2_f[:, 4400:4400 + D]

        def weight(ap):
            return ap.rearrange("p (k n) -> p k n", k=KT)

        def wslot(i):
            return weight(ws[:, i * WSLOT:(i + 1) * WSLOT])

        w_fc = weight(hn_f[:, 0:WSLOT])
        whh = [r2_f[:, 0:WSLOT], r2_f[:, WSLOT:2 * WSLOT], hn_f[:, WSLOT:2 * WSLOT]]
        whh16 = [a.bitcast(F16).rearrange("p (a k n) -> p a k n", a=2, k=KT) for a in whh]
        at = 4 * WSLOT
        agg_x = [a.bitcast(F16).rearrange("p (a n) -> p a n", a=2) for a in
                 (big[:, tail:tail + N], big[:, tail + N:tail + 2 * N], adj[:, at:at + N], adj[:, at + N:at + 2 * N])]
        l2_bias = adj[:, at + 2 * N:at + 2 * N + D]
        at += 2 * N + D
        l2_tmp = [adj[0:NP, at + i * D:at + (i + 1) * D] for i in range(2)]
        layer1_f32 = [adj[:, at + i * D:at + (i + 1) * D] for i in range(2)]
        l2w16 = [adj[:, i * WSLOT:(i + 1) * WSLOT].bitcast(F16).rearrange("p (a k n) -> p a k n", a=2, k=KT) for i in range(4)]
        cnt16 = big[:, 0:NT * N].bitcast(F16).rearrange("p (t a n) -> p t a n", t=NT, a=2)
        rows16 = hn_f.bitcast(F16).rearrange("p (t a n) -> p t a n", t=NT, a=2)
        r1_16 = r1[:].rearrange("p k n -> p (k n)").bitcast(F16).rearrange("p (a k n) -> p a k n", a=2, k=KT)
        r2_16 = r2_f.bitcast(F16).rearrange("p (a k n) -> p a k n", a=2, k=KT)
        cnt_f32 = ws[0:NP, 0:N]
        invdeg_l2 = adj[:, 2 * WSLOT:2 * WSLOT + N]

        iota16 = r2_f[:, 0:625].bitcast(F16)
        src_hot = r2_f[:, 625:625 * 3].bitcast(BF16).rearrange("p (h n) -> p h n", h=2)
        dst_hot = r2_f[:, 3125:3225].bitcast(BF16).rearrange("p (h n) -> p h n", h=2)
        zero_b = r2_f[:, 3400:3400 + 250].bitcast(BF16)
        e_stage = hn_f[:, 0:750].rearrange("p (a h e) -> p a h e", a=3, h=2)
        e_int = hn_f[:, 750:1250].bitcast(I32).rearrange("p (a h e) -> p a h e", a=2, h=2)
        e_col = hn_f[:, 1250:1250 + 3 * ET].rearrange("p (a t) -> p a t", a=3)
        e_src, e_dst, e_w = e_col[:, 0], e_col[:, 1], e_col[:, 2]
        w_part = hn_f[:, 1730:2370].rearrange("p (t a) -> p t a", a=4)
        w_bf = hn_f[:, 2370:2450].bitcast(BF16)
        w_res = hn_f[:, 2610:2610 + 2 * ET].rearrange("p (a t) -> p a t", a=2)
        p_lim = hn_f[0:EH, 2930:2932]
        w_lim = hn_f[:, 2934:2936]
        pair_no = hn_f[:, 2936:2936 + 2 * EH].rearrange("p (a t) -> p a t", a=2)
        hit = hn_f[:, 3256:3256 + EH]
        hit_b = hn_f[:, 3416:3416 + EH]
        span = hn_f[:, 3576:3578]
        row = hn_f[0:1, 3578:3578 + 6 * NW].rearrange("p (a w) -> p a w", a=6)
        cparts = [a.rearrange("p (t c) -> p t c", t=NT) for a in (hn_f[:, 3880:4630], r2_f[:, 3650:4400])]

        ident = sb("ident", [P, P])
        ones = sb("ones", [P, P])
        bounds = sb("bounds", [1, 4, NW], I32)
        inv_col = sb("inv_col", [P, NT])
        invdeg_col = sb("invdeg_col", [P, NT])
        bcol = sb("bcol_sb", [P, 56])
        b1c, b2c, bihc, bhhc = bcol[:, 0:4], bcol[:, 4:8], bcol[:, 8:20], bcol[:, 20:32]
        gamc, betc, blc = bcol[:, 32:36], bcol[:, 36:40], bcol[:, 40:56]
        gate_w = sb("gate_w", [P, KT, NE])
        gate_b = sb("gate_b_sb", [P, NE])
        gates = sb("gates", [P, NT, NE])
        gsel = sb("gsel", [P, NE, NT])
        gtmp = sb("gtmp", [P, 3, NT])
        stat = sb("stat", [P, 3, 6])
        mv = sb("mv", [P, 4])
        bnc = sb("bnc", [P, 2, KT])
        wmax = sb("wmax", [P, 12])
        scl = sb("scl", [P, 2])
        scw = sb("scw", [P, 2])
        pbias = sb("pbias", [P, 12])
        h16 = sb("h16", [P, 2, 2, 2, 2], F16)
        mul_rz = sb("mul_rz", [P, 6])
        mul_n = sb("mul_n", [P, 2, 8])
        sum_rz = sb("sum_rz", [P, 2, 2, 6])
        sum_n = sb("sum_n", [P, 2, 8])
        upd_mul = sb("upd_mul", [P, 2, 14])
        upd_add = sb("upd_add", [P, 2, 14])
        upd = sb("upd", [P, 2, 2, 14])
        signs = sb("signs", [P, 4])
        minus_half = sb("minus_half", [P, 1])
        ebias = sb("ebias", [P, KT])
        warm = sb("warm", [P, 1])
        agg_scale = sb("agg_scale", [P, NT])
        cnt_max = sb("cnt_max", [P, NT])
        cnt_top = sb("cnt_top", [P, 2])
        has_lo = sb("has_lo", [1, 1], I32)
        top = sb("top", [P, 6])
        esc = sb("esc", [P, 8])

        d_cnt = nc.dram_tensor("edge_counts", [NT, NP, N], F32, kind="Internal").ap()
        d_wt = nc.dram_tensor("edge_weights", [NT, NP, N], F32, kind="Internal").ap()
        d_adj = nc.dram_tensor("adj_rows", [NT, NP, N], F32, kind="Internal").ap()
        d_invdeg = nc.dram_tensor("invdeg", [P, N], F32, kind="Internal").ap()

        sems = {}

        def s(name):
            if name not in sems:
                sems[name] = sem(name)
            return sems[name]

        block = ctx.enter_context(nc.Block())

        def w_rows(dst_ap, src):
            return dst_ap, src.rearrange("(k p) n -> p k n", p=P)

        def tiles(ap):
            return ap.rearrange("t p n -> p t n")

        @block.sync
        def _(sp):
            for a, name in enumerate(("src", "dst")):
                sp.dma_start(e_int[0:EH, a], io[name].rearrange("(q h e) -> q h e", h=2, e=EP)).then_inc(s("edges_in"), 16)
            sp.dma_start(e_stage[0:EH, 2], io["edge_weight"].rearrange("(q h e) -> q h e", h=2, e=EP)).then_inc(s("edges_in"), 16)
            sp.dma_start(r1[:], io["xT"].rearrange("(k p) n -> p k n", p=P)).then_inc(s("xcols_in"), 16)
            sp.dma_start(*w_rows(wslot(0), io["W1"])).then_inc(s("w1_in"), 16)
            sp.dma_start(*w_rows(wslot(1), io["W2"])).then_inc(s("w2_in"), 16)
            sp.dma_start(bcol[:], io["bcol"]).then_inc(s("small_in"), 16)
            sp.dma_start(gate_w[:], io["gate_W"].rearrange("(k p) e -> p k e", p=P)).then_inc(s("small_in"), 16)
            sp.dma_start(gate_b[:], io["gate_b"].partition_broadcast(P)).then_inc(s("small_in"), 16)
            sp.dma_start(xr[0:NP], io["x"].rearrange("(t p) d -> p t d", p=NP)).then_inc(s("x_in"), 16)
            sp.dma_start(fc_bias, io["b_fc"].partition_broadcast(P)).then_inc(s("bfc_in"), 16)
            sp.wait_ge(s("win_counts"), NW)
            for h in range(2):
                half = slice(5 * h, 5 * h + 5)
                sp.dma_start(tiles(d_cnt[half]), adj_v[0:NP, half]).then_inc(s(f"cnt_out{h}"), 16)
            sp.wait_ge(s("win_weights"), NW + 2)
            sp.dma_start(tiles(d_wt), wt_v[0:NP]).then_inc(s("wt_out"), 16)
            sp.wait_ge(s("invdeg_ready"), 1)
            sp.dma_start(d_invdeg, invdeg_row).then_inc(s("invdeg_out"), 16)
            sp.wait_ge(s("tr_stored"), 3 * NT)
            sp.dma_start(tiles(d_adj), wt_v[0:NP]).then_inc(s("adj_out"), 16)
            sp.wait_ge(s("h2_done"), NT)
            for g, place in enumerate((weight(whh[0]), weight(whh[1]), wslot(1))):
                sp.dma_start(*w_rows(place, io["W_hhT"][:, g * D:(g + 1) * D])).then_inc(s("whh_in"), 16)
            sp.wait_ge(s("whh_split"), 2)
            sp.dma_start(*w_rows(wslot(0), io["W_ihT"][:, 0:D])).then_inc(s("wih_in0"), 16)
            sp.wait_ge(s("whh_split"), 3)
            sp.dma_start(*w_rows(wslot(1), io["W_ihT"][:, D:2 * D])).then_inc(s("wih_in1"), 16)
            sp.wait_ge(s("conv2_done"), 12)
            sp.dma_start(*w_rows(w_fc, io["W_fc"])).then_inc(s("wfc_in"), 16)
            sp.wait_ge(s("adj_out"), 16)
            sp.dma_start(adj_v[0:NP], tiles(d_adj)).then_inc(s("adj_in"), 16)
            sp.wait_ge(s("pre_done"), 12)
            sp.dma_start(*w_rows(wslot(0), io["W_ihT"][:, 2 * D:3 * D])).then_inc(s("wih_in2"), 16)
            sp.wait_ge(s("pre_done"), 36)
            sp.dma_start(*w_rows(wslot(0), io["l1_W1"])).then_inc(s("l1w1_in"), 16)
            sp.dma_start(*w_rows(wslot(1), io["l1_W2"])).then_inc(s("l1w2_in"), 16)
            for c in range(2):
                sp.wait_ge(s(f"gru_put{c}"), N + 1)
            sp.dma_start(l1_bias, io["l1_b1"].partition_broadcast(P)).then_inc(s("l1b1_in"), 16)
            sp.dma_start(invdeg_row, d_invdeg).then_inc(s("invdeg_in"), 16)
            sp.wait_ge(s("cnt_out0"), 16)
            sp.wait_ge(s("cnt_out1"), 16)
            sp.dma_start(wt_v[0:NP], tiles(d_cnt)).then_inc(s("cnt_in"), 16)
            sp.wait_ge(s("l1h1_stored"), NT)
            sp.dma_start(l1_bias, io["l1_b2"].partition_broadcast(P)).then_inc(s("l1b2_in"), 16)
            def l2_weights(e, layer):
                for m, name in enumerate((f"Wl{layer}", f"Wr{layer}")):
                    sp.dma_start(wslot(m), io[name][bass.ds(e, 1)].rearrange("e (k p) n -> p (e k) n", p=P)).then_inc(s(f"ew{layer}_in"), 16)

            sp.wait_ge(s("l1h2_done"), NT)
            sp.wait_ge(s("cnt_ready"), NT)
            l2_weights(0, 0)
            with sp.Fori(0, NE) as e:
                sp.wait_ge(s("ew0_split"), e + 1)
                l2_weights(e, 1)
                sp.wait_ge(s("eadd"), e * NT)
                sp.dma_start(l2_bias, io["bl1"][bass.ds(e, 1)].rearrange("e d -> (e d)").partition_broadcast(P)).then_inc(s("eb_in"), 16)
                sp.wait_ge(s("ew1_split"), e + 1)
                l2_weights(sp.snap((e + 1) % NE), 0)
            sp.wait_ge(s("ew0_split"), NE + 1)
            sp.dma_start(*w_rows(wslot(0), io["l3_W"])).then_inc(s("l3w_in"), 16)
            sp.wait_ge(s("eadd"), NE * NT)
            sp.wait_ge(s("wt_out"), 16)
            sp.dma_start(adj_v[0:NP], tiles(d_wt)).then_inc(s("wt_in"), 16)
            for t in range(NT):
                sp.wait_ge(s("final_ln"), t + 1)
                sp.dma_start(io["out"][t * NP:(t + 1) * NP], xr[0:NP, t]).then_inc(s("out_stored"), 16)
            sp.wait_ge(s("out_stored"), 16 * NT)

        @block.gpsimd
        def _(pool):
            pool.memset(ident[:], 0.0).then_inc(s("ident0"), 1)
            pool.memset(ones[:], 1.0).then_inc(s("const"), 1)
            pool.memset(zero_b, 0.0).then_inc(s("const"), 1)
            pool.memset(minus_half[:], -0.5).then_inc(s("const"), 1)
            pool.memset(big[:, N * 12:], 0.0).then_inc(s("const"), 1)
            pool.wait_ge(s("ident0"), 1)
            pool.affine_select(out=ident[:], in_=ident[:], compare_op=ALU.not_equal, fill=1.0, base=0,
                               pattern=[[-1, P]], channel_multiplier=1).then_inc(s("const"), 1)
            small = dict(allow_small_or_imprecise_dtypes=True)
            pool.iota(iota16, [[1, N]], base=0, channel_multiplier=0, **small).then_inc(s("const"), 1)
            pool.iota(pair_no[:, 0], [[1, EH]], base=1, channel_multiplier=0, **small).then_inc(s("const"), 1)
            pool.iota(pair_no[:, 1], [[-1, EH]], base=EH, channel_multiplier=0, **small).then_inc(s("const"), 1)
            pool.iota(w_lim, [[WD, 2]], base=0, channel_multiplier=WD, **small).then_inc(s("const"), 1)
            pool.sem_inc(s("win_weights"), 2)
            with pool.Fori(0, NW // 2) as i:
                for u in range(2):
                    w = 2 * i + u
                    c = cparts[u][0:NP]
                    pool.wait_ge(s("parts_ready"), w + 1)
                    pool.tensor_tensor(c[:, :, 0:WD], c[:, :, 0:WD], c[:, :, WD:2 * WD], ALU.add).then_inc(s("parts_half"), 1)
                    pool.wait_ge(s("parts_half"), w + 1)
                    pool.tensor_tensor(c[:, :, 0:WD], c[:, :, 0:WD], c[:, :, 2 * WD:3 * WD], ALU.add).then_inc(s("parts_sum"), 1)
                    pool.wait_ge(s("parts_sum"), w + 1)
                    pool.tensor_copy(wt_v[0:NP, :, bass.ds(w * WD, WD)], c[:, :, 0:WD]).then_inc(s("win_weights"), 1)
            pool.wait_ge(s("deg1_col"), 1)
            pool.tensor_tensor(inv_col[0:NP], inv_col[0:NP], minus_half[0:NP, 0:1].to_broadcast([NP, NT]), ALU.pow).then_inc(s("inv_col_ready"), 1)
            pool.wait_ge(s("top_part"), 1)
            pool.partition_all_reduce(wmax[:, 7:8], wmax[:, 6:7], P, bass.bass_isa.ReduceOp.max).then_inc(s("top_all"), 1)
            for c in range(2):
                pool.sem_inc(s(f"gru_kept{c}"), 2)
            with pool.Fori(0, N // 2) as i:
                for u in range(2):
                    t = 2 * i + u
                    for c in range(2):
                        pool.wait_ge(s(f"gru_upd{c}"), t + 1)
                        pool.tensor_copy(r1[:, 2 * c:2 * c + 2, bass.ds(t, 1)], upd[:, 1 - u, c, 2:14:7]).then_inc(s(f"gru_kept{c}"), 1)
            def roots(n0, n1):
                for n in range(n0, n1):
                    p = slice(0, P) if NT <= n < NT + KT else slice(0, NP)
                    pool.wait_ge(s("var"), n + 1)
                    pool.tensor_tensor(mv[p, 2:3], mv[p, 2:3], minus_half[p, 0:1], ALU.pow).then_inc(s("root"), 1)

            roots(0, 2 * NT + KT)
            pool.wait_ge(s("top_part"), 2)
            pool.partition_all_reduce(cnt_top[:, 1:2], cnt_top[:, 0:1], P, bass.bass_isa.ReduceOp.max).then_inc(s("top_all"), 1)
            pool.wait_ge(s("top_part"), 3)
            pool.partition_all_reduce(top[:, 4:5], top[:, 5:6], P, bass.bass_isa.ReduceOp.max).then_inc(s("top_all"), 1)
            for n in range(2 * NE + 1):
                pool.wait_ge(s("top_part"), n + 4)
                pool.partition_all_reduce(top[:, 3:4], top[:, 2:3], P, bass.bass_isa.ReduceOp.max).then_inc(s("top_all"), 1)
            roots(2 * NT + KT, 4 * NT + KT)

        @block.tensor
        def _(pe):
            mm = nc.tensor.matmul

            def out_rows(i, bank0, done, stored, base=0):
                if i >= 4:
                    pe.wait_ge(s(stored), base + i - 3)
                return psum[:, bank0 + i % 4]

            def rows_product(name, bank0, cols, w, base=0, before=None):
                for t in range(NT):
                    if before:
                        before(t)
                    o = out_rows(t, bank0, None, f"{name}_stored", base)
                    for k in range(KT):
                        m = mm(o[0:NP], cols[:, k, t * NP:(t + 1) * NP], w[:, k], start=(k == 0), stop=(k == KT - 1))
                    m.then_inc(s(f"{name}_done"), 1)

            def agg_cols(name, bank0, rows, mat):
                i = 0
                for f in range(KT):
                    for n0, n1 in NCH:
                        o = out_rows(i, bank0, None, f"{name}_stored")
                        for t in range(NT):
                            m = mm(o[:, 0:n1 - n0], rows[0:NP, t, f * P:(f + 1) * P], mat[0:NP, t, n0:n1],
                                   start=(t == 0), stop=(t == NT - 1))
                        m.then_inc(s(f"{name}_done"), 1)
                        i += 1

            def turn(name, t, bank0):
                pe.wait_ge(s(f"{name}_ln"), t + 1)
                if t >= 4:
                    pe.wait_ge(s(f"{name}_turned"), t - 3)
                for k in range(KT):
                    m = nc.tensor.transpose(psum[:, bank0 + t % 4, k * NP:(k + 1) * NP], xr[0:NP, t, k * P:(k + 1) * P], ident[0:NP, 0:NP])
                m.then_inc(s(f"{name}_turn"), 1)

            pe.wait_ge(s("const"), 9)
            pe.wait_ge(s("edges_f"), 1)
            for a in range(3):
                for h in range(2):
                    m = nc.tensor.transpose(psum[0:EP, a, h * EH:(h + 1) * EH], e_stage[0:EH, a, h], ident[0:EH, 0:EH])
            m.then_inc(s("edges_turn"), 1)
            pe.wait_ge(s("limits"), 1)
            for a in range(2):
                m = mm(psum[0:NW, 3, a * EH:(a + 1) * EH], p_lim[:, a:a + 1].to_broadcast([EH, NW]), ident[0:EH, 0:EH],
                       start=True, stop=True, skip_group_check=True)
            m.then_inc(s("limits_all"), 1)
            pe.wait_ge(s("span"), 1)
            for a in range(2):
                m = mm(psum[0:1, 4, a * NW:(a + 1) * NW], span[0:NW, a:a + 1], ident[0:NW, 0:NW], start=True, stop=True, skip_group_check=True)
            m.then_inc(s("span_row"), 1)
            pe.wait_ge(s("bounds"), 1)
            with pe.Fori(0, NW // 2) as i:
                for u in range(2):
                    w = 2 * i + u
                    blocks = pe.value_load(bounds[0:1, 1, bass.ds(w, 1)], min_val=1, max_val=EH)
                    before = pe.value_load(bounds[0:1, 2, bass.ds(w, 1)], min_val=0, max_val=EH * (NW + 1))
                    pe.wait_ge(s("win_read"), w + 1)
                    for b in range(2):
                        mm(psum[0:NP, 2 * u + b, 0:1], zero_b[0:NP, 0:NP], zero_b[0:NP, 0:1], start=True, stop=False, skip_group_check=True)
                    with pe.Fori(0, blocks) as j:
                        g = before + j
                        for h in range(2):
                            pe.wait_ge(s(f"hot_ready{h}"), g + 1)
                            for t in range(NT):
                                m = mm(psum[0:NP, 2 * u + t // 5, (t % 5) * 100:(t % 5) * 100 + 100],
                                       src_hot[0:EP, h, t * NP:(t + 1) * NP], dst_hot[0:EP, h], start=False, stop=False, skip_group_check=True)
                            m.then_inc(s(f"hot_used{h}"), 1)
                    for b in range(2):
                        m = mm(psum[0:NP, 2 * u + b, 0:1], zero_b[0:NP, 0:NP], zero_b[0:NP, 0:1], start=False, stop=True, skip_group_check=True)
                    m.then_inc(s("win_done"), 1)
            pe.wait_ge(s("win_counts"), NW)
            for c, (n0, n1) in enumerate(NCH):
                for t in range(NT):
                    m = mm(psum[:, 4 + c, 0:n1 - n0], ones[0:NP], adj_v[0:NP, t, n0:n1], start=(t == 0), stop=(t == NT - 1))
                m.then_inc(s("deg"), 1)
            pe.wait_ge(s("xcols_in"), 16)
            pe.wait_ge(s("w1_in"), 16)
            pe.wait_ge(s("win_read"), NW + 2)
            pe.wait_ge(s("deg1"), 3)
            for t in range(NT):
                m = mm(psum[0:NP, 7, t:t + 1], inv_row[0:1, t * NP:(t + 1) * NP], ones[0:1, 0:1], start=True, stop=True, skip_group_check=True)
            m.then_inc(s("deg1_turn"), 1)

            def inv_everywhere(h1_tile):
                if h1_tile == 2:
                    pe.wait_ge(s("inv_col_ready"), 1)
                    for t in range(NT):
                        m = mm(psum[:, 4 + t // 4, (t % 4) * NP:(t % 4 + 1) * NP], inv_col[0:NP, t:t + 1].to_broadcast([NP, P]), ident[0:NP, 0:NP],
                               start=True, stop=True, skip_group_check=True)
                    m.then_inc(s("inv_rows"), 1)

            rows_product("h1", 0, r1, wslot(0), before=inv_everywhere)
            pe.wait_ge(s("h1_stored"), NT)
            pe.wait_ge(s("norm"), NT)
            agg_cols("conv1", 4, hn, adj_v)
            for d in range(NT):
                for q in range(3):
                    n = 3 * d + q
                    if n >= 4:
                        pe.wait_ge(s("tr_stored"), n - 3)
                    for t in range(4 * q, min(4 * q + 4, NT)):
                        m = nc.tensor.transpose(psum[0:NP, n % 4, (t - 4 * q) * NP:(t - 4 * q + 1) * NP], adj_v[0:NP, t, d * NP:(d + 1) * NP], ident[0:NP, 0:NP])
                    m.then_inc(s("tr_done"), 1)
            pe.wait_ge(s("conv1_stored"), 12)
            pe.wait_ge(s("w2_in"), 16)
            rows_product("h2", 4, r2, wslot(1))
            pe.wait_ge(s("h2_stored"), NT)
            pe.wait_ge(s("tr_stored"), 3 * NT)
            agg_cols("conv2", 0, hn, adj_v)
            pe.wait_ge(s("conv2_stored"), 12)
            i = 0
            for g in range(3):
                pe.wait_ge(s(f"wih_in{g}"), 16)
                for j in range(KT):
                    for n0, n1 in NCH:
                        o = out_rows(i, 4, None, "pre_stored")
                        for k in range(KT):
                            m = mm(o[:, 0:n1 - n0], wslot(g % 2)[:, k, j * P:(j + 1) * P], r1[:, k, n0:n1], start=(k == 0), stop=(k == KT - 1))
                        m.then_inc(s("pre_done"), 1)
                        i += 1
            pe.wait_ge(s("gru_init"), 1)
            pe.wait_ge(s("whh_split"), 3)

            every = ((0, 0), (0, 1), (1, 0), (1, 1))

            def gru_gate(u, c, kc, g, pieces=every):
                for j, k in pieces:
                    at = (4 if g == 2 else 3) * j
                    for part in range(2):
                        m = mm(psum[:, 4 * c + g, at:at + 2], whh16[g][:, part, 2 * kc + k, (2 * c + j) * P:(2 * c + j + 1) * P],
                               h16[:, u, kc, k], start=(kc == 0 and j == 0 and k == 0 and part == 0),
                               stop=(kc == 1 and k == 1 and part == 1), skip_group_check=True)
                return m

            with pe.Fori(0, N // 2) as i:
                for u in range(2):
                    t = 2 * i + u
                    pe.wait_ge(s("gru_state0"), t + 1)
                    pe.wait_ge(s("gru_put0"), t + 1)
                    for g in (0, 2, 1):
                        gru_gate(u, 0, 0, g)
                    pe.wait_ge(s("gru_put1"), t + 1)
                    gru_gate(u, 1, 0, 0)
                    gru_gate(u, 1, 0, 2, every[:1])
                    pe.wait_ge(s("gru_state1"), t + 1)
                    gru_gate(u, 0, 1, 0).then_inc(s("gru_r_mm0"), 1)
                    gru_gate(u, 0, 1, 2).then_inc(s("gru_n_mm0"), 1)
                    gru_gate(u, 0, 1, 1).then_inc(s("gru_z_mm0"), 1)
                    gru_gate(u, 1, 1, 0).then_inc(s("gru_r_mm1"), 1)
                    gru_gate(u, 1, 0, 2, every[1:])
                    gru_gate(u, 1, 1, 2).then_inc(s("gru_n_mm1"), 1)
                    gru_gate(u, 1, 0, 1)
                    gru_gate(u, 1, 1, 1).then_inc(s("gru_z_mm1"), 1)
            for c in range(2):
                pe.wait_ge(s(f"gru_kept{c}"), N + 2)
                pe.wait_ge(s(f"gru_put{c}"), N + 1)
            pe.wait_ge(s("wfc_in"), 16)
            rows_product("fc", 4, r1, w_fc, before=lambda t: turn("fc", t - 3, 0) if t >= 3 else None)
            for t in range(NT - 3, NT):
                turn("fc", t, 0)
            pe.wait_ge(s("fc_turned"), NT)
            pe.wait_ge(s("l1w1_in"), 16)
            rows_product("l1h1", 4, r2, wslot(0))
            pe.wait_ge(s("l1h1_stored"), NT)
            pe.wait_ge(s("adj_in"), 16)
            agg_cols("l1agg", 0, hn, adj_v)
            pe.wait_ge(s("l1norm"), KT)
            pe.wait_ge(s("l1w2_in"), 16)
            rows_product("l1h2", 4, r1, wslot(1))
            pe.wait_ge(s("l1h2_stored"), NT)
            for d in range(NT):
                if d >= 3:
                    turn("l1out", d - 3, 4)
                o = out_rows(d, 0, None, "l1out_stored")
                for t in range(NT):
                    m = mm(o[0:NP], adj_v[0:NP, t, d * NP:(d + 1) * NP], hn[0:NP, t], start=(t == 0), stop=(t == NT - 1))
                m.then_inc(s("l1out_done"), 1)
            for t in range(NT - 3, NT):
                turn("l1out", t, 4)
            pe.wait_ge(s("l1out_turned"), NT)
            for t in range(NT):
                for k in range(KT):
                    m = mm(psum[0:NP, 0, t * NE:(t + 1) * NE], r1[:, k, t * NP:(t + 1) * NP], gate_w[:, k], start=(k == 0), stop=(k == KT - 1), skip_group_check=True)
            m.then_inc(s("logits"), 1)

            def mm_parts(o, a, b, start, stop):
                for i, (pa, pb) in enumerate(((0, 0), (0, 1), (1, 0))):
                    m = mm(o, a(pa), b(pb), start=start and i == 0, stop=stop and i == 2)
                return m

            pe.wait_ge(s("cnt_ready"), NT)
            pe.wait_ge(s("x_split"), NT)
            lo_runs = pe.value_load(has_lo[0:1, 0:1], min_val=0, max_val=1)

            def mm_counts(o, counts_left, counts, rows, start):
                def tile(t, c, start, stop):
                    for a in range(2):
                        left, right = (counts(t, c), rows(t, a)) if counts_left else (rows(t, a), counts(t, c))
                        m = mm(o, left, right, start=start and a == 0, stop=stop and a == 1)
                    return m

                for t in range(NT - 1):
                    tile(t, 0, start and t == 0, False)
                with pe.If(lo_runs):
                    for t in range(NT):
                        tile(t, 1, False, False)
                return tile(NT - 1, 0, False, True)

            i = 0
            for f in range(KT):
                for n0, n1 in NCH:
                    o = out_rows(i, 4, None, "aggx_stored")
                    m = mm_counts(o[:, 0:n1 - n0], False, lambda t, c: cnt16[0:NP, t, c, n0:n1], lambda t, a: rows16[0:NP, t, a, f * P:(f + 1) * P], True)
                    m.then_inc(s("aggx_done"), 1)
                    i += 1
            pe.wait_ge(s("aggx_stored"), 12)
            pe.wait_ge(s("x_split"), NT + KT + 1)
            pe.wait_ge(s("gates_read"), 1)
            with pe.Fori(0, NE // 2) as ei:
                for u in range(2):
                    e = 2 * ei + u
                    b0, b1 = (0, 4) if u == 0 else (4, 0)
                    pe.wait_ge(s("ew0_split"), e + 1)
                    i = 0
                    for f in range(KT):
                        for n0, n1 in NCH:
                            o = out_rows(i, b0, None, "layer1_stored", e * 12)[:, 0:n1 - n0]
                            for k in range(KT):
                                mm_parts(o, lambda a: l2w16[0][:, a, k, f * P:(f + 1) * P], lambda a: agg_x[k][:, a, n0:n1], k == 0, False)
                                m = mm_parts(o, lambda a: l2w16[1][:, a, k, f * P:(f + 1) * P], lambda a: r2_16[:, a, k, n0:n1], False, k == KT - 1)
                            m.then_inc(s("layer1_done"), 1)
                            i += 1
                    pe.wait_ge(s("layer1_split"), e * 12 + 12)
                    pe.wait_ge(s("ew1_split"), e + 1)
                    pe.wait_ge(s("eout_stored"), e * NT)
                    for t in range(NT):
                        o = out_rows(t, b1, None, "u_stored", e * NT)
                        for k in range(KT):
                            m = mm_parts(o[0:NP], lambda a: r1_16[:, a, k, t * NP:(t + 1) * NP], lambda a: l2w16[2][:, a, k], k == 0, k == KT - 1)
                        m.then_inc(s("u_done"), 1)
                    for d in range(NT):
                        if d >= 2:
                            pe.wait_ge(s("eout_stored"), e * NT + d - 1)
                        b = b0 + 2 * (d % 2)
                        for k in range(KT):
                            mm_parts(psum[0:NP, b], lambda a: r1_16[:, a, k, d * NP:(d + 1) * NP], lambda a: l2w16[3][:, a, k], k == 0, k == KT - 1)
                        if d == 0:
                            pe.wait_ge(s("u_stored"), e * NT + NT)
                        m = mm_counts(psum[0:NP, b + 1], True, lambda t, c: cnt16[0:NP, t, c, d * NP:(d + 1) * NP], lambda t, a: rows16[0:NP, t, a], True)
                        m.then_inc(s("eout_done"), 1)
            for t in range(NT):
                turn("l2", t, 0)
            pe.wait_ge(s("l2_turned"), NT)
            pe.wait_ge(s("l3w_in"), 16)
            rows_product("z", 4, r2, wslot(0))
            pe.wait_ge(s("z_stored"), NT)
            pe.wait_ge(s("wt_in"), 16)
            for d in range(NT):
                o = out_rows(d, 0, None, "l3_stored")
                for t in range(NT):
                    m = mm(o[0:NP], adj_v[0:NP, t, d * NP:(d + 1) * NP], hn[0:NP, t], start=(t == 0), stop=(t == NT - 1))
                m.then_inc(s("l3_done"), 1)

        @block.scalar
        def _(act):
            def take_cols(name, bank0, dst, func, bias=None, base=0, bias_at=None):
                i = 0
                for f in range(KT):
                    for n0, n1 in NCH:
                        act.wait_ge(s(f"{name}_done"), base + i + 1)
                        o = psum[:, bank0 + i % 4, 0:n1 - n0]
                        to = dst[f][:, n0:n1] if isinstance(dst, list) else dst[:, f, n0:n1]
                        if func is None:
                            m = nc.scalar.copy(to, o)
                        else:
                            m = nc.scalar.activation(to, o, func, bias=bias[:, f:f + 1])
                        m.then_inc(s(f"{name}_stored"), 1)
                        i += 1

            def take_rows(name, bank0, base=0):
                for t in range(NT):
                    act.wait_ge(s(f"{name}_done"), base + t + 1)
                    nc.scalar.copy(hn[0:NP, t], psum[0:NP, bank0 + t % 4]).then_inc(s(f"{name}_stored"), 1)

            def take_turned(name, bank0, to=r2):
                for t in range(NT):
                    act.wait_ge(s(f"{name}_turn"), t + 1)
                    nc.scalar.copy(to[:, :, t * NP:(t + 1) * NP], psum[:, bank0 + t % 4, 0:4 * NP].rearrange("p (k n) -> p k n", k=KT)).then_inc(s(f"{name}_turned"), 1)

            act.wait_ge(s("const"), 9)
            nc.scalar.copy(warm[:], ident[:, 0:1]).then_inc(s("warm"), 1)
            act.sem_inc(s("win_read"), 2)
            with act.Fori(0, NW // 2) as i:
                for u in range(2):
                    w = 2 * i + u
                    acc = psum[0:NP, 2 * u:2 * u + 2, 0:500].rearrange("p b (t c) -> p b t c", c=100)
                    act.wait_ge(s("win_done"), w + 1)
                    nc.scalar.copy(adj_v[0:NP, :, bass.ds(w * WD, WD)].rearrange("p (b t) c -> p b t c", b=2), acc[:, :, :, 0:WD]).then_inc(s("win_counts"), 1)
                    act.wait_ge(s("win_weights"), w + 1)
                    nc.scalar.copy(cparts[u][0:NP].rearrange("p (b t) c -> p b t c", b=2), acc[:, :, :, WD:4 * WD]).then_inc(s("parts_ready"), 1)
                    act.wait_ge(s("parts_ready"), w + 1)
                    act.sem_inc(s("win_read"), 1)
            act.wait_ge(s("win_weights"), NW + 2)
            take_rows("h1", 0)
            act.wait_ge(s("small_in"), 48)
            act.wait_ge(s("fc_bias_used"), 1)
            take_cols("conv1", 4, r2, ACT.Relu, b1c)
            take_rows("h2", 4)
            take_cols("conv2", 0, r1, ACT.Relu, b2c)
            act.wait_ge(s("gru_init"), 1)
            nc.scalar.activation(warm[:], scl[:, 1:2], ACT.Sigmoid).then_inc(s("warm"), 1)

            def put(t, c, g):
                columns = psum[:, 4 * c + 2, 3:8:4] if g == 2 else psum[:, 4 * c + g, 2:6:3]
                return nc.scalar.copy(columns, big[:, bass.ds(t * 12 + c * 6 + 2 * g, 2)])

            for c in range(2):
                for g in range(2):
                    put(0, c, g)
                put(0, c, 2).then_inc(s(f"gru_put{c}"), 1)
            with act.Fori(0, N // 2) as i:
                for u in range(2):
                    t = 2 * i + u

                    def gate_r(c):
                        act.wait_ge(s(f"gru_r_sum{c}"), t + 1)
                        nc.scalar.activation(mul_n[:, c, 3:8:4], sum_rz[:, c, 0, 2:6:3], ACT.Sigmoid).then_inc(s(f"gru_r{c}"), 1)

                    def gate_z(c):
                        act.wait_ge(s(f"gru_z_sum{c}"), t + 1)
                        nc.scalar.activation(upd_mul[:, c, 2:14:7], sum_rz[:, c, 1, 2:6:3], ACT.Sigmoid).then_inc(s(f"gru_z{c}"), 1)

                    def gate_n(c):
                        act.wait_ge(s(f"gru_n_sum{c}"), t + 1)
                        nc.scalar.activation(upd_add[:, c, 0:14:7], sum_n[:, c, 3:8:4], ACT.Tanh).then_inc(s(f"gru_n{c}"), 1)

                    gate_r(0)
                    put(t + 1, 0, 0)
                    gate_z(0)
                    gate_n(0)
                    gate_r(1)
                    put(t + 1, 0, 1)
                    put(t + 1, 0, 2).then_inc(s("gru_put0"), 1)
                    put(t + 1, 1, 0)
                    gate_n(1)
                    put(t + 1, 1, 2)
                    gate_z(1)
                    put(t + 1, 1, 1).then_inc(s("gru_put1"), 1)
            take_turned("fc", 0)
            take_cols("l1agg", 0, r1, None)
            for f in range(KT):
                act.wait_ge(s("bn_ready"), f + 1)
                nc.scalar.activation(r1[:, f], r1[:, f], ACT.Relu, scale=bnc[:, 0, f:f + 1], bias=bnc[:, 1, f:f + 1]).then_inc(s("l1norm"), 1)
            take_turned("l1out", 4, r1)
            act.wait_ge(s("l1out_done"), NT)
            for t in range(NT):
                act.wait_ge(s("l1out_ln"), t + 1)
                nc.scalar.activation(rows16[0:NP, t, 0], xr[0:NP, t], ACT.Copy, scale=XS).then_inc(s("x_hi"), 1)
            act.wait_ge(s("l1out_turned"), NT)
            for k in range(KT):
                nc.scalar.activation(r2_16[:, 0, k], r1[:, k], ACT.Copy, scale=XS).then_inc(s("x_hi"), 1)
            act.wait_ge(s("gate_in"), 1)
            nc.scalar.activation(gates[0:NP], gates[0:NP], ACT.Exp).then_inc(s("gate_exp"), 1)
            i = 0
            for f in range(KT):
                for n0, n1 in NCH:
                    act.wait_ge(s("aggx_stored"), i + 1)
                    nc.scalar.copy(agg_x[f][:, 0, n0:n1], layer1_f32[i % 2][:, 0:n1 - n0]).then_inc(s("part_hi"), 1)
                    i += 1
            act.wait_ge(s("x_split"), NT + KT)
            with act.Fori(0, NE // 2) as ei:
                for u in range(2):
                    e = 2 * ei + u
                    b0, b1 = (0, 4) if u == 0 else (4, 0)
                    act.wait_ge(s("ew0_split"), e + 1)
                    nc.scalar.copy(ebias[:], blc[:, bass.ds(e * KT, KT)]).then_inc(s("ebias"), 1)
                    act.wait_ge(s("ebias"), 2 * e + 1)
                    nc.scalar.activation(ebias[:], ebias[:], ACT.Copy, scale=esc[:, 1:2]).then_inc(s("ebias"), 1)
                    act.wait_ge(s("ebias"), 2 * e + 2)
                    act.wait_ge(s("eadd"), e * NT)
                    i = 0
                    for f in range(KT):
                        for n0, n1 in NCH:
                            act.wait_ge(s("layer1_done"), e * 12 + i + 1)
                            if i >= 2:
                                act.wait_ge(s("layer1_split"), e * 12 + i - 1)
                            for to in (layer1_f32[i % 2][:, 0:n1 - n0], r1_16[:, 0, f, n0:n1]):
                                m = nc.scalar.activation(to, psum[:, b0 + i % 4, 0:n1 - n0], ACT.Relu, scale=esc[:, 3:4], bias=ebias[:, f:f + 1])
                            m.then_inc(s("layer1_stored"), 1)
                            i += 1
                    for t in range(NT):
                        act.wait_ge(s("u_done"), e * NT + t + 1)
                        nc.scalar.activation(rows16[0:NP, t, 0], psum[0:NP, b1 + t % 4], ACT.Copy, scale=US).then_inc(s("part_hi"), 1)
                    for t in range(NT):
                        act.wait_ge(s("eout_done"), e * NT + t + 1)
                        if t >= 2:
                            act.wait_ge(s("eadd"), e * NT + t - 1)
                        nc.scalar.activation(l2_tmp[t % 2], psum[0:NP, b0 + 2 * (t % 2) + 1], ACT.Copy, scale=agg_scale[0:NP, t:t + 1]).then_inc(s("part_hi"), 1)
            take_turned("l2", 0)
            take_rows("z", 4)

        @block.vector
        def _(dve):
            v = nc.vector
            linked, roots = [0], [0]

            def link(ins):
                linked[0] += 1
                ins.then_inc(s("dve_link"), 1)
                dve.wait_ge(s("dve_link"), linked[0])

            def ln_rows(t, name):
                x = xr[0:NP, t]
                link(v.bn_stats(stat[0:NP, 0], x))
                link(v.bn_aggr(mv[0:NP, 0:2], stat[0:NP, 0]))
                roots[0] += 1
                v.tensor_scalar(mv[0:NP, 2:3], mv[0:NP, 1:2], LN_EPS, None, ALU.add).then_inc(s("var"), 1)
                dve.wait_ge(s("root"), roots[0])
                v.tensor_scalar(x, x, mv[0:NP, 0:1], mv[0:NP, 2:3], ALU.subtract, ALU.mult).then_inc(s(name), 1)

            dve.wait_ge(s("edges_in"), 48)
            link(v.tensor_copy(e_stage[0:EH, 0:2], e_int[0:EH]))
            dve.sem_inc(s("edges_f"), 1)
            pair_dst = e_stage[0:EH, 1].rearrange("p h e -> p (h e)")
            link(v.tensor_reduce(p_lim[:, 0:1], pair_dst, AX.X, ALU.min))
            link(v.tensor_reduce(p_lim[:, 1:2], pair_dst, AX.X, ALU.max))
            dve.sem_inc(s("limits"), 1)
            dve.wait_ge(s("edges_turn"), 1)
            link(v.tensor_copy(e_col[0:EP], psum[0:EP, 0:3, 0:ET]))
            link(v.memset(w_part[0:EP, :, 0], 1.0))
            rest = e_w
            for a in range(3):
                link(v.tensor_copy(w_bf[0:EP], rest[0:EP]))
                link(v.tensor_copy(w_part[0:EP, :, a + 1], w_bf[0:EP]))
                if a < 2:
                    link(v.tensor_tensor(w_res[0:EP, a], rest[0:EP], w_bf[0:EP], ALU.subtract))
                    rest = w_res[:, a]
            dve.wait_ge(s("const"), 9)
            dve.wait_ge(s("limits_all"), 1)
            link(v.tensor_scalar(hit[0:NW], psum[0:NW, 3, 0:EH], w_lim[0:NW, 1:2], None, ALU.is_lt))
            link(v.scalar_tensor_tensor(out=hit_b[0:NW], in0=psum[0:NW, 3, EH:2 * EH], scalar=w_lim[0:NW, 0:1], in1=hit[0:NW], op0=ALU.is_ge, op1=ALU.mult))
            for a in range(2):
                link(v.tensor_tensor(hit[0:NW], hit_b[0:NW], pair_no[0:NW, a], ALU.mult))
                link(v.tensor_reduce(span[0:NW, a:a + 1], hit[0:NW], AX.X, ALU.max))
            dve.sem_inc(s("span"), 1)
            dve.wait_ge(s("span_row"), 1)
            last, first, count, total, before = (row[:, a] for a in range(5))
            link(v.tensor_scalar(first, psum[0:1, 4, NW:2 * NW], -1.0, float(EH), ALU.mult, ALU.add))
            link(v.tensor_scalar(first, first, float(EH - 1), None, ALU.min))
            link(v.tensor_copy(last, psum[0:1, 4, 0:NW]))
            link(v.scalar_tensor_tensor(out=last, in0=first, scalar=1.0, in1=last, op0=ALU.add, op1=ALU.max))
            link(v.tensor_tensor(count, last, first, ALU.subtract))
            link(v.tensor_tensor_scan(total, ones[0:1, 0:NW], count, 0.0, ALU.mult, ALU.add))
            link(v.tensor_tensor(before, total, count, ALU.subtract))
            offset = row[:, 5]
            link(v.tensor_scalar(before, before, float(EH), None, ALU.add))
            link(v.tensor_tensor(offset, before, first, ALU.subtract))
            link(v.scalar_tensor_tensor(out=offset, in0=offset, scalar=float(EH), in1=last, op0=ALU.mult, op1=ALU.add))
            link(v.tensor_scalar(offset, offset, -1.0, None, ALU.add))
            for a, val in enumerate((first, count, before, offset)):
                link(v.tensor_copy(bounds[:, a], val))
            dve.sem_inc(s("bounds"), 1)
            for h in range(2):
                dve.sem_inc(s(f"hot_used{h}"), EH + 1)
                dve.sem_inc(s(f"hot_ready{h}"), EH)
            with dve.Fori(0, NW) as w:
                first = dve.value_load(bounds[0:1, 0, bass.ds(w, 1)], min_val=0, max_val=EH - 1)
                packed = dve.value_load(bounds[0:1, 3, bass.ds(w, 1)], min_val=0, max_val=EH * EH * (NW + 2))
                end, offset = dve.snap(packed % EH + 1), dve.snap(packed // EH)
                with dve.Fori(first, end) as pair:
                    for h in range(2):
                        column = pair + h * EH
                        dve.wait_ge(s(f"hot_used{h}"), offset + pair + 1)
                        v.tensor_scalar(src_hot[0:EP, h], iota16[0:EP], e_src[0:EP, bass.ds(column, 1)], None, ALU.is_equal)
                        v.scalar_tensor_tensor(
                            out=dst_hot[0:EP, h].rearrange("p (a c) -> p a c", a=4),
                            in0=iota16[0:EP, bass.ds(w * WD, WD)].unsqueeze(1).broadcast_to([EP, 4, WD]), scalar=e_dst[0:EP, bass.ds(column, 1)],
                            in1=w_part[0:EP, bass.ds(column, 1), :].rearrange("p t a -> p (t a)").unsqueeze(2).broadcast_to([EP, 4, WD]),
                            op0=ALU.is_equal, op1=ALU.mult).then_inc(s(f"hot_ready{h}"), 1)
            dve.wait_ge(s("x_in"), 16)
            dve.wait_ge(s("bfc_in"), 16)
            link(v.tensor_tensor(xr[0:NP], xr[0:NP], fc_bias[0:NP].unsqueeze(1).broadcast_to([NP, NT, D]), ALU.add))
            dve.sem_inc(s("fc_bias_used"), 1)
            for c, (n0, n1) in enumerate(NCH):
                dve.wait_ge(s("deg"), c + 1)
                v.tensor_scalar(inv_row[:, n0:n1], psum[:, 4 + c, 0:n1 - n0], 1.0, None, ALU.add).then_inc(s("deg1"), 1)
                link(v.tensor_scalar(invdeg_row[:, n0:n1], psum[:, 4 + c, 0:n1 - n0], 1.0, None, ALU.max))
            dve.wait_ge(s("deg1_turn"), 1)
            link(v.tensor_scalar(invdeg_col[0:NP], psum[0:NP, 7, 0:NT], -1.0, 1.0, ALU.add, ALU.max))
            v.tensor_copy(inv_col[0:NP], psum[0:NP, 7, 0:NT]).then_inc(s("deg1_col"), 1)
            link(v.reciprocal(invdeg_row, invdeg_row))
            link(v.reciprocal(invdeg_col[0:NP], invdeg_col[0:NP]))
            dve.sem_inc(s("invdeg_ready"), 1)
            dve.wait_ge(s("inv_rows"), 1)
            for b in range(3):
                n0, n1 = 4 * NP * b, min(4 * NP * (b + 1), N)
                link(v.tensor_copy(inv_row[:, n0:n1], psum[:, 4 + b, 0:n1 - n0]))
            for t in range(NT):
                dve.wait_ge(s(f"cnt_out{t // 5}"), 16)
                diag = adj_v[0:NP, t, t * NP:(t + 1) * NP]
                link(v.tensor_tensor(diag, diag, ident[0:NP, 0:NP], ALU.add))
                v.scalar_tensor_tensor(out=adj_v[0:NP, t], in0=adj_v[0:NP, t], scalar=inv_col[0:NP, t:t + 1], in1=inv_row[0:NP],
                                       op0=ALU.mult, op1=ALU.mult).then_inc(s("norm"), 1)
            dve.wait_ge(s("wt_out"), 16)
            for d in range(NT):
                for q in range(3):
                    n = 3 * d + q
                    dve.wait_ge(s("tr_done"), n + 1)
                    width = min(4, NT - 4 * q) * NP
                    v.tensor_copy(wt_v[0:NP, d, 4 * q * NP:4 * q * NP + width], psum[0:NP, n % 4, 0:width]).then_inc(s("tr_stored"), 1)
            dve.wait_ge(s("whh_in"), 48)
            for g, place in enumerate((whh[0], whh[1], ws[:, WSLOT:2 * WSLOT])):
                link(v.tensor_reduce(wmax[:, 2 * g:2 * g + 1], place, AX.X, ALU.max))
                link(v.tensor_reduce(wmax[:, 2 * g + 1:2 * g + 2], place, AX.X, ALU.min))
            link(v.tensor_scalar(wmax[:, 8:11], wmax[:, 1:6:2], -1.0, None, ALU.mult))
            link(v.tensor_tensor(wmax[:, 8:11], wmax[:, 8:11], wmax[:, 0:6:2], ALU.max))
            link(v.tensor_reduce(wmax[:, 6:7], wmax[:, 8:11], AX.X, ALU.max))
            dve.sem_inc(s("top_part"), 1)
            dve.wait_ge(s("top_all"), 1)
            link(v.tensor_scalar(wmax[:, 7:8], wmax[:, 7:8], 2.0 ** -60, None, ALU.max))
            bits = wmax[:, 7:8].bitcast(I32)
            link(v.tensor_scalar(bits, bits, 0x7F800000, None, ALU.bitwise_and))
            one = float(1 << 23)
            scl_i, scw_i = scl[:].bitcast(I32), scw[:].bitcast(I32)
            link(v.tensor_scalar(scw_i[:, 0:1], bits, -1.0, (13 + 2 * 127) * one, ALU.mult, ALU.add))
            link(v.tensor_scalar(scl_i[:, 0:1], scw_i[:, 0:1], 12 * one, None, ALU.add))
            link(v.tensor_scalar(scl_i[:, 1:2], scl_i[:, 0:1], -1.0, 2 * 127 * one, ALU.mult, ALU.add))
            link(v.tensor_scalar(scw[:, 1:2], scw[:, 0:1], -1.0, None, ALU.mult))

            def split(g, source):
                flat = whh[g].bitcast(F16)
                hi, lo = flat[:, 0:WSLOT], flat[:, WSLOT:2 * WSLOT]
                sc = scw[:, 1:2] if g == 1 else scw[:, 0:1]
                link(v.tensor_scalar(hi, source, sc, None, ALU.mult))
                link(v.scalar_tensor_tensor(out=lo, in0=source, scalar=sc, in1=hi, op0=ALU.mult, op1=ALU.subtract))
                dve.sem_inc(s("whh_split"), 1)

            dve.wait_ge(s("h1_done"), NT)
            for g in range(2):
                link(v.tensor_copy(ws[:, 0:WSLOT], whh[g]))
                split(g, ws[:, 0:WSLOT])
            dve.wait_ge(s("conv2_done"), 12)
            split(2, ws[:, WSLOT:2 * WSLOT])
            link(v.tensor_tensor(pbias[:, 0:8], bihc[:, 0:8], bhhc[:, 0:8], ALU.add))
            link(v.tensor_copy(pbias[:, 8:12], bihc[:, 8:12]))
            link(v.tensor_scalar(pbias[:, 4:8], pbias[:, 4:8], -1.0, None, ALU.mult))
            dve.wait_ge(s("adj_out"), 16)
            dve.wait_ge(s("invdeg_out"), 16)
            i = 0
            for g in range(3):
                for j in range(KT):
                    for n0, n1 in NCH:
                        dve.wait_ge(s("pre_done"), i + 1)
                        q = (j // 2) * 6 + g * 2 + j % 2
                        v.tensor_scalar(pi_v[:, n0:n1, q], psum[:, 4 + i % 4, 0:n1 - n0], -1.0 if g == 1 else 1.0,
                                        pbias[:, 4 * g + j:4 * g + j + 1], ALU.mult, ALU.add).then_inc(s("pre_stored"), 1)
                        i += 1
            dve.wait_ge(s("pre_stored"), 36)
            link(v.memset(h16[:], 0.0))
            link(v.memset(mul_rz[:], 1.0))
            link(v.memset(mul_rz[:, 0:6:3], 0.0))
            link(v.tensor_copy(mul_rz[:, 2:6:3], scl[:, 1:2].to_broadcast([P, 2])))
            link(v.memset(mul_n[:], 1.0))
            link(v.memset(mul_n[:, :, 0:8:4], 0.0))
            for c in range(2):
                link(v.tensor_copy(mul_n[:, c, 2:8:4], scl[:, 1:2].to_broadcast([P, 2])))
            link(v.memset(upd_mul[:], 1.0))
            link(v.memset(upd_mul[:, :, 0:14:7], 0.0))
            link(v.memset(upd_mul[:, :, 3:14:7], HS))
            link(v.memset(upd_mul[:, :, 6:14:7], 0.0))
            link(v.memset(upd_add[:], 0.0))
            link(v.memset(upd_add[:, :, 4:14:7], ROUND))
            link(v.memset(upd_add[:, :, 5:14:7], -ROUND))
            link(v.memset(signs[:], 1.0))
            link(v.memset(signs[:, 0:4:2], -1.0))
            for c in range(2):
                link(v.memset(psum[:, 4 * c:4 * c + 3, 0:8], 0.0))
                link(v.tensor_copy(psum[:, 4 * c + 2, 2:8:4], bhhc[:, 8 + 2 * c:10 + 2 * c]))
            dve.sem_inc(s("gru_init"), 1)
            for c in range(2):
                dve.sem_inc(s(f"gru_state{c}"), 1)
                dve.sem_inc(s(f"gru_fresh{c}"), 1)
            signs_v = signs[:].rearrange("p (j a) -> p j a", a=2)

            def sevens(ap):
                return ap.rearrange("p (j a) -> p j a", a=7)

            def scan_rz(t, c, g):
                dve.wait_ge(s(f"gru_{'rz'[g]}_mm{c}"), t + 1)
                v.tensor_tensor_scan(sum_rz[:, c, g], mul_rz[:], psum[:, 4 * c + g, 0:6], 0.0, ALU.mult, ALU.add).then_inc(s(f"gru_{'rz'[g]}_sum{c}"), 1)

            def scan_n(t, c):
                dve.wait_ge(s(f"gru_n_mm{c}"), t + 1)
                dve.wait_ge(s(f"gru_r{c}"), t + 1)
                v.tensor_tensor_scan(sum_n[:, c], mul_n[:, c], psum[:, 4 * c + 2, 0:8], 0.0, ALU.mult, ALU.add).then_inc(s(f"gru_n_sum{c}"), 1)

            def update(t, u, c):
                dve.wait_ge(s(f"gru_kept{c}"), t + 1)
                dve.wait_ge(s(f"gru_fresh{c}"), t + 1)
                for gate in "zn" if c == 0 else "nz":
                    dve.wait_ge(s(f"gru_{gate}{c}"), t + 1)
                v.tensor_tensor_scan(upd[:, 1 - u, c], upd_mul[:, c], upd_add[:, c], 0.0, ALU.mult, ALU.add).then_inc(s(f"gru_upd{c}"), 1)

            def parts(t, u, c):
                dve.wait_ge(s(f"gru_upd{c}"), t + 1)
                new = sevens(upd[:, 1 - u, c])
                v.tensor_tensor(h16[:, 1 - u, c], new[:, :, 3:6:2], new[:, :, 5:7], ALU.subtract).then_inc(s(f"gru_state{c}"), 1)
                v.tensor_tensor(sevens(upd_add[:, c])[:, :, 1:3], new[:, :, 2:3].broadcast_to([P, 2, 2]), signs_v, ALU.mult).then_inc(s(f"gru_fresh{c}"), 1)

            with dve.Fori(0, N // 2) as i:
                for u in range(2):
                    t = 2 * i + u
                    scan_rz(t, 0, 0)
                    scan_rz(t, 0, 1)
                    scan_n(t, 0)
                    scan_rz(t, 1, 0)
                    update(t, u, 0)
                    scan_n(t, 1)
                    parts(t, u, 0)
                    scan_rz(t, 1, 1)
                    update(t, u, 1)
                    parts(t, u, 1)
            for t in range(NT):
                dve.wait_ge(s("fc_done"), t + 1)
                v.tensor_tensor(xr[0:NP, t], psum[0:NP, 4 + t % 4], xr[0:NP, t], ALU.add).then_inc(s("fc_stored"), 1)
                dve.wait_ge(s("fc_stored"), t + 1)
                ln_rows(t, "fc_ln")
            dve.wait_ge(s("l1b1_in"), 16)
            for t in range(NT):
                dve.wait_ge(s("l1h1_done"), t + 1)
                v.tensor_tensor(hn[0:NP, t], psum[0:NP, 4 + t % 4], l1_bias[0:NP], ALU.add).then_inc(s("l1h1_stored"), 1)
            dve.wait_ge(s("cnt_in"), 16)
            dve.wait_ge(s("invdeg_in"), 16)
            for t in range(NT):
                link(v.tensor_reduce(cnt_max[0:NP, t:t + 1], wt_v[0:NP, t], AX.X, ALU.max))
                link(v.tensor_copy(cnt_f32, wt_v[0:NP, t]))
                link(v.tensor_copy(cnt16[0:NP, t, 0], cnt_f32))
                v.tensor_tensor(cnt16[0:NP, t, 1], cnt_f32, cnt16[0:NP, t, 0], ALU.subtract).then_inc(s("cnt_ready"), 1)
                dve.wait_ge(s("cnt_ready"), t + 1)
            link(v.memset(cnt_top[:, 0:1], 0.0))
            v.tensor_reduce(cnt_top[0:NP, 0:1], cnt_max[0:NP], AX.X, ALU.max).then_inc(s("top_part"), 1)
            for f in range(KT):
                for c, (n0, n1) in enumerate(NCH):
                    dve.wait_ge(s("l1agg_stored"), 3 * f + c + 1)
                    link(v.bn_stats(stat[:, c], r1[:, f, n0:n1]))
                link(v.bn_aggr(mv[:, 0:2], stat[:].rearrange("p a b -> p (a b)")))
                roots[0] += 1
                v.tensor_scalar(mv[:, 2:3], mv[:, 1:2], 1e-5, None, ALU.add).then_inc(s("var"), 1)
                dve.wait_ge(s("root"), roots[0])
                link(v.tensor_tensor(bnc[:, 0, f:f + 1], mv[:, 2:3], gamc[:, f:f + 1], ALU.mult))
                link(v.tensor_tensor(mv[:, 3:4], mv[:, 0:1], bnc[:, 0, f:f + 1], ALU.mult))
                link(v.tensor_tensor(bnc[:, 1, f:f + 1], betc[:, f:f + 1], mv[:, 3:4], ALU.subtract))
                dve.sem_inc(s("bn_ready"), 1)
            dve.wait_ge(s("l1b2_in"), 16)
            for t in range(NT):
                dve.wait_ge(s("l1h2_done"), t + 1)
                v.tensor_tensor(hn[0:NP, t], psum[0:NP, 4 + t % 4], l1_bias[0:NP], ALU.add).then_inc(s("l1h2_stored"), 1)
            for t in range(NT):
                dve.wait_ge(s("l1out_done"), t + 1)
                v.tensor_tensor(xr[0:NP, t], psum[0:NP, t % 4], xr[0:NP, t], ALU.add).then_inc(s("l1out_stored"), 1)
                dve.wait_ge(s("l1out_stored"), t + 1)
                ln_rows(t, "l1out_ln")
            dve.wait_ge(s("top_all"), 2)
            link(v.tensor_scalar(cnt_top[0:1, 1:2], cnt_top[0:1, 1:2], EXACT, None, ALU.is_gt))
            link(v.tensor_copy(has_lo[:], cnt_top[0:1, 1:2]))
            link(v.tensor_copy(invdeg_l2, invdeg_row))
            for t in range(NT):
                dve.wait_ge(s("x_hi"), t + 1)
                v.scalar_tensor_tensor(out=rows16[0:NP, t, 1], in0=xr[0:NP, t], scalar=XS, in1=rows16[0:NP, t, 0], op0=ALU.mult, op1=ALU.subtract).then_inc(s("x_split"), 1)

            expert, steps = [None], [0]

            def step(ins):
                if expert[0] is None:
                    link(ins)
                else:
                    steps[0] += 1
                    ins.then_inc(s("l2_link"), 1)
                    dve.wait_ge(s("l2_link"), expert[0] * L2_STEPS + steps[0])

            def power(to, of, shift):
                step(v.tensor_scalar(to.bitcast(I32), of.bitcast(I32), 0x7F800000, None, ALU.bitwise_and))
                step(v.tensor_scalar(to.bitcast(I32), to.bitcast(I32), -1.0, (shift + 2 * 127) * one, ALU.mult, ALU.add))

            def largest(layer, n_in, part):
                if part == 0:
                    dve.wait_ge(s(f"ew{layer}_in"), n_in)
                    step(v.tensor_reduce(top[:, 0:1], ws[:], AX.X, ALU.max))
                else:
                    step(v.tensor_reduce(top[:, 1:2], ws[:], AX.X, ALU.min))
                    step(v.tensor_scalar(top[:, 1:2], top[:, 1:2], -1.0, None, ALU.mult))
                    v.tensor_tensor(top[:, 2:3], top[:, 0:1], top[:, 1:2], ALU.max).then_inc(s("top_part"), 1)

            def scales(layer, n_all):
                dve.wait_ge(s("top_all"), n_all)
                step(v.tensor_scalar(top[:, 3:4], top[:, 3:4], 2.0 ** -60, None, ALU.max))
                if layer == 0:
                    step(v.tensor_scalar(top[:, 5:6], top[:, 3:4], 2.0 * D, top[:, 4:5], ALU.mult, ALU.add))
                    power(esc[:, 0:1], top[:, 3:4], 13)
                    power(esc[:, 1:2], top[:, 5:6], 10)
                    step(v.tensor_scalar(esc[:, 5:6].bitcast(I32), esc[:, 0:1].bitcast(I32), -1.0, 2 * 127 * one, ALU.mult, ALU.add))
                    step(v.scalar_tensor_tensor(out=esc[:, 3:4], in0=esc[:, 5:6], scalar=1.0 / XS, in1=esc[:, 1:2], op0=ALU.mult, op1=ALU.mult))
                else:
                    power(esc[:, 2:3], top[:, 3:4], 9)
                    for a, b in ((5, 1), (6, 2)):
                        step(v.tensor_scalar(esc[:, a:a + 1].bitcast(I32), esc[:, b:b + 1].bitcast(I32), -1.0, 2 * 127 * one, ALU.mult, ALU.add))
                    step(v.tensor_tensor(esc[:, 4:5], esc[:, 5:6], esc[:, 6:7], ALU.mult))
                    step(v.tensor_scalar(agg_scale[0:NP], invdeg_col[0:NP], esc[0:NP, 4:5], 1.0 / US, ALU.mult, ALU.mult))

            def split_weight(layer, m):
                to = l2w16[2 * layer + m]
                scale = esc[:, 2 * layer:2 * layer + 1]
                step(v.tensor_scalar(to[:, 0], wslot(m), scale, None, ALU.mult))
                last = v.scalar_tensor_tensor(out=to[:, 1], in0=wslot(m), scalar=scale, in1=to[:, 0], op0=ALU.mult, op1=ALU.subtract)
                if m == 1:
                    last.then_inc(s(f"ew{layer}_split"), 1)

            link(v.tensor_reduce(top[:, 0:1], blc, AX.X, ALU.max))
            link(v.tensor_reduce(top[:, 1:2], blc, AX.X, ALU.min))
            link(v.tensor_scalar(top[:, 1:2], top[:, 1:2], -1.0, None, ALU.mult))
            v.tensor_tensor(top[:, 5:6], top[:, 0:1], top[:, 1:2], ALU.max).then_inc(s("top_part"), 1)
            dve.wait_ge(s("top_all"), 3)
            for part in range(2):
                largest(0, 32, part)
            dve.wait_ge(s("logits"), 1)
            link(v.tensor_tensor(gates[0:NP], psum[0:NP, 0, 0:NT * NE].rearrange("p (t e) -> p t e", e=NE), gate_b[0:NP].unsqueeze(1).broadcast_to([NP, NT, NE]), ALU.add))
            dve.sem_inc(s("gates_read"), 1)
            link(v.tensor_reduce(gtmp[0:NP, 0], gates[0:NP], AX.X, ALU.max))
            link(v.tensor_tensor(gates[0:NP], gates[0:NP], gtmp[0:NP, 0].unsqueeze(2).broadcast_to([NP, NT, NE]), ALU.subtract))
            dve.sem_inc(s("gate_in"), 1)
            dve.wait_ge(s("gate_exp"), 1)
            link(v.tensor_reduce(gtmp[0:NP, 0], gates[0:NP], AX.X, ALU.add))
            link(v.reciprocal(gtmp[0:NP, 0], gtmp[0:NP, 0]))
            link(v.tensor_tensor(gates[0:NP], gates[0:NP], gtmp[0:NP, 0].unsqueeze(2).broadcast_to([NP, NT, NE]), ALU.mult))
            for a in range(NE):
                n_beat = gtmp[0:NP, 1]
                link(v.memset(n_beat, 0.0))
                for b in range(NE):
                    if b != a:
                        link(v.tensor_tensor(gtmp[0:NP, 2], gates[0:NP, :, b], gates[0:NP, :, a], ALU.is_ge if b < a else ALU.is_gt))
                        link(v.tensor_tensor(n_beat, n_beat, gtmp[0:NP, 2], ALU.add))
                link(v.scalar_tensor_tensor(out=gsel[0:NP, a], in0=n_beat, scalar=2.0, in1=gates[0:NP, :, a], op0=ALU.is_lt, op1=ALU.mult))
            for k in range(KT):
                dve.wait_ge(s("x_hi"), NT + k + 1)
                v.scalar_tensor_tensor(out=r2_16[:, 1, k], in0=r1[:, k], scalar=XS, in1=r2_16[:, 0, k], op0=ALU.mult, op1=ALU.subtract).then_inc(s("x_split"), 1)
            scales(0, 4)

            def lower(i):
                f, (n0, n1) = i // 3, NCH[i % 3]
                dve.wait_ge(s("part_hi"), i + 1)
                link(v.tensor_tensor(agg_x[f][:, 1, n0:n1], layer1_f32[i % 2][:, 0:n1 - n0], agg_x[f][:, 0, n0:n1], ALU.subtract))

            for i in range(12):
                n0, n1 = NCH[i % 3]
                dve.wait_ge(s("aggx_done"), i + 1)
                v.tensor_tensor(layer1_f32[i % 2][:, 0:n1 - n0], psum[:, 4 + i % 4, 0:n1 - n0], invdeg_l2[:, n0:n1], ALU.mult).then_inc(s("aggx_stored"), 1)
                if i >= 1:
                    lower(i - 1)
                if i in (2, 5):
                    split_weight(0, i // 3)
            lower(11)
            dve.sem_inc(s("x_split"), 1)
            with dve.Fori(0, NE // 2) as ei:
                for u in range(2):
                    e = 2 * ei + u
                    expert[0], steps[0] = e, 0
                    b0, b1 = (0, 4) if u == 0 else (4, 0)
                    i = 0
                    for f in range(KT):
                        for n0, n1 in NCH:
                            dve.wait_ge(s("layer1_stored"), e * 12 + i + 1)
                            v.tensor_tensor(r1_16[:, 1, f, n0:n1], layer1_f32[i % 2][:, 0:n1 - n0], r1_16[:, 0, f, n0:n1], ALU.subtract).then_inc(s("layer1_split"), 1)
                            if i in (4, 5):
                                largest(1, e * 32 + 32, i - 4)
                            if i == 7:
                                scales(1, 2 * e + 5)
                            if i in (8, 10):
                                split_weight(1, i // 2 - 4)
                            i += 1
                    for t in range(NT):
                        dve.wait_ge(s("part_hi"), 12 + e * 2 * NT + t + 1)
                        v.scalar_tensor_tensor(out=rows16[0:NP, t, 1], in0=psum[0:NP, b1 + t % 4], scalar=US, in1=rows16[0:NP, t, 0],
                                               op0=ALU.mult, op1=ALU.subtract).then_inc(s("u_stored"), 1)
                    dve.wait_ge(s("eb_in"), e * 16 + 16)
                    for t in range(NT):
                        tmp = l2_tmp[t % 2]
                        dve.wait_ge(s("eout_done"), e * NT + t + 1)
                        dve.wait_ge(s("part_hi"), 12 + e * 2 * NT + NT + t + 1)
                        v.scalar_tensor_tensor(out=tmp, in0=psum[0:NP, b0 + 2 * (t % 2)], scalar=esc[0:NP, 4:5], in1=tmp, op0=ALU.mult, op1=ALU.add).then_inc(s("eout_stored"), 1)
                        dve.wait_ge(s("eout_stored"), e * NT + t + 1)
                        step(v.tensor_tensor(tmp, tmp, l2_bias[0:NP], ALU.add))
                        v.tensor_scalar(tmp, tmp, 0.0, gsel[0:NP, bass.ds(e, 1), t:t + 1].rearrange("p a t -> p (a t)"), ALU.max, ALU.mult).then_inc(s("eweighted"), 1)
                        dve.wait_ge(s("eweighted"), e * NT + t + 1)
                        v.tensor_tensor(xr[0:NP, t], xr[0:NP, t], tmp, ALU.add).then_inc(s("eadd"), 1)
                        if t in (2, 3):
                            largest(0, e * 32 + 64, t - 2)
                        if t == 5:
                            scales(0, 2 * e + 6)
                        if t in (6, 7):
                            split_weight(0, t - 6)
                    assert steps[0] == L2_STEPS
            dve.wait_ge(s("eadd"), NE * NT)
            for t in range(NT):
                ln_rows(t, "l2_ln")
            dve.wait_ge(s("l2_ln"), NT)
            for t in range(NT):
                dve.wait_ge(s("l3_done"), t + 1)
                v.scalar_tensor_tensor(out=xr[0:NP, t], in0=psum[0:NP, t % 4], scalar=0.0, in1=xr[0:NP, t], op0=ALU.max, op1=ALU.add).then_inc(s("l3_stored"), 1)
                dve.wait_ge(s("l3_stored"), t + 1)
                ln_rows(t, "final_ln")


def kernel(**inputs):
    import numpy as np
    import concourse.bacc as bacc
    from concourse.bass_utils import run_bass_kernel_spmd

    a = {k: np.asarray(x) for k, x in inputs.items()}

    def cols(x):
        return x.reshape(-1, P).T

    arrays = {
        "x": a["x"], "xT": a["x"].T, "src": a["src"], "dst": a["dst"], "edge_weight": a["edge_weight"],
        "W1": a["L0_gnn_W1"], "W2": a["L0_gnn_W2"], "W_ihT": a["L0_gnn_W_ih"].T, "W_hhT": a["L0_gnn_W_hh"].T,
        "W_fc": a["L0_gnn_W_fc"], "b_fc": a["L0_gnn_b_fc"],
        "l1_W1": a["L1_gnn_W1"], "l1_b1": a["L1_gnn_b1"], "l1_W2": a["L1_gnn_W2"], "l1_b2": a["L1_gnn_b2"],
        "gate_W": a["L2_gnn_gate_W"], "gate_b": a["L2_gnn_gate_b"],
        "Wl0": a["L2_gnn_Wl"][:, 0], "Wl1": a["L2_gnn_Wl"][:, 1], "Wr0": a["L2_gnn_Wr"][:, 0], "Wr1": a["L2_gnn_Wr"][:, 1],
        "bl1": a["L2_gnn_bl"][:, 1], "l3_W": a["L3_gnn_W"],
        "bcol": np.concatenate([cols(a[n]) for n in ("L0_gnn_b1", "L0_gnn_b2", "L0_gnn_b_ih", "L0_gnn_b_hh", "L1_gnn_gamma", "L1_gnn_beta")]
                               + [cols(a["L2_gnn_bl"][:, 0])], axis=1),
    }
    arrays = {f"in_{k}": np.ascontiguousarray(x) for k, x in arrays.items()}
    nc = bacc.Bacc("TRN2", target_bir_lowering=False, num_devices=1)
    io = {k[3:]: nc.dram_tensor(k, x.shape, mybir.dt.from_np(x.dtype), kind="ExternalInput").ap() for k, x in arrays.items()}
    io["out"] = nc.dram_tensor("out", (N, D), F32, kind="ExternalOutput").ap()
    layout(nc, io)
    r = run_bass_kernel_spmd(nc, [arrays], core_ids=[0])
    return r.results[0]["out"]
```
